# Optimizing a Trainium2 kernel written in Bass

```python
import numpy as np
import jax
import jax.numpy as jnp

def _softmax(x, axis=-1):
    return jax.nn.softmax(x, axis=axis)

def _gelu(x):
    return jax.nn.gelu(x, approximate=True)

def _silu(x):
    return jax.nn.silu(x)

def _sigmoid(x):
    return jax.nn.sigmoid(x)

def _layernorm(x, axis=-1, eps=1e-05):
    m = jnp.mean(x, axis=axis, keepdims=True)
    v = jnp.var(x, axis=axis, keepdims=True)
    return (x - m) / jnp.sqrt(v + eps)

def _scatter_add(tgt, idx, src, axis=0):
    return tgt.at[idx].add(src)

def _segment_sum(src, seg, n):
    return jax.ops.segment_sum(src, seg, n)
kernel_name = 'mk_seq_postln_d1_jaxref_r8_d2a42f'

def setup_inputs(seed: int=0):
    np.random.seed(seed)
    _w = jnp.asarray

    def _L0_attn_setup():
        import jax, jax.numpy as jnp
        import numpy as np
        import math
        B, S, DIM = (1, 256, 128)
        H, KVH = (16, 4)
        HD = DIM // H
        KV_DIM = KVH * HD

        def _rms_norm(x):
            eps = jnp.finfo(x.dtype).eps
            return x * jax.lax.rsqrt(jnp.mean(x * x, axis=-1, keepdims=True) + eps)

        def _polar_rotary(seq_len, head_dim, dtype):
            angles = jnp.arange(0, head_dim, 2, dtype=jnp.float32) / head_dim * math.pi
            pos = jnp.arange(seq_len, dtype=jnp.float32)
            radius = 1.0 / (1.0 + pos[:, None] * 0.01)
            ang = pos[:, None] * angles[None, :]
            cos = (radius * jnp.cos(ang)).astype(dtype)
            sin = (radius * jnp.sin(ang)).astype(dtype)
            return (cos[None, None], sin[None, None])

        def _apply_rotary(x, cos, sin):
            half = x.shape[-1] // 2
            x1, x2 = (x[..., :half], x[..., half:])
            return jnp.concatenate([x1 * cos + x2 * sin, x1 * -sin + x2 * cos], axis=-1)

        def _causal_attn(q, k, v, scale, mask):
            s = jnp.einsum('bhqd,bhkd->bhqk', q, k) * scale
            s = jnp.where(mask, s, jnp.finfo(s.dtype).min)
            p = jax.nn.softmax(s, axis=-1)
            return jnp.einsum('bhqk,bhkd->bhqd', p, v)
        key = jax.random.key(seed)
        ks = jax.random.split(key, 8)
        std = 0.02
        return {'x': jax.random.normal(ks[0], (B, S, DIM), jnp.float32), 'Wq': jax.random.normal(ks[1], (DIM, DIM), jnp.float32) * std, 'Wk': jax.random.normal(ks[2], (KV_DIM, DIM), jnp.float32) * std, 'Wv': jax.random.normal(ks[3], (KV_DIM, DIM), jnp.float32) * std, 'Wg': jax.random.normal(ks[4], (KV_DIM, DIM), jnp.float32) * std, 'Wo': jax.random.normal(ks[5], (DIM, DIM), jnp.float32) * std, 'q_gain': jnp.full((H,), 1.0, jnp.float32), 'lambda_param': jnp.full((H,), 0.5, jnp.float32)}
    _L0_attn_in = _L0_attn_setup()

    def _L0_ffn_setup():
        import jax, jax.numpy as jnp
        import numpy as np
        B, S, DIM = (4, 512, 128)
        BASE_COUPLING = 0.1
        NUM_CYCLES = 3

        def _gelu(x):
            return jax.nn.gelu(x, approximate=False)

        def _coupling_net(h, w1, b1, w2, b2, w3, b3, w4, b4):
            h = _gelu(h @ w1 + b1)
            h = _gelu(h @ w2 + b2)
            h = _gelu(h @ w3 + b3)
            return jax.nn.sigmoid(h @ w4 + b4)

        def _global_net(h, w1, b1, w2, b2, w3, b3):
            h = _gelu(h @ w1 + b1)
            h = _gelu(h @ w2 + b2)
            return jax.nn.sigmoid(h @ w3 + b3)

        def _twist(x):
            o_r, o_i, p_r, p_i = jnp.split(x, 4, axis=-1)
            return jnp.concatenate([p_r, -p_i, -o_r, o_i], axis=-1)
        key = jax.random.key(seed)
        ks = jax.random.split(key, 9)
        d = DIM

        def w(k, fan_in, fan_out):
            return jax.random.normal(k, (fan_in, fan_out), dtype=jnp.float32) / np.sqrt(fan_in).astype(np.float32)
        inp = {'x': jax.random.normal(ks[0], (B, S, d), dtype=jnp.float32)}
        cn_dims = [(d, d), (d, d // 2), (d // 2, d // 4), (d // 4, 1)]
        for i, (a, b) in enumerate(cn_dims):
            inp[f'cn_w{i + 1}'] = w(ks[1 + i], a, b)
            inp[f'cn_b{i + 1}'] = jnp.zeros((b,), dtype=jnp.float32)
        gc_dims = [(d, d // 2), (d // 2, d // 4), (d // 4, 1)]
        for i, (a, b) in enumerate(gc_dims):
            inp[f'gc_w{i + 1}'] = w(ks[5 + i], a, b)
            inp[f'gc_b{i + 1}'] = jnp.zeros((b,), dtype=jnp.float32)
        inp['adaptive_range'] = jnp.full((1,), 0.2, dtype=jnp.float32)
        return inp
    _L0_ffn_in = _L0_ffn_setup()
    _d = {'L0_attn_x': _L0_attn_in['x'], 'L0_attn_Wq': _L0_attn_in['Wq'], 'L0_attn_Wk': _L0_attn_in['Wk'], 'L0_attn_Wv': _L0_attn_in['Wv'], 'L0_attn_Wg': _L0_attn_in['Wg'], 'L0_attn_Wo': _L0_attn_in['Wo'], 'L0_attn_q_gain': _L0_attn_in['q_gain'], 'L0_attn_lambda_param': _L0_attn_in['lambda_param'], 'L0_ffn_cn_w1': _L0_ffn_in['cn_w1'], 'L0_ffn_cn_b1': _L0_ffn_in['cn_b1'], 'L0_ffn_cn_w2': _L0_ffn_in['cn_w2'], 'L0_ffn_cn_b2': _L0_ffn_in['cn_b2'], 'L0_ffn_cn_w3': _L0_ffn_in['cn_w3'], 'L0_ffn_cn_b3': _L0_ffn_in['cn_b3'], 'L0_ffn_cn_w4': _L0_ffn_in['cn_w4'], 'L0_ffn_cn_b4': _L0_ffn_in['cn_b4'], 'L0_ffn_gc_w1': _L0_ffn_in['gc_w1'], 'L0_ffn_gc_b1': _L0_ffn_in['gc_b1'], 'L0_ffn_gc_w2': _L0_ffn_in['gc_w2'], 'L0_ffn_gc_b2': _L0_ffn_in['gc_b2'], 'L0_ffn_gc_w3': _L0_ffn_in['gc_w3'], 'L0_ffn_gc_b3': _L0_ffn_in['gc_b3'], 'L0_ffn_adaptive_range': _L0_ffn_in['adaptive_range']}
    _x0 = _d['L0_attn_x']
    _d['L0_attn_x'] = jax.random.normal(jax.random.fold_in(jax.random.key(seed), 1), (16, 256, 128), dtype=_x0.dtype)
    del _x0
    return _d

def reference(L0_attn_x, L0_attn_Wq, L0_attn_Wk, L0_attn_Wv, L0_attn_Wg, L0_attn_Wo, L0_attn_q_gain, L0_attn_lambda_param, L0_ffn_cn_w1, L0_ffn_cn_b1, L0_ffn_cn_w2, L0_ffn_cn_b2, L0_ffn_cn_w3, L0_ffn_cn_b3, L0_ffn_cn_w4, L0_ffn_cn_b4, L0_ffn_gc_w1, L0_ffn_gc_b1, L0_ffn_gc_w2, L0_ffn_gc_b2, L0_ffn_gc_w3, L0_ffn_gc_b3, L0_ffn_adaptive_range):

    def _L0_attn_ref(x, Wq, Wk, Wv, Wg, Wo, q_gain, lambda_param):
        import jax, jax.numpy as jnp
        import numpy as np
        import math
        B, S, DIM = (1, 256, 128)
        H, KVH = (16, 4)
        HD = DIM // H
        KV_DIM = KVH * HD

        def _rms_norm(x):
            eps = jnp.finfo(x.dtype).eps
            return x * jax.lax.rsqrt(jnp.mean(x * x, axis=-1, keepdims=True) + eps)

        def _polar_rotary(seq_len, head_dim, dtype):
            angles = jnp.arange(0, head_dim, 2, dtype=jnp.float32) / head_dim * math.pi
            pos = jnp.arange(seq_len, dtype=jnp.float32)
            radius = 1.0 / (1.0 + pos[:, None] * 0.01)
            ang = pos[:, None] * angles[None, :]
            cos = (radius * jnp.cos(ang)).astype(dtype)
            sin = (radius * jnp.sin(ang)).astype(dtype)
            return (cos[None, None], sin[None, None])

        def _apply_rotary(x, cos, sin):
            half = x.shape[-1] // 2
            x1, x2 = (x[..., :half], x[..., half:])
            return jnp.concatenate([x1 * cos + x2 * sin, x1 * -sin + x2 * cos], axis=-1)

        def _causal_attn(q, k, v, scale, mask):
            s = jnp.einsum('bhqd,bhkd->bhqk', q, k) * scale
            s = jnp.where(mask, s, jnp.finfo(s.dtype).min)
            p = jax.nn.softmax(s, axis=-1)
            return jnp.einsum('bhqk,bhkd->bhqd', p, v)
        bsz, seqlen, dim = x.shape
        q = (x @ Wq.T).reshape(bsz, seqlen, H, HD).transpose(0, 2, 1, 3)
        k = (x @ Wk.T).reshape(bsz, seqlen, KVH, HD).transpose(0, 2, 1, 3)
        v = (x @ Wv.T).reshape(bsz, seqlen, KVH, HD).transpose(0, 2, 1, 3)
        v_g = jax.nn.sigmoid((x @ Wg.T).reshape(bsz, seqlen, KVH, HD).transpose(0, 2, 1, 3))
        v = v * v_g
        q = _rms_norm(q)
        k = _rms_norm(k)
        cos, sin = _polar_rotary(seqlen, HD, q.dtype)
        q = _apply_rotary(q, cos, sin)
        k = _apply_rotary(k, cos, sin)
        q = q * q_gain.astype(q.dtype)[None, :, None, None]
        rep = H // KVH
        k = jnp.repeat(k, rep, axis=1)
        v = jnp.repeat(v, rep, axis=1)
        half = HD // 2
        q1, q2 = (q[..., :half], q[..., half:])
        k1, k2 = (k[..., :half], k[..., half:])
        v1, v2 = (v[..., :half], v[..., half:])
        scale = 1.0 / math.sqrt(half)
        mask = jnp.tril(jnp.ones((seqlen, seqlen), dtype=bool))[None, None]
        a1 = _causal_attn(q1, k1, v1, scale, mask)
        a2 = _causal_attn(q2, k2, v2, scale, mask)
        lp = lambda_param.astype(q.dtype)[None, :, None, None]
        y = jnp.concatenate([a1 - lp * a2, a1 + lp * a2], axis=-1)
        y = y.transpose(0, 2, 1, 3).reshape(bsz, seqlen, dim)
        return y @ Wo.T

    def _L0_ffn_ref(x, cn_w1, cn_b1, cn_w2, cn_b2, cn_w3, cn_b3, cn_w4, cn_b4, gc_w1, gc_b1, gc_w2, gc_b2, gc_w3, gc_b3, adaptive_range):
        import jax, jax.numpy as jnp
        import numpy as np
        B, S, DIM = (4, 512, 128)
        BASE_COUPLING = 0.1
        NUM_CYCLES = 3

        def _gelu(x):
            return jax.nn.gelu(x, approximate=False)

        def _coupling_net(h, w1, b1, w2, b2, w3, b3, w4, b4):
            h = _gelu(h @ w1 + b1)
            h = _gelu(h @ w2 + b2)
            h = _gelu(h @ w3 + b3)
            return jax.nn.sigmoid(h @ w4 + b4)

        def _global_net(h, w1, b1, w2, b2, w3, b3):
            h = _gelu(h @ w1 + b1)
            h = _gelu(h @ w2 + b2)
            return jax.nn.sigmoid(h @ w3 + b3)

        def _twist(x):
            o_r, o_i, p_r, p_i = jnp.split(x, 4, axis=-1)
            return jnp.concatenate([p_r, -p_i, -o_r, o_i], axis=-1)
        global_context = x.mean(axis=1, keepdims=True)
        gf = _global_net(global_context, gc_w1, gc_b1, gc_w2, gc_b2, gc_w3, gc_b3)
        out = x
        for _ in range(NUM_CYCLES):
            tf = _coupling_net(out, cn_w1, cn_b1, cn_w2, cn_b2, cn_w3, cn_b3, cn_w4, cn_b4)
            combined = 0.7 * gf + 0.3 * tf
            coupling = BASE_COUPLING + adaptive_range * (combined - 0.5) * 2.0
            out = out + coupling * _twist(out)
        return out
    x = L0_attn_x
    x = _layernorm(x + _L0_attn_ref(x, L0_attn_Wq, L0_attn_Wk, L0_attn_Wv, L0_attn_Wg, L0_attn_Wo, L0_attn_q_gain, L0_attn_lambda_param), axis=-1)
    x = _layernorm(x + _L0_ffn_ref(x, L0_ffn_cn_w1, L0_ffn_cn_b1, L0_ffn_cn_w2, L0_ffn_cn_b2, L0_ffn_cn_w3, L0_ffn_cn_b3, L0_ffn_cn_w4, L0_ffn_cn_b4, L0_ffn_gc_w1, L0_ffn_gc_b1, L0_ffn_gc_w2, L0_ffn_gc_b2, L0_ffn_gc_w3, L0_ffn_gc_b3, L0_ffn_adaptive_range), axis=-1)
    return x

_drawn_inputs = setup_inputs


def setup_inputs(seed=0):
    import zlib

    import numpy as np

    out = dict(_drawn_inputs(seed))
    spreads = {'L0_attn_q_gain': (1.0, 0.6),
     'L0_attn_lambda_param': (0.5, 0.6),
     'L0_ffn_cn_b1': (0.0, 2.0),
     'L0_ffn_cn_b2': (0.0, 2.0),
     'L0_ffn_cn_b3': (0.0, 2.0),
     'L0_ffn_gc_b1': (0.0, 0.8),
     'L0_ffn_gc_b2': (0.0, 2.0)}
    factors = {'L0_attn_Wq': 8.0,
     'L0_attn_Wk': 8.0,
     'L0_attn_Wv': 8.0,
     'L0_attn_Wg': 8.0,
     'L0_attn_Wo': 8.0,
     'L0_ffn_cn_w1': 8.0,
     'L0_ffn_cn_w2': 7.791,
     'L0_ffn_cn_w3': 6.696,
     'L0_ffn_cn_w4': 4.287,
     'L0_ffn_gc_w1': 8.0,
     'L0_ffn_gc_w2': 8.0,
     'L0_ffn_gc_w3': 8.0}
    for name, (base, spread) in spreads.items():
        noise = np.random.default_rng([zlib.crc32(name.encode()), seed]).standard_normal(out[name].shape)
        drawn = base * np.exp(spread * noise) if base else spread * noise
        out[name] = jnp.asarray(drawn.astype(out[name].dtype))
    for name, factor in factors.items():
        out[name] = (out[name] * factor).astype(out[name].dtype)
    return out
```

```python
import concourse.bass as bass
from concourse import mybir
from contextlib import ExitStack

F32 = mybir.dt.float32
BF16 = mybir.dt.bfloat16
I32 = mybir.dt.int32
ALU = mybir.AluOpType
ACT = mybir.ActivationFunctionType
AX = mybir.AxisListType

BATCH, SEQ, DIM = 16, 256, 128
HEADS, G, HD = 16, 4, 8
R = HEADS // G
HALF = HD // 2
T = SEQ // 128
KV = G * HD
QK = DIM + KV
PROJ = DIM + 3 * KV
SLOTS = 8
OUTROW = HALF + 1
PAD = 3 * OUTROW
VWIDTH = PAD + 32
SAFE_GAIN = 8.0
FUTURE = -1e30
CYCLES = 3
TOK = BATCH * SEQ
LN_EPS = 1e-5
RMS_EPS = 1.1920928955078125e-07

KINDS = [(0, 0), (0, 1), (1, 1)]
DIAGONAL = (0, 2)
BLOCKS = len(KINDS) * R * 2


def reach(eng, sem, n):
    if not isinstance(n, int) or n > 0:
        eng.wait_ge(sem, n)


def reach_alone(eng, sem, n, zeros_ready):
    eng.wait_ge(zeros_ready, 1)
    reach(eng, sem, n)


def block_kernel(nc, A, out):
    ctx = ExitStack()
    with ctx:
        def sb(name, shape, dt=F32):
            return ctx.enter_context(nc.sbuf_tensor(name, shape, dt))

        def ps(name, shape, dt=F32):
            return ctx.enter_context(nc.psum_tensor(name, shape, dt))

        def sem(name):
            return ctx.enter_context(nc.semaphore(name))

        ident = sb("ident", [128, 128])
        ident16 = sb("ident16", [128, 128], BF16)
        future_in = sb("future_in", [128, 128])
        future16 = sb("future16", [128, G, 128], BF16)
        gain_sq = sb("gain_sq", [128, HEADS])
        gain_top = sb("gain_top", [128, 1])
        bounded = sb("bounded", [128, 1], I32)
        w_proj = sb("w_proj", [128, PROJ])
        w_o0 = sb("w_o0", [128, DIM])
        w_o1 = sb("w_o1", [128, DIM])
        w_out = sb("w_out", [128, DIM])
        lam = sb("lam", [128, 1])
        sel_s = sb("sel_s", [128, 3])
        mix = sb("mix", [128, 2])
        gain = sb("gain", [128, HEADS])
        trig = sb("trig", [128, 2, T, HALF])
        rope_cos = sb("rope_cos", [128, T, HEADS + G, 2, HALF])
        rope_sin = sb("rope_sin", [128, T, HEADS + G, 2, HALF])
        minus_half = sb("minus_half", [128, T * (HEADS + G)])
        rms_eps = sb("rms_eps", [128, T * (HEADS + G)])
        ln_eps = sb("ln_eps", [128, 4])

        xT_in = [sb(f"xT_in{p}", [128, SEQ]) for p in range(2)]
        x_res = [sb(f"x_res{p}", [128, T, DIM]) for p in range(2)]
        qkvg = sb("qkvg", [128, T, PROJ])
        square = sb("square", [128, T, QK])
        mean_sq = sb("mean_sq", [128, T * (HEADS + G)])
        mean_eps = sb("mean_eps", [128, T * (HEADS + G)])
        rstd = sb("rstd", [128, T * (HEADS + G)])
        normed = sb("normed", [128, T, HEADS + G, 2, HALF])
        turned = sb("turned", [128, T, HEADS + G, 2, HALF])
        turned2 = sb("turned2", [128, T, HEADS + G, 2, HALF])
        NQ = T * R * 2 * G
        NK = T * 2 * G
        roped = sb("roped", [128, NQ + NK, HALF])
        rest1 = sb("rest1", [128, NQ + NK, HALF])
        parts = sb("parts", [128, NQ + NK, SLOTS, HALF], BF16)
        block_max = sb("block_max", [128, len(KINDS), R * 2 * G])
        row_max = sb("row_max", [128, NQ])
        minus_max = sb("minus_max", [128, NQ])
        gate_exp = sb("gate_exp", [128, T, KV])
        gate_den = sb("gate_den", [128, T, KV])
        gate = sb("gate", [128, T, KV])
        qT = [sb(f"qT{p}", [128, T, R, 2, 128], BF16) for p in range(2)]
        kT = [sb(f"kT{p}", [128, G, T, 2, 128], BF16) for p in range(2)]
        values = [sb(f"values{p}", [128, T, G, 2, VWIDTH]) for p in range(2)]

        probs = sb("probs", [128, len(KINDS), G, 2, R * 128])
        o_sb = sb("o_sb", [128, R * 128])
        rden = sb("rden", [128, R * G, T * 2])
        heads = sb("heads", [128, T, DIM])
        headsT = sb("headsT", [128, T * 128])
        summed = sb("summed", [128, T, DIM])
        stats = sb("stats", [128, T, 6])
        moments = sb("moments", [128, T, 2])
        var_eps = sb("var_eps", [128, T])
        ln_rstd = sb("ln_rstd", [128, T])
        x1 = sb("x1", [128, T, DIM])
        X0 = sb("X0", [128, TOK])
        xsum = sb("xsum", [128, BATCH])

        X = sb("X", [128, TOK])
        Y = sb("Y", [128, TOK])
        cn_w1 = sb("cn_w1", [128, 128])
        cn_w2 = sb("cn_w2", [128, 64])
        cn_w3 = sb("cn_w3", [128, 64])
        cn_w4 = sb("cn_w4", [128, 4])
        cn_b1 = sb("cn_b1", [128, 1])
        cn_b2 = sb("cn_b2", [128, 1])
        cn_b3 = sb("cn_b3", [128, 1])
        cn_b4 = sb("cn_b4", [4, 2])
        gc_w1 = sb("gc_w1", [128, 64])
        gc_w2 = sb("gc_w2", [64, 32])
        gc_w3 = sb("gc_w3", [32, 1])
        gc_b1 = sb("gc_b1", [64, 1])
        gc_b2 = sb("gc_b2", [32, 1])
        gc_b3 = sb("gc_b3", [4, 2])
        arange_in = sb("arange_in", [128, 1])
        arange7 = sb("arange7", [4, 1])
        spread = sb("spread", [36, 4, 128])
        pick = sb("pick", [36, 4, 128])
        hg1 = sb("hg1", [64, BATCH])
        hg2 = sb("hg2", [32, BATCH])
        tanh_g = sb("tanh_g", [4, 4])
        h1 = sb("h1", [128, 4 * 512])
        h2 = sb("h2", [128, 2 * 512])
        h3 = sb("h3", [128, 512])
        coup = [sb(f"coup{h}", [36, 512]) for h in range(2)]
        cY = sb("cY", [128, 2, 512])
        cX = sb("cX", [128, 2, 512])
        f_stats = sb("f_stats", [128, 2, 4, 6])
        f_mom = sb("f_mom", [128, 2, 4, 2])
        f_var = sb("f_var", [128, 2, 4])
        f_rstd = sb("f_rstd", [128, 2, 4])
        f_shift = sb("f_shift", [128, 2, 4])
        result = sb("result", [128, 4, 4, DIM])

        S = [ps(f"S{i}", [128, 2, R * 128]) for i in range(2)]
        O = ps("O", [128, R * 128])
        MA = ps("MA", [128, 512])
        MB = ps("MB", [128, 512])
        MC = ps("MC", [128, 512])
        MA16 = MA[:, :].bitcast(BF16)
        MB16 = MB[:, :].bitcast(BF16)
        MC16 = MC[:, :].bitcast(BF16)

        names = ("consts_loaded ffn_loaded tables_ready zeros_ready half_ready "
                 "proj_done qkvg_ready gate_exp_ready gate_den_done gate_done values_ready "
                 "square_done mean_sq_done mean_eps_done rstd_ready normed_done cos_done sin_done roped_done "
                 "part0_done rest1_done part1_done parts_ready gain_step_done bounded_ready slot_cleared "
                 "block_scored block_max_done max_step_done max_parts_ready "
                 "q0_turned_max q1_turned_max q0_ready_max q1_ready_max "
                 "q0_turned q1_turned k_turned q0_ready q1_ready k_ready "
                 "o_ready o_turned rden_done heads_done heads_turned headsT_ready projected summed_done "
                 "stats_done moments_done var_eps_done ln_rstd_ready x1_ready x1_turned X0_ready xsum_ready "
                 "zeros_done half_ready2 w_out_step_done pick_done g1_done hg1_ready g2_done hg2_ready g3_done tanh_g_ready coup_ready spread_ready XY_ready "
                 "h3_done gelu3_done z_done tanh_ready sum_ready "
                 "turned_back f_stats_done f_moments_done f_norm_step_done result_ready").split()
        n_ = {n: sem(n) for n in names}
        xT_loaded = [sem(f"xT_loaded{p}") for p in range(2)]
        res_loaded = [sem(f"res_loaded{p}") for p in range(2)]
        scores_done = [[sem(f"scores_done_{k}{g}") for g in range(G)] for k in range(3)]
        exp_done = [[sem(f"exp_done_{k}{g}") for g in range(G)] for k in range(3)]
        masked = {k: [sem(f"masked_{k}{g}") for g in range(G)] for k in DIAGONAL}
        pv_done = [[sem(f"pv_done_{k}{s}") for s in range(2)] for k in range(3)]
        h1_done = [sem(f"h1_done{c}") for c in range(2)]
        gelu1_done = [sem(f"gelu1_done{c}") for c in range(2)]
        h2_done = [sem(f"h2_done{c}") for c in range(2)]
        gelu2_done = [sem(f"gelu2_done{c}") for c in range(2)]
        spread_done = [sem(f"spread_done{c}") for c in range(4)]
        cY_done = [sem(f"cY_done{c}") for c in range(4)]
        cX_done = [sem(f"cX_done{c}") for c in range(4)]
        X_done = [sem(f"X_done{c}") for c in range(4)]
        Y_done = [sem(f"Y_done{c}") for c in range(4)]
        stored = [sem(f"stored{c}") for c in range(4)]
        block = ctx.enter_context(nc.Block())

        CONSTS = ("ident trig gain sel_s lam w_o0 w_o1 future".split())

        def batches(eng, step):
            step(0, 0, 0)
            step(1, 1, 0)
            with eng.Fori(1, BATCH // 2 - 1) as i:
                step(eng.snap(i * 2), 0, i)
                step(eng.snap(i * 2 + 1), 1, i)
            step(BATCH - 2, 0, BATCH // 2 - 1)
            step(BATCH - 1, 1, BATCH // 2 - 1)

        def cycles(eng, half_cycle):
            half_cycle(0, 0, True, False)
            half_cycle(1, 1, True, False)
            half_cycle(2, 0, False, False)
            half_cycle(3, 1, False, False)
            half_cycle(4, 0, False, True)
            half_cycle(5, 1, False, True)

        @block.sync
        def _(sp):
            sp.dma_start(w_proj[:, :], A["w_proj"]).then_inc(n_["consts_loaded"], 16)
            for p in range(2):
                sp.dma_start(xT_in[p][:, :], A["xT"][p]).then_inc(xT_loaded[p], 16)
            tiles = dict(ident=ident, trig=trig, gain=gain, sel_s=sel_s, lam=lam, w_o0=w_o0, w_o1=w_o1, future=future_in)
            for name in CONSTS:
                sp.dma_start(tiles[name][:], A[name]).then_inc(n_["consts_loaded"], 16)
            for p in range(2):
                sp.dma_start(x_res[p][:, :, :], A["x"][p].rearrange("(t p) d -> p t d", p=128)).then_inc(res_loaded[p], 16)

            def load(n, p):
                src = A["xT"][bass.ds(n + 2, 1)].rearrange("o d s -> d (o s)")
                res = A["x"][bass.ds(n + 2, 1)].rearrange("o (t p) d -> p (o t) d", p=128)
                sp.wait_ge(n_["proj_done"], n + 1)
                sp.dma_start(xT_in[p][:, :], src).then_inc(xT_loaded[p], 16)
                sp.wait_ge(n_["summed_done"], n + 1)
                sp.dma_start(x_res[p][:, :, :], res).then_inc(res_loaded[p], 16)

            load(0, 0)
            load(1, 1)
            sp.wait_ge(n_["zeros_ready"], 2)
            loads = [(cn_w1[:, :], "cn_w1"), (cn_w2[:, :], "cn_w2"), (cn_w3[0:64, 0:32], "cn_w3"),
                     (cn_w3[64:128, 32:64], "cn_w3"), (cn_b1[:, :], "cn_b1"), (cn_b2[:, :], "cn_b2"),
                     (cn_b3[:, :], "cn_b3"), (cn_b4[:, 0:1], "cn_b4"), (gc_w1[:, :], "gc_w1"), (gc_w2[:, :], "gc_w2"),
                     (gc_w3[:, :], "gc_w3"), (gc_b1[:, :], "gc_b1"), (gc_b2[:, :], "gc_b2"), (gc_b3[:, 0:1], "gc_b3"),
                     (arange_in[:, :], "arange_in"), (pick[:, :, :], "pick")]
            loads += [(cn_w4[32 * c:32 * c + 32, c:c + 1], "cn_w4") for c in range(4)]
            assert len(loads) == FFN_LOADS
            for dst, name in loads:
                sp.dma_start(dst, A[name]).then_inc(n_["ffn_loaded"], 16)
            with sp.Fori(1, BATCH // 2 - 1) as i:
                load(sp.snap(i * 2), 0)
                load(sp.snap(i * 2 + 1), 1)
            for f in range(8):
                sp.wait_ge(n_["result_ready"], f + 1)
                sp.dma_start(out.rearrange("(f t p) d -> f p t d", t=4, p=128)[f], result[:, f % 4, :, :])\
                  .then_inc(stored[f % 4], 16)
            for c in range(4):
                sp.wait_ge(stored[c], 32)

        @block.tensor
        def _(pe):
            def project(b, p, half_b):
                pe.wait_ge(xT_loaded[p], (half_b + 1) * 16)
                for t in range(T):
                    mm = pe.matmul(MA[:, t * PROJ:(t + 1) * PROJ], xT_in[p][:, t * 128:(t + 1) * 128], w_proj[:, :],
                                   start=True, stop=True)
                mm.then_inc(n_["proj_done"], 1)

            def turn_queries(b, parts_in="parts_ready", turned="turned"):
                pe.wait_ge(n_[parts_in], b + 1)
                reach(pe, n_["heads_done"], b - 1)
                reach(pe, n_["headsT_ready"], b - 1)
                for t, bank in enumerate((MB16, MC16)):
                    for n in range(R * 2):
                        u = (t * R * 2 + n) * G
                        mm = pe.transpose(bank[:, n * 128:(n + 1) * 128],
                                          parts[:, u:u + G, :, :].rearrange("p u s d -> p (u s d)"), ident16[:, :])
                    mm.then_inc(n_[f"q{t}_{turned}"], 1)

            def turn_keys(b):
                pe.wait_ge(n_["parts_ready"], b + 1)
                pe.wait_ge(n_["qkvg_ready"], b + 1)
                reach(pe, n_["summed_done"], b - 1)
                for n in range(T * 2):
                    u = NQ + n * G
                    mm = pe.transpose(MA16[:, n * 128:(n + 1) * 128],
                                      parts[:, u:u + G, :, :].rearrange("p u s d -> p (u s d)"), ident16[:, :])
                mm.then_inc(n_["k_turned"], 1)

            def blocks_for_maximum(b, p):
                pe.wait_ge(n_["q0_ready"], b + 1)
                pe.wait_ge(n_["q1_ready"], b + 1)
                pe.wait_ge(n_["k_ready"], b + 1)
                for k, (kt, qt) in enumerate(KINDS):
                    for n in range(R * 2):
                        if k * R * 2 + n >= 2:
                            pe.wait_ge(n_["block_max_done"], b * BLOCKS + k * R * 2 + n - 1)
                        r, s = n // 2, n % 2
                        bank = (MB, MC)[n % 2]
                        mm = pe.matmul(bank[:, :].rearrange("p (g n) -> p g n", g=G), qT[p][:, qt, r, s, :],
                                       kT[p][:, :, kt, s, :], start=True, stop=k not in DIAGONAL)
                        if k in DIAGONAL:
                            mm = pe.matmul(bank[:, :], ident16[:, :], future16[:, :, :].rearrange("p g n -> p (g n)"),
                                           start=False, stop=True)
                        mm.then_inc(n_["block_scored"], 1)
                turn_queries(b, "max_parts_ready", "turned_max")

            def scores(b, p, k, g, general):
                pair = k * G + g
                kt, qt = KINDS[k]
                if k == 0 and g == 0:
                    pe.wait_ge(n_["k_ready"], b + 1)
                    pe.wait_ge(n_["q0_ready_max" if general else "q0_ready"], b + 1)
                if k == 1 and g == 0:
                    pe.wait_ge(n_["q1_ready_max" if general else "q1_ready"], b + 1)
                if pair >= 2:
                    pe.wait_ge(exp_done[(pair - 2) // G][(pair - 2) % G], b + 1)
                else:
                    reach(pe, exp_done[2][2 + pair], b)
                for s in range(2):
                    mm = pe.matmul(S[pair % 2][:, s, :], kT[p][:, g, kt, s, :], qT[p][:, qt, :, s, :],
                                   start=True, stop=True)
                mm.then_inc(scores_done[k][g], 1)

            def weigh(b, p, k, s):
                kt, qt = KINDS[k]
                first = k == 0 and s == 0
                if first:
                    pe.wait_ge(n_["values_ready"], b + 1)
                    reach(pe, n_["o_ready"], b)
                if s == 0:
                    for g in range(G):
                        pe.wait_ge((masked if k in DIAGONAL else exp_done)[k][g], b + 1)
                at = PAD - OUTROW * (qt * 2 + s)
                for g in range(G):
                    mm = pe.matmul(O[32 * g:32 * g + 32, :], values[p][:, kt, g, s, at:at + 32], probs[:, k, g, s, :],
                                   start=first, stop=(k == 2 and s == 1))
                mm.then_inc(pv_done[k][s], 1)

            def turn_outputs(b):
                pe.wait_ge(n_["o_ready"], b + 1)
                reach(pe, n_["xsum_ready"], b)
                for r in range(R):
                    mm = pe.transpose(MB[:, r * 128:(r + 1) * 128], o_sb[:, r * 128:(r + 1) * 128], ident[:, :])
                mm.then_inc(n_["o_turned"], 1)

            def turn_heads(b):
                pe.wait_ge(n_["heads_done"], b + 1)
                for t in range(T):
                    mm = pe.transpose(MC[:, t * 128:(t + 1) * 128], heads[:, t, :], ident[:, :])
                mm.then_inc(n_["heads_turned"], 1)

            def output_projection(b, more):
                pe.wait_ge(n_["headsT_ready"], b + 1)
                if more:
                    pe.wait_ge(n_["qkvg_ready"], b + 3)
                for t in range(T):
                    mm = pe.matmul(MA[:, t * 128:(t + 1) * 128], headsT[:, t * 128:(t + 1) * 128], w_out[:, :],
                                   start=True, stop=True)
                mm.then_inc(n_["projected"], 1)

            def turn_x1(b):
                pe.wait_ge(n_["x1_ready"], b + 1)
                for t in range(T):
                    mm = pe.transpose(MB[:, t * 128:(t + 1) * 128], x1[:, t, :], ident[:, :])
                mm.then_inc(n_["x1_turned"], 1)

            def attend(b, p, half_b, general):
                first, second, last = (isinstance(b, int) and b == n for n in (0, 1, BATCH - 1))
                scores(b, p, 0, 0, general)
                if not last:
                    project(b + 1, 1 - p, half_b + p)
                scores(b, p, 0, 1, general)
                if not first and not second:
                    turn_x1(b - 2)
                scores(b, p, 0, 2, general)
                if not first:
                    weigh(b - 1, 1 - p, 2, 0)
                scores(b, p, 0, 3, general)
                if not first:
                    weigh(b - 1, 1 - p, 2, 1)
                    turn_outputs(b - 1)
                scores(b, p, 1, 0, general)
                scores(b, p, 1, 1, general)
                scores(b, p, 1, 2, general)
                weigh(b, p, 0, 0)
                if not first:
                    turn_heads(b - 1)
                scores(b, p, 1, 3, general)
                weigh(b, p, 0, 1)
                scores(b, p, 2, 0, general)
                if not first:
                    output_projection(b - 1, not last)
                scores(b, p, 2, 1, general)
                if not last:
                    turn_queries(b + 1)
                scores(b, p, 2, 2, general)
                weigh(b, p, 1, 0)
                if not last:
                    turn_keys(b + 1)
                    if general:
                        blocks_for_maximum(b + 1, 1 - p)
                scores(b, p, 2, 3, general)
                weigh(b, p, 1, 1)

            def attention(general):
                project(0, 0, 0)
                turn_queries(0)
                turn_keys(0)
                if general:
                    blocks_for_maximum(0, 0)
                pe.wait_ge(n_["w_out_step_done"], 3)
                batches(pe, lambda b, p, half_b: attend(b, p, half_b, general))
                last = BATCH - 1
                turn_x1(last - 1)
                weigh(last, last % 2, 2, 0)
                weigh(last, last % 2, 2, 1)
                turn_outputs(last)
                turn_heads(last)
                output_projection(last, False)
                turn_x1(last)

            pe.wait_ge(n_["consts_loaded"], 16 * (1 + len(CONSTS)))
            pe.wait_ge(n_["bounded_ready"], 1)
            is_bounded = pe.value_load(bounded[0:1, 0:1], min_val=0, max_val=1)
            with pe.If(is_bounded > 0):
                attention(False)
            with pe.Else():
                attention(True)

            pe.wait_ge(n_["xsum_ready"], BATCH)
            pe.wait_ge(n_["ffn_loaded"], 16 * FFN_LOADS)

            def dense1(u, h, first):
                for c in range(2):
                    if not first:
                        for j in (2 * c, 2 * c + 1):
                            pe.wait_ge(X_done[j], u - 1)
                    if u >= 1:
                        pe.wait_ge(gelu1_done[c], u)
                    for j in range(2):
                        at = h * 2048 + (2 * c + j) * 512
                        mm = pe.matmul(S[c][:, j, :], cn_w1[:, :], X[:, at:at + 512] if not first else X0[:, at:at + 512],
                                       start=True, stop=True)
                    mm.then_inc(h1_done[c], 1)

            def dense2(u):
                for c in range(2):
                    pe.wait_ge(gelu1_done[c], u + 1)
                    if c == 1:
                        pe.wait_ge(gelu2_done[0], u + 1)
                    elif u >= 1:
                        pe.wait_ge(gelu2_done[1], u)
                    for j in range(2):
                        mm = pe.matmul(MA[64 * j:64 * j + 64, :], cn_w2[:, :], h1[:, (2 * c + j) * 512:(2 * c + j + 1) * 512],
                                       start=True, stop=True)
                    mm.then_inc(h2_done[c], 1)

            def dense3(u):
                if u >= 1:
                    pe.wait_ge(n_["tanh_ready"], u)
                for c in range(2):
                    pe.wait_ge(gelu2_done[c], u + 1)
                    mm = pe.matmul(MB[64 * c:64 * c + 64, :], cn_w3[:, :], h2[:, c * 512:(c + 1) * 512],
                                   start=True, stop=True)
                mm.then_inc(n_["h3_done"], 1)

            def dense4(u):
                pe.wait_ge(n_["gelu3_done"], u + 1)
                pe.matmul(MB[0:4, :], cn_w4[:, :], h3[:, :], start=True, stop=True).then_inc(n_["z_done"], 1)

            def spread_coupling(u, h):
                pe.wait_ge(n_["tanh_ready"], u + 1)
                for j in range(4):
                    if j >= 2:
                        pe.wait_ge((cX_done if u < 4 else cY_done)[j - 2], u + 1)
                    elif u >= 1:
                        pe.wait_ge((cX_done if u - 1 < 4 else cY_done)[j + 2], u)
                    pe.matmul((O, MC)[j % 2][:, :], spread[:, j, :], coup[h][:, :], start=True, stop=True)\
                      .then_inc(spread_done[j], 1)

            pe.matmul(MB[0:64, 0:BATCH], gc_w1[:, :], xsum[:, :], start=True, stop=True).then_inc(n_["g1_done"], 1)
            pe.wait_ge(n_["hg1_ready"], 1)
            pe.matmul(MB[0:32, 0:BATCH], gc_w2[:, :], hg1[:, :], start=True, stop=True).then_inc(n_["g2_done"], 1)
            pe.wait_ge(n_["hg2_ready"], 1)
            for n in range(4):
                first_batch = 8 * (n // 2) + n % 2
                mm = pe.matmul(MB[0:4, n:n + 1], hg2[:, first_batch:first_batch + 7:2], gc_w3[:, :], start=True, stop=True)
            mm.then_inc(n_["g3_done"], 1)
            pe.wait_ge(n_["tanh_g_ready"], 1)

            def half_cycle(u, h, first, last):
                dense1(u, h, first)
                if u == 0:
                    pe.wait_ge(n_["coup_ready"], 1)
                    pe.wait_ge(n_["spread_ready"], 1)
                else:
                    spread_coupling(u - 1, 1 - h)
                dense2(u)
                dense3(u)
                dense4(u)

            def turn_back(f):
                pe.wait_ge(X_done[f % 4], CYCLES * 2 - 1 + f // 4)
                if f >= 4:
                    pe.wait_ge(n_["result_ready"], f - 3)
                bank = S[(f % 4) // 2][:, f % 2, :]
                for t in range(4):
                    at = f * 512 + t * 128
                    mm = pe.transpose(bank[:, t * 128:(t + 1) * 128], X0[:, at:at + 128], ident[:, :])
                mm.then_inc(n_["turned_back"], 1)

            cycles(pe, half_cycle)
            for f in range(4):
                turn_back(f)
            spread_coupling(5, 1)
            for f in range(4, 8):
                turn_back(f)

        @block.scalar
        def _(act):
            def copy_projection(b):
                act.wait_ge(n_["proj_done"], b + 1)
                reach(act, n_["values_ready"], b)
                act.activation(qkvg[:, :, :].rearrange("p t c -> p (t c)"), MA[:, 0:T * PROJ], ACT.Copy)\
                   .then_inc(n_["qkvg_ready"], 1)

            def gate_exponentials(b):
                act.wait_ge(n_["qkvg_ready"], b + 1)
                act.activation(gate_exp[:, :, :], qkvg[:, :, QK + KV:PROJ], ACT.Exp, scale=-1.0)\
                   .then_inc(n_["gate_exp_ready"], 1)

            def exponentials(b, k, g):
                act.wait_ge(scores_done[k][g], b + 1)
                if g == 0:
                    reach(act, pv_done[k][1], b)
                act.activation(probs[:, k, g, :, :], S[(k * G + g) % 2][:, :, :], ACT.Exp).then_inc(exp_done[k][g], 1)

            def copy_heads(b):
                act.wait_ge(n_["heads_turned"], b + 1)
                reach(act, n_["projected"], b)
                act.activation(headsT[:, :], MC[:, 0:T * 128], ACT.Copy).then_inc(n_["headsT_ready"], 1)

            def attend(b, p, half_b):
                first, second, last = (isinstance(b, int) and b == n for n in (0, 1, BATCH - 1))
                exponentials(b, 0, 0)
                exponentials(b, 0, 1)
                if not last:
                    copy_projection(b + 1)
                    gate_exponentials(b + 1)
                exponentials(b, 0, 2)
                exponentials(b, 0, 3)
                exponentials(b, 1, 0)
                exponentials(b, 1, 1)
                exponentials(b, 1, 2)
                exponentials(b, 1, 3)
                if not first:
                    copy_heads(b - 1)
                for g in range(G):
                    exponentials(b, 2, g)

            copy_projection(0)
            gate_exponentials(0)
            batches(act, attend)
            copy_heads(BATCH - 1)

            act.wait_ge(n_["ffn_loaded"], 16 * FFN_LOADS)
            act.mul(cn_b4[:, 1:2], cn_b4[:, 0:1], 0.5)
            act.mul(gc_b3[:, 1:2], gc_b3[:, 0:1], 0.5).then_inc(n_["half_ready"], 1)
            act.wait_ge(n_["half_ready"], 1)
            act.wait_ge(n_["g1_done"], 1)
            act.activation(hg1[:, :], MB[0:64, 0:BATCH], ACT.Gelu, bias=gc_b1[:, :], scale=1.0 / SEQ).then_inc(n_["hg1_ready"], 1)
            act.wait_ge(n_["g2_done"], 1)
            act.activation(hg2[:, :], MB[0:32, 0:BATCH], ACT.Gelu, bias=gc_b2[:, :]).then_inc(n_["hg2_ready"], 1)
            act.wait_ge(n_["g3_done"], 1)
            act.activation(tanh_g[:, :], MB[0:4, 0:4], ACT.Tanh, bias=gc_b3[:, 1:2], scale=0.5).then_inc(n_["tanh_g_ready"], 1)

            def half_cycle(u, h, first, last):
                for c in range(2):
                    act.wait_ge(h1_done[c], u + 1)
                    if u >= 1:
                        act.wait_ge(h2_done[c], u)
                    act.activation(h1[:, c * 1024:(c + 1) * 1024], S[c][:, :, :].rearrange("p s n -> p (s n)"),
                                   ACT.Gelu, bias=cn_b1[:, :]).then_inc(gelu1_done[c], 1)
                for c in range(2):
                    act.wait_ge(h2_done[c], u + 1)
                    if u >= 1:
                        act.wait_ge(n_["h3_done"], u)
                    act.activation(h2[:, c * 512:(c + 1) * 512], MA[:, :], ACT.Gelu, bias=cn_b2[:, :]).then_inc(gelu2_done[c], 1)
                act.wait_ge(n_["h3_done"], u + 1)
                if u >= 1:
                    act.wait_ge(n_["z_done"], u)
                act.activation(h3[:, :], MB[:, :], ACT.Gelu, bias=cn_b3[:, :]).then_inc(n_["gelu3_done"], 1)
                act.wait_ge(n_["z_done"], u + 1)
                if u >= 2:
                    act.wait_ge(spread_done[3], u - 1)
                else:
                    act.wait_ge(n_["coup_ready"], 1)
                act.activation(coup[h][0:4, :], MB[0:4, :], ACT.Tanh, bias=cn_b4[:, 1:2], scale=0.5).then_inc(n_["tanh_ready"], 1)

            cycles(act, half_cycle)
            for f in range(8):
                act.wait_ge(n_["f_norm_step_done"], 4 * (f + 1))
                if f >= 4:
                    act.wait_ge(stored[f % 4], 16)
                bank = S[(f % 4) // 2][:, f % 2, :]
                for t in range(4):
                    a = act.activation(result[:, f % 4, t, :], bank[:, t * 128:(t + 1) * 128], ACT.Identity,
                                       bias=f_shift[:, f % 2, t:t + 1], scale=f_rstd[:, f % 2, t:t + 1])
                a.then_inc(n_["result_ready"], 1)

        @block.vector
        def _(dve):
            dve.memset(rms_eps[:, :], HD * RMS_EPS)
            dve.memset(ln_eps[:, :], LN_EPS)
            dve.memset(minus_half[:, :], -0.5).then_inc(n_["half_ready2"], 1)
            dve.wait_ge(n_["consts_loaded"], 16 * (1 + len(CONSTS)))
            dve.tensor_copy(ident16[:, :], ident[:, :])
            dve.tensor_copy(future16[:, :, :], future_in[:, :].rearrange("p (o n) -> p o n", o=1).broadcast_to([128, G, 128]))
            dve.tensor_tensor(gain_sq[:, :], gain[:, :], gain[:, :], ALU.mult).then_inc(n_["gain_step_done"], 1)
            dve.wait_ge(n_["gain_step_done"], 1)
            dve.tensor_reduce(gain_top[:, :], gain_sq[:, :], AX.X, ALU.max).then_inc(n_["gain_step_done"], 1)
            dve.wait_ge(n_["gain_step_done"], 2)
            dve.tensor_scalar(bounded[:, :], gain_top[:, :], SAFE_GAIN ** 2, None, ALU.is_le).then_inc(n_["bounded_ready"], 1)
            SCALE, ROOT = HALF ** -0.5 * HD ** 0.5, HD ** 0.5
            for t in range(T):
                for s in range(2):
                    for table, c, sign in ((rope_cos, 0, 1.0), (rope_sin, 1, 1.0 - 2.0 * s)):
                        row = trig[:, c, t, :].rearrange("p (o d) -> p o d", o=1)
                        dve.scalar_tensor_tensor(
                            out=table[:, t, 0:HEADS, s, :], in0=row.broadcast_to([128, HEADS, HALF]), scalar=SCALE * sign,
                            in1=gain[:, :].rearrange("p (h o) -> p h o", o=1).broadcast_to([128, HEADS, HALF]),
                            op0=ALU.mult, op1=ALU.mult)
                        last = dve.tensor_scalar(table[:, t, HEADS:, s, :], row.broadcast_to([128, G, HALF]), ROOT * sign, None, ALU.mult)
            last.then_inc(n_["tables_ready"], 1)

            def project(b):
                x_heads = qkvg[:, :, 0:QK].rearrange("p t (h c) -> p t h c", c=HD)
                n3 = normed[:, :, :, :, :].rearrange("p t h s d -> p (t h) (s d)")
                dve.wait_ge(n_["qkvg_ready"], b + 1)
                dve.tensor_tensor(square[:, :, :], qkvg[:, :, 0:QK], qkvg[:, :, 0:QK], ALU.mult).then_inc(n_["square_done"], 1)
                dve.wait_ge(n_["square_done"], b + 1)
                dve.tensor_reduce(mean_sq[:, :], square[:, :, :].rearrange("p t (h c) -> p (t h) c", c=HD), AX.X, ALU.add)\
                   .then_inc(n_["mean_sq_done"], 1)
                dve.wait_ge(n_["gate_exp_ready"], b + 1)
                dve.tensor_scalar(gate_den[:, :, :], gate_exp[:, :, :], 1.0, None, ALU.add).then_inc(n_["gate_den_done"], 1)
                dve.wait_ge(n_["gate_den_done"], b + 1)
                dve.reciprocal(gate[:, :, :], gate_den[:, :, :]).then_inc(n_["gate_done"], 1)
                dve.wait_ge(n_["rstd_ready"], b + 1)
                r4 = rstd[:, :].rearrange("p (t h o) -> p t h o", t=T, o=1).broadcast_to([128, T, HEADS + G, HD])
                dve.tensor_tensor(normed[:, :, :, :, :].rearrange("p t h s d -> p t h (s d)"), x_heads, r4, ALU.mult)\
                   .then_inc(n_["normed_done"], 1)
                dve.wait_ge(n_["normed_done"], b + 1)
                flat = lambda a: a.rearrange("p t h s d -> p (t h s d)")
                dve.tensor_tensor(flat(turned[:, :, :, :, :]), flat(normed[:, :, :, :, :]), flat(rope_cos[:, :, :, :, :]), ALU.mult)\
                   .then_inc(n_["cos_done"], 1)
                swap = lambda a: a.rearrange("p t h s d -> p (t h) s d")
                dve.tensor_tensor(swap(turned2[:, :, :, :, :]), swap(normed[:, :, :, :, :])[:, :, ::-1, :],
                                  swap(rope_sin[:, :, :, :, :]), ALU.mult).then_inc(n_["sin_done"], 1)

            def rotate(b):
                dve.wait_ge(n_["sin_done"], b + 1)
                for t in range(T):
                    q0, k0 = t * R * 2 * G, NQ + t * 2 * G
                    by_unit = lambda a: a[:, t, 0:HEADS, :, :].rearrange("p (g r) s d -> p (r s) g d", g=G)
                    dve.tensor_tensor(roped[:, q0:q0 + R * 2 * G, :].rearrange("p (n g) d -> p n g d", g=G),
                                      by_unit(turned), by_unit(turned2), ALU.add)
                    by_unit = lambda a: a[:, t, HEADS:, :, :].rearrange("p g s d -> p s g d")
                    last = dve.tensor_tensor(roped[:, k0:k0 + 2 * G, :].rearrange("p (s g) d -> p s g d", g=G),
                                             by_unit(turned), by_unit(turned2), ALU.add)
                last.then_inc(n_["roped_done"], 1)

            def split(b):
                def slots(lo, n, a, b_, src):
                    dst = parts[:, a:b_, lo:lo + n, :]
                    src = src[:, a:b_, :].rearrange("p u (o d) -> p u o d", o=1)
                    return dst, (src.broadcast_to([128, b_ - a, n, HALF]) if n > 1 else src)
                N = NQ + NK
                dve.wait_ge(n_["roped_done"], b + 1)
                reach(dve, n_["k_turned"], b)
                dve.tensor_copy(*slots(0, 1, 0, N, roped)).then_inc(n_["part0_done"], 1)
                dve.tensor_copy(*slots(1, 2, 0, NQ, roped))
                dve.tensor_copy(*slots(4, 2, NQ, N, roped))
                dve.wait_ge(n_["part0_done"], b + 1)
                dve.tensor_tensor(rest1[:, :, :], roped[:, :, :], parts[:, :, 0, :], ALU.subtract).then_inc(n_["rest1_done"], 1)
                dve.wait_ge(n_["rest1_done"], b + 1)
                dve.tensor_copy(*slots(3, 1, 0, N, rest1)).then_inc(n_["part1_done"], 1)
                dve.tensor_copy(*slots(4, 1, 0, NQ, rest1))
                dve.tensor_copy(*slots(1, 1, NQ, N, rest1))
                dve.wait_ge(n_["part1_done"], b + 1)
                dve.tensor_tensor(parts[:, 0:NQ, 5, :], rest1[:, 0:NQ, :], parts[:, 0:NQ, 3, :], ALU.subtract)
                dve.tensor_tensor(parts[:, NQ:N, 2, :], rest1[:, NQ:N, :], parts[:, NQ:N, 3, :], ALU.subtract)\
                   .then_inc(n_["parts_ready"], 1)

            def gate_values(b, p):
                dve.wait_ge(n_["gate_done"], b + 1)
                dve.tensor_tensor(values[p][:, :, :, :, PAD:PAD + HALF].rearrange("p t g s d -> p t (g s) d"),
                                  qkvg[:, :, QK:QK + KV].rearrange("p t (n d) -> p t n d", d=HALF),
                                  gate[:, :, :].rearrange("p t (n d) -> p t n d", d=HALF), ALU.mult)\
                   .then_inc(n_["values_ready"], 1)

            def copy_queries(b, p, suffix=""):
                for t, bank in enumerate((MB16, MC16)):
                    dve.wait_ge(n_[f"q{t}_turned{suffix}"], b + 1)
                    dve.tensor_copy(qT[p][:, t, :, :, :].rearrange("p r s n -> p (r s n)"), bank[:, :])\
                       .then_inc(n_[f"q{t}_ready{suffix}"], 1)

            def copy_keys(b, p):
                dve.wait_ge(n_["k_turned"], b + 1)
                for g in range(G):
                    q = slice(32 * g, 32 * g + 32)
                    last = dve.tensor_copy(kT[p][q, g, :, :, :].rearrange("p t s n -> p (t s n)"), MA16[q, 0:T * 2 * 128])
                last.then_inc(n_["k_ready"], 1)

            def subtract_maximum(b, p):
                for k in range(len(KINDS)):
                    for n in range(R * 2):
                        dve.wait_ge(n_["block_scored"], b * BLOCKS + k * R * 2 + n + 1)
                        dve.tensor_reduce(block_max[:, k, n * G:(n + 1) * G], (MB, MC)[n % 2][:, :].rearrange("p (g n) -> p g n", g=G),
                                          AX.X, ALU.max).then_inc(n_["block_max_done"], 1)
                dve.wait_ge(n_["block_max_done"], (b + 1) * BLOCKS)
                dve.tensor_scalar(row_max[:, 0:NQ // 2], block_max[:, 0, :], 1.0, None, ALU.mult)
                dve.tensor_tensor(row_max[:, NQ // 2:], block_max[:, 1, :], block_max[:, 2, :], ALU.max).then_inc(n_["max_step_done"], 1)
                dve.wait_ge(n_["max_step_done"], b * 6 + 1)
                dve.tensor_scalar(minus_max[:, :], row_max[:, :], -1.0, None, ALU.mult).then_inc(n_["max_step_done"], 1)
                slot = lambda d: parts[:, 0:NQ, 6, d]
                dve.wait_ge(n_["max_step_done"], b * 6 + 2)
                dve.tensor_copy(slot(0), minus_max[:, :]).then_inc(n_["max_step_done"], 1)
                dve.wait_ge(n_["max_step_done"], b * 6 + 3)
                dve.tensor_tensor(row_max[:, :], minus_max[:, :], slot(0), ALU.subtract).then_inc(n_["max_step_done"], 1)
                dve.wait_ge(n_["max_step_done"], b * 6 + 4)
                dve.tensor_copy(slot(1), row_max[:, :]).then_inc(n_["max_step_done"], 1)
                dve.wait_ge(n_["max_step_done"], b * 6 + 5)
                dve.tensor_tensor(minus_max[:, :], row_max[:, :], slot(1), ALU.subtract).then_inc(n_["max_step_done"], 1)
                dve.wait_ge(n_["max_step_done"], b * 6 + 6)
                dve.tensor_copy(slot(2), minus_max[:, :]).then_inc(n_["max_parts_ready"], 1)
                copy_queries(b, p, "_max")
                dve.memset(parts[:, 0:NQ, 6, 0:3], 0.0).then_inc(n_["slot_cleared"], 1)

            def copy_outputs(b):
                dve.wait_ge(pv_done[2][1], b + 1)
                dve.tensor_copy(o_sb[:, :], O[:, :]).then_inc(n_["o_ready"], 1)

            def normalize_heads(b):
                turned_o = MB[:, :].rearrange("p (n c) -> p n c", c=32)[:, :, 0:4 * OUTROW]\
                    .rearrange("p n (w c) -> p n w c", c=OUTROW)
                dve.wait_ge(n_["o_turned"], b + 1)
                dve.reciprocal(rden[:, :, :], turned_o[:, :, :, HALF]).then_inc(n_["rden_done"], 1)
                dve.wait_ge(n_["rden_done"], b + 1)
                for t in range(T):
                    last = dve.tensor_tensor(
                        heads[:, t, :].rearrange("p (n s d) -> p n s d", s=2, d=HALF),
                        turned_o[:, :, 2 * t:2 * t + 2, 0:HALF],
                        rden[:, :, 2 * t:2 * t + 2].rearrange("p n (s o) -> p n s o", o=1).broadcast_to([128, R * G, 2, HALF]),
                        ALU.mult)
                last.then_inc(n_["heads_done"], 1)

            def add_residual(b, p, half_b):
                dve.wait_ge(n_["projected"], b + 1)
                dve.wait_ge(res_loaded[p], (half_b + 1) * 16)
                dve.tensor_tensor(summed[:, :, :].rearrange("p t d -> p (t d)"), MA[:, 0:T * 128],
                                  x_res[p][:, :, :].rearrange("p t d -> p (t d)"), ALU.add).then_inc(n_["summed_done"], 1)
                dve.wait_ge(n_["summed_done"], b + 1)
                for t in range(T):
                    last = dve.bn_stats(stats[:, t, :], summed[:, t, :])
                last.then_inc(n_["stats_done"], 1)
                reach_alone(dve, n_["stats_done"], b + 1, n_["zeros_ready"])
                for t in range(T):
                    last = dve.bn_aggr(moments[:, t, :], stats[:, t, :])
                last.then_inc(n_["moments_done"], 1)

            def normalize(b):
                dve.wait_ge(n_["ln_rstd_ready"], b + 1)
                reach(dve, n_["x1_turned"], b)
                for t in range(T):
                    last = dve.tensor_scalar(x1[:, t, :], summed[:, t, :], moments[:, t, 0:1], ln_rstd[:, t:t + 1],
                                             ALU.subtract, ALU.mult)
                last.then_inc(n_["x1_ready"], 1)

            def keep_x1(b):
                at = b * SEQ
                dve.wait_ge(n_["x1_turned"], b + 1)
                dve.tensor_scalar(X0[:, bass.ds(at, SEQ)], MB[:, 0:SEQ], 1.0, None, ALU.mult).then_inc(n_["X0_ready"], 1)
                dve.tensor_reduce(xsum[:, bass.ds(b, 1)], MB[:, 0:SEQ], AX.X, ALU.add).then_inc(n_["xsum_ready"], 1)

            def attend(b, p, half_b, general):
                first, second, last = (isinstance(b, int) and b == n for n in (0, 1, BATCH - 1))
                if not first and not second:
                    keep_x1(b - 2)
                if not last:
                    project(b + 1)
                    rotate(b + 1)
                if not first:
                    copy_outputs(b - 1)
                if not last:
                    gate_values(b + 1, 1 - p)
                if not first:
                    normalize_heads(b - 1)
                if not last:
                    split(b + 1)
                if not first:
                    add_residual(b - 1, 1 - p, half_b - (1 - p))
                if not last:
                    copy_queries(b + 1, 1 - p)
                    copy_keys(b + 1, 1 - p)
                    if general:
                        subtract_maximum(b + 1, 1 - p)
                if not first:
                    normalize(b - 1)

            dve.tensor_scalar(mix[:, 0:1], lam[:, :], sel_s[:, 1:2], sel_s[:, 0:1], ALU.mult, ALU.add)
            dve.tensor_scalar(mix[:, 1:2], lam[:, :], sel_s[:, 2:3], sel_s[:, 0:1], ALU.mult, ALU.add).then_inc(n_["w_out_step_done"], 1)
            dve.wait_ge(n_["w_out_step_done"], 1)
            dve.tensor_scalar(w_out[:, :], w_o1[:, :], mix[:, 0:1], None, ALU.mult).then_inc(n_["w_out_step_done"], 1)
            dve.wait_ge(n_["w_out_step_done"], 2)
            dve.scalar_tensor_tensor(out=w_out[:, :], in0=w_o0[:, :], scalar=mix[:, 1:2], in1=w_out[:, :],
                                     op0=ALU.mult, op1=ALU.add).then_inc(n_["w_out_step_done"], 1)
            dve.wait_ge(n_["tables_ready"], 1)
            dve.wait_ge(n_["zeros_ready"], 1)

            def attention(general):
                project(0)
                rotate(0)
                gate_values(0, 0)
                split(0)
                copy_queries(0, 0)
                copy_keys(0, 0)
                if general:
                    subtract_maximum(0, 0)
                batches(dve, lambda b, p, half_b: attend(b, p, half_b, general))
                last_b = BATCH - 1
                keep_x1(last_b - 1)
                copy_outputs(last_b)
                normalize_heads(last_b)
                add_residual(last_b, 1, BATCH // 2 - 1)
                normalize(last_b)
                keep_x1(last_b)

            is_bounded = dve.value_load(bounded[0:1, 0:1], min_val=0, max_val=1)
            with dve.If(is_bounded > 0):
                attention(False)
            with dve.Else():
                attention(True)

            dve.wait_ge(n_["ffn_loaded"], 16 * FFN_LOADS)
            dve.tensor_scalar(arange7[:, :], arange_in[0:4, :], 0.7, None, ALU.mult)
            dve.tensor_scalar(spread[:, :, :], pick[:, :, :], 1.0, None, ALU.mult).then_inc(n_["pick_done"], 1)
            dve.wait_ge(n_["pick_done"], 1)
            dve.tensor_scalar(spread[0:4, :, :], pick[0:4, :, :], arange_in[0:4, :], 0.3, ALU.mult, ALU.mult)\
               .then_inc(n_["spread_ready"], 1)
            dve.wait_ge(n_["X0_ready"], BATCH)
            for q, (src, sign) in enumerate(((2, 1.0), (3, -1.0), (0, -1.0), (1, 1.0))):
                last = dve.tensor_scalar(Y[32 * q:32 * q + 32, :], X0[32 * src:32 * src + 32, :], sign, None, ALU.mult)
            last.then_inc(n_["XY_ready"], 1)
            dve.wait_ge(n_["tanh_g_ready"], 1)
            dve.wait_ge(n_["zeros_ready"], 3)
            dve.wait_ge(n_["spread_ready"], 1)
            for h in range(2):
                last = dve.tensor_scalar(coup[h][32:36, :].rearrange("p (n c) -> p n c", n=2),
                                         tanh_g[:, 2 * h:2 * h + 2].rearrange("p (n o) -> p n o", o=1).broadcast_to([4, 2, SEQ]),
                                         arange7[:, :], 0.1, ALU.mult, ALU.add)
            last.then_inc(n_["coup_ready"], 1)
            dve.wait_ge(n_["XY_ready"], 1)

            def half_cycle(u, h, first, last):
                for j in range(4):
                    at = slice(h * 2048 + j * 512, h * 2048 + (j + 1) * 512)
                    c = (O, MC)[j % 2]
                    old = X0 if first else X
                    dve.wait_ge(spread_done[j], u + 1)
                    dve.tensor_tensor(cY[:, j % 2, :], c[:, :], Y[:, at], ALU.mult).then_inc(cY_done[j], 1)
                    if not last:
                        if j >= 2:
                            dve.wait_ge(Y_done[j - 2], u + 1)
                        elif u >= 1:
                            dve.wait_ge(Y_done[j + 2], u)
                        dve.tensor_tensor(cX[:, j % 2, :], c[:, :], old[:, at], ALU.mult).then_inc(cX_done[j], 1)
                        dve.wait_ge(cY_done[j], u + 1)
                        dve.tensor_tensor(X[:, at], old[:, at], cY[:, j % 2, :], ALU.add).then_inc(X_done[j], 1)
                    else:
                        dve.wait_ge(cY_done[j], u + 1)
                        dve.wait_ge(n_["sum_ready"], (u - 4) * 4 + j + 1)
                        dve.tensor_tensor(X0[:, at], X0[:, at], cY[:, j % 2, :], ALU.add).then_inc(X_done[j], 1)

            def stats_of(f):
                dve.wait_ge(n_["turned_back"], f + 1)
                if f >= 2:
                    dve.wait_ge(n_["result_ready"], f - 1)
                bank = S[(f % 4) // 2][:, f % 2, :]
                for t in range(4):
                    last = dve.bn_stats(f_stats[:, f % 2, t, :], bank[:, t * 128:(t + 1) * 128])
                last.then_inc(n_["f_stats_done"], 1)
                dve.wait_ge(n_["f_stats_done"], f + 1)
                for t in range(4):
                    last = dve.bn_aggr(f_mom[:, f % 2, t, :], f_stats[:, f % 2, t, :])
                last.then_inc(n_["f_moments_done"], 1)

            cycles(dve, half_cycle)
            for f in range(8):
                stats_of(f)

        @block.gpsimd
        def _(pool):
            for p in range(2):
                pool.memset(kT[p][:, :, :, :, :], 0.0)
                pool.memset(values[p][:, :, :, :, :], 0.0)
            pool.memset(parts[:, :, :, :], 0.0).then_inc(n_["zeros_done"], 1)
            pool.wait_ge(n_["zeros_done"], 1)
            for p in range(2):
                pool.memset(values[p][:, :, :, :, PAD + HALF:PAD + OUTROW], 1.0)
            pool.memset(parts[:, NQ:, 6, 0:3], 1.0).then_inc(n_["zeros_ready"], 1)
            pool.memset(cn_w3[:, :], 0.0)
            pool.memset(cn_w4[:, :], 0.0).then_inc(n_["zeros_ready"], 1)
            for h in range(2):
                last = pool.memset(coup[h][:, :], 0.0)
            last.then_inc(n_["zeros_ready"], 1)

            def root(count, mean, eps, shifted, sem_in, sem_mid, out_, sem_out):
                n = shifted.shape[-1]
                pool.wait_ge(sem_in, count)
                pool.tensor_tensor(shifted, mean, eps[:, 0:n], ALU.add).then_inc(sem_mid, 1)
                pool.wait_ge(sem_mid, count)
                pool.tensor_tensor(out_, shifted, minus_half[:, 0:n], ALU.pow).then_inc(sem_out, 1)

            def mask(count, k, g):
                reach_alone(pool, exp_done[k][g], count, n_["zeros_ready"])
                p = probs[:, k, g, :, :].rearrange("p s (r q) -> p (s r) q", q=128)
                pool.affine_select(out=p, in_=p, compare_op=ALU.is_ge, fill=0.0, base=0,
                                   pattern=[[0, 2 * R], [1, 128]], channel_multiplier=-1).then_inc(masked[k][g], 1)

            def attend(now, first, last):
                mask(now, 0, 0)
                if not last:
                    root(now + 1, mean_sq[:, :], rms_eps, mean_eps[:, :], n_["mean_sq_done"], n_["mean_eps_done"],
                         rstd[:, :], n_["rstd_ready"])
                for g in range(1, G):
                    mask(now, 0, g)
                mask(now, 2, 0)
                mask(now, 2, 1)
                if not first:
                    root(now - 1, moments[:, :, 1], ln_eps, var_eps[:, :], n_["moments_done"], n_["var_eps_done"],
                         ln_rstd[:, :], n_["ln_rstd_ready"])
                mask(now, 2, 2)
                mask(now, 2, 3)

            pool.wait_ge(n_["half_ready2"], 1)
            root(1, mean_sq[:, :], rms_eps, mean_eps[:, :], n_["mean_sq_done"], n_["mean_eps_done"],
                 rstd[:, :], n_["rstd_ready"])
            attend(1, True, False)
            attend(2, False, False)
            with pool.Fori(3, BATCH - 1) as now:
                attend(now, False, False)
            attend(BATCH - 1, False, False)
            attend(BATCH, False, True)
            last_b = BATCH - 1
            root(last_b + 1, moments[:, :, 1], ln_eps, var_eps[:, :], n_["moments_done"], n_["var_eps_done"],
                 ln_rstd[:, :], n_["ln_rstd_ready"])

            pool.wait_ge(n_["XY_ready"], 1)

            def half_cycle(u, h, first, last):
                for j in range(4):
                    at = slice(h * 2048 + j * 512, h * 2048 + (j + 1) * 512)
                    if not last:
                        pool.wait_ge(cX_done[j], u + 1)
                        pool.tensor_tensor(Y[:, at], Y[:, at], cX[:, j % 2, :], ALU.subtract).then_inc(Y_done[j], 1)
                    else:
                        pool.wait_ge(X_done[j], u - 1)
                        pool.tensor_tensor(X0[:, at], X0[:, at], X[:, at], ALU.add).then_inc(n_["sum_ready"], 1)

            cycles(pool, half_cycle)
            for f in range(8):
                pool.wait_ge(n_["f_moments_done"], f + 1)
                pool.tensor_tensor(f_var[:, f % 2, :], f_mom[:, f % 2, :, 1], ln_eps[:, :], ALU.add).then_inc(n_["f_norm_step_done"], 1)
                pool.wait_ge(n_["f_norm_step_done"], 4 * f + 1)
                pool.tensor_tensor(f_rstd[:, f % 2, :], f_var[:, f % 2, :], minus_half[:, 0:4], ALU.pow).then_inc(n_["f_norm_step_done"], 1)
                pool.wait_ge(n_["f_norm_step_done"], 4 * f + 2)
                pool.tensor_tensor(f_var[:, f % 2, :], f_mom[:, f % 2, :, 0], f_rstd[:, f % 2, :], ALU.mult).then_inc(n_["f_norm_step_done"], 1)
                pool.wait_ge(n_["f_norm_step_done"], 4 * f + 3)
                pool.tensor_scalar(f_shift[:, f % 2, :], f_var[:, f % 2, :], -1.0, None, ALU.mult).then_inc(n_["f_norm_step_done"], 1)


FFN_LOADS = 20


def constants():
    import math
    import numpy as np
    pos = np.arange(SEQ, dtype=np.float32)
    angles = (np.arange(0, HD, 2, dtype=np.float32) / np.float32(HD) * np.float32(math.pi)).astype(np.float32)
    ang = pos[:, None] * angles[None, :]
    radius = np.float32(1.0) / (np.float32(1.0) + pos[:, None] * np.float32(0.01))
    table = np.stack([radius * np.cos(ang), radius * np.sin(ang)]).astype(np.float32)
    trig = table.reshape(2, T, 128, HALF).transpose(2, 0, 1, 3)
    s = (np.arange(128) // HALF) % 2
    sel_s = np.stack([s == 0, s == 1, -(s == 1).astype(np.float32)], 1).astype(np.float32)
    pick = np.zeros((36, 4, 128), np.float32)
    for c in range(4):
        pick[c, c] = 1.0
        pick[32 + c, c] = 1.0
    return dict(ident=np.eye(128, dtype=np.float32), trig=np.ascontiguousarray(trig), sel_s=sel_s, pick=pick,
                future=np.triu(np.full((128, 128), FUTURE, np.float32), 1))


def kernel(**inputs):
    import numpy as np
    import concourse.bacc as bacc
    from concourse.bass_utils import run_bass_kernel_spmd
    I = {k.replace("L0_attn_", "").replace("L0_ffn_", ""): np.asarray(v) for k, v in inputs.items()}
    x = I["x"]
    woT = np.transpose(I["Wo"]).reshape(G, R, 2, HALF, DIM).transpose(1, 0, 2, 3, 4)

    def by_head(a):
        return np.broadcast_to(a.reshape(G, R).T[:, :, None, None], (R, G, 2, HALF)).reshape(128, 1)

    def both(half):
        return np.broadcast_to(woT[:, :, half:half + 1], (R, G, 2, HALF, DIM)).reshape(128, DIM)

    col = lambda a, n: np.tile(a.reshape(-1, 1), (n, 1))
    arrays = dict(
        x=x, xT=np.transpose(x, (0, 2, 1)),
        w_proj=np.concatenate([np.transpose(I[n]) for n in ("Wq", "Wk", "Wv", "Wg")], 1),
        w_o0=both(0), w_o1=both(1), lam=by_head(I["lambda_param"]),
        gain=np.broadcast_to(I["q_gain"][None, :], (128, HEADS)),
        cn_w1=I["cn_w1"], cn_w2=I["cn_w2"], cn_w3=I["cn_w3"], cn_w4=I["cn_w4"],
        cn_b1=col(I["cn_b1"], 1), cn_b2=col(I["cn_b2"], 2), cn_b3=col(I["cn_b3"], 4), cn_b4=col(I["cn_b4"], 4),
        gc_w1=I["gc_w1"], gc_w2=I["gc_w2"], gc_w3=I["gc_w3"],
        gc_b1=col(I["gc_b1"], 1), gc_b2=col(I["gc_b2"], 1), gc_b3=col(I["gc_b3"], 4),
        arange_in=col(I["adaptive_range"], 128), **constants())
    arrays = {k: np.ascontiguousarray(v) for k, v in arrays.items()}
    nc = bacc.Bacc("TRN2", target_bir_lowering=False, num_devices=1)
    aps = {k: nc.dram_tensor(f"in_{k}", v.shape, mybir.dt.from_np(v.dtype), kind="ExternalInput").ap()
           for k, v in arrays.items()}
    out = nc.dram_tensor("out", (TOK, DIM), F32, kind="ExternalOutput").ap()
    block_kernel(nc, aps, out)
    r = run_bass_kernel_spmd(nc, [{f"in_{k}": v for k, v in arrays.items()}], core_ids=[0])
    return r.results[0]["out"].reshape(BATCH, SEQ, DIM)
```

```python
import concourse.bass as bass
from concourse import mybir
from contextlib import ExitStack

F32 = mybir.dt.float32
BF16 = mybir.dt.bfloat16
I32 = mybir.dt.int32
ALU = mybir.AluOpType
ACT = mybir.ActivationFunctionType
AX = mybir.AxisListType

BATCH, SEQ, DIM = 16, 256, 128
HEADS, G, HD = 16, 4, 8
R = HEADS // G
HALF = HD // 2
T = SEQ // 128
KV = G * HD
QK = DIM + KV
PROJ = DIM + 3 * KV
SLOTS = 8
OUTROW = HALF + 1
PAD = 3 * OUTROW
VWIDTH = PAD + 32
SAFE_GAIN = 8.0
FUTURE = -1e30
CYCLES = 3
TOK = BATCH * SEQ
NEWTON = 3
ROOT_BITS = float(0x5F3759DF)
LN_EPS = 1e-5
RMS_EPS = 1.1920928955078125e-07

KINDS = [(0, 0), (0, 1), (1, 1)]
DIAGONAL = (0, 2)
MASKED_ON_PE = (3,)
BLOCKS = len(KINDS) * R * 2


def reach(eng, sem, n):
    if not isinstance(n, int) or n > 0:
        eng.wait_ge(sem, n)


def reach_alone(eng, sem, n, zeros_ready):
    eng.wait_ge(zeros_ready, 1)
    reach(eng, sem, n)


def block_kernel(nc, A, out):
    ctx = ExitStack()
    with ctx:
        def sb(name, shape, dt=F32):
            return ctx.enter_context(nc.sbuf_tensor(name, shape, dt))

        def ps(name, shape, dt=F32):
            return ctx.enter_context(nc.psum_tensor(name, shape, dt))

        def sem(name):
            return ctx.enter_context(nc.semaphore(name))

        ident = sb("ident", [128, 128])
        ident16 = sb("ident16", [128, 128], BF16)
        future_in = sb("future_in", [128, 128])
        future16 = sb("future16", [128, G, 128], BF16)
        gain_sq = sb("gain_sq", [128, HEADS])
        gain_top = sb("gain_top", [128, 1])
        bounded = sb("bounded", [128, 1], I32)
        w_proj = sb("w_proj", [128, PROJ])
        w_o0 = sb("w_o0", [128, DIM])
        w_o1 = sb("w_o1", [128, DIM])
        w_out = sb("w_out", [128, DIM])
        lam = sb("lam", [128, 1])
        sel_s = sb("sel_s", [128, 3])
        mix = sb("mix", [128, 2])
        gain = sb("gain", [128, HEADS])
        trig = sb("trig", [128, 2, T, HALF])
        rope_cos = sb("rope_cos", [128, T, HEADS + G, 2, HALF])
        rope_sin = sb("rope_sin", [128, T, HEADS + G, 2, HALF])
        minus_half = sb("minus_half", [128, T * (HEADS + G)])
        ln_eps = sb("ln_eps", [128, 4])

        xT_in = [sb(f"xT_in{p}", [128, SEQ]) for p in range(2)]
        x_res = [sb(f"x_res{p}", [128, T, DIM]) for p in range(2)]
        qkvg = [sb(f"qkvg{p}", [128, T, PROJ]) for p in range(2)]
        square = sb("square", [128, T, QK])
        sum_sq = sb("sum_sq", [128, T * (HEADS + G)])
        sum_eps = sb("sum_eps", [128, T * (HEADS + G)])
        estimate = [sb(f"estimate{n}", [128, T * (HEADS + G)]) for n in range(NEWTON)]
        root_sq = sb("root_sq", [128, T * (HEADS + G)])
        root_step = sb("root_step", [128, T * (HEADS + G)])
        minus_half_sum = sb("minus_half_sum", [128, T * (HEADS + G)])
        rstd = sb("rstd", [128, T, HEADS + G, 2])
        rotated = sb("rotated", [128, T, QK])
        one_half = sb("one_half", [128, T * (HEADS + G)])
        turned = sb("turned", [128, T, HEADS + G, 2, HALF])
        turned2 = sb("turned2", [128, T, HEADS + G, 2, HALF])
        NQ = T * R * 2 * G
        NK = T * 2 * G
        roped = sb("roped", [128, NQ + NK, HALF])
        rest1 = sb("rest1", [128, NQ + NK, HALF])
        parts = sb("parts", [128, NQ + NK, SLOTS, HALF], BF16)
        block_max = sb("block_max", [128, len(KINDS), R * 2 * G])
        row_max = sb("row_max", [128, NQ])
        minus_max = sb("minus_max", [128, NQ])
        gate = [sb(f"gate{p}", [128, T, KV]) for p in range(2)]
        qT = [sb(f"qT{p}", [128, T, R, 2, 128], BF16) for p in range(2)]
        kT = [sb(f"kT{p}", [128, G, T, 2, 128], BF16) for p in range(2)]
        values = [sb(f"values{p}", [128, T, G, 2, VWIDTH]) for p in range(2)]

        probs = sb("probs", [128, len(KINDS), G, 2, R * 128])
        o_sb = sb("o_sb", [128, R * 128])
        rden = sb("rden", [128, R * G, T * 2])
        heads = sb("heads", [128, T, DIM])
        headsT = sb("headsT", [128, T * 128])
        summed = sb("summed", [128, T, DIM])
        stats = sb("stats", [128, T, 6])
        moments = sb("moments", [128, T, 2])
        var_eps = sb("var_eps", [128, T])
        ln_rstd = sb("ln_rstd", [128, T])
        x1 = sb("x1", [128, T, DIM])
        X0 = sb("X0", [128, TOK])
        xsum = sb("xsum", [128, BATCH])

        X = sb("X", [128, TOK])
        Y = sb("Y", [128, TOK])
        cn_w1 = sb("cn_w1", [128, 128])
        cn_w2 = sb("cn_w2", [128, 64])
        cn_w3 = sb("cn_w3", [128, 64])
        cn_w4 = sb("cn_w4", [128, 4])
        cn_b1 = sb("cn_b1", [128, 1])
        cn_b2 = sb("cn_b2", [128, 1])
        cn_b3 = sb("cn_b3", [128, 1])
        cn_b4 = sb("cn_b4", [4, 2])
        gc_w1 = sb("gc_w1", [128, 64])
        gc_w2 = sb("gc_w2", [64, 32])
        gc_w3 = sb("gc_w3", [32, 1])
        gc_b1 = sb("gc_b1", [64, 1])
        gc_b2 = sb("gc_b2", [32, 1])
        gc_b3 = sb("gc_b3", [4, 2])
        arange_in = sb("arange_in", [128, 1])
        arange7 = sb("arange7", [4, 1])
        spread = sb("spread", [36, 4, 128])
        pick = sb("pick", [36, 4, 128])
        hg1 = sb("hg1", [64, BATCH])
        hg2 = sb("hg2", [32, BATCH])
        tanh_g = sb("tanh_g", [4, 4])
        h1 = sb("h1", [128, 4 * 512])
        h2 = sb("h2", [128, 2 * 512])
        h3 = sb("h3", [128, 512])
        coup = [sb(f"coup{h}", [36, 512]) for h in range(2)]
        cY = sb("cY", [128, 2, 512])
        cX = sb("cX", [128, 2, 512])
        f_stats = sb("f_stats", [128, 2, 4, 6])
        f_mom = sb("f_mom", [128, 2, 4, 2])
        f_var = sb("f_var", [128, 2, 4])
        f_rstd = sb("f_rstd", [128, 2, 4])
        f_shift = sb("f_shift", [128, 2, 4])
        result = sb("result", [128, 4, 4, DIM])

        S = [ps(f"S{i}", [128, 2, R * 128]) for i in range(2)]
        O = ps("O", [128, R * 128])
        MA = ps("MA", [128, 512])
        MB = ps("MB", [128, 512])
        MC = ps("MC", [128, 512])
        MB16 = MB[:, :].bitcast(BF16)
        MC16 = MC[:, :].bitcast(BF16)

        names = ("consts_loaded ffn_loaded tables_ready zeros_ready half_ready "
                 "proj_done qkvg_ready gate_ready values_ready "
                 "square_done sum_sq_done sum_eps_done estimate_ready root_step_done rstd_ready turned_done rotated_done roped_done "
                 "part0_done rest1_done part1_done parts_ready gain_step_done bounded_ready slot_cleared "
                 "block_scored block_max_done max_step_done max_parts_ready "
                 "q0_turned_max q1_turned_max q0_ready_max q1_ready_max "
                 "q0_turned q1_turned k_turned q0_ready q1_ready k_ready k_ready_act "
                 "o_ready o_turned rden_done heads_done heads_turned headsT_ready projected summed_done "
                 "stats_done moments_done var_eps_done ln_rstd_ready x1_ready x1_turned X0_ready xsum_ready "
                 "zeros_done half_ready2 w_out_step_done pick_done g1_done hg1_ready g2_done hg2_ready g3_done tanh_g_ready coup_ready spread_ready XY_ready "
                 "h3_done gelu3_done z_done tanh_ready sum_ready "
                 "turned_back f_stats_done f_moments_done f_norm_step_done result_ready").split()
        n_ = {n: sem(n) for n in names}
        xT_loaded = [sem(f"xT_loaded{p}") for p in range(2)]
        res_loaded = [sem(f"res_loaded{p}") for p in range(2)]
        scores_done = [[sem(f"scores_done_{k}{g}") for g in range(G)] for k in range(3)]
        exp_done = [[sem(f"exp_done_{k}{g}") for g in range(G)] for k in range(3)]
        masked = {k: [sem(f"masked_{k}{g}") for g in range(G)] for k in DIAGONAL}
        pv_done = [[sem(f"pv_done_{k}{s}") for s in range(2)] for k in range(3)]
        h1_done = [sem(f"h1_done{c}") for c in range(2)]
        gelu1_done = [sem(f"gelu1_done{c}") for c in range(2)]
        h2_done = [sem(f"h2_done{c}") for c in range(2)]
        gelu2_done = [sem(f"gelu2_done{c}") for c in range(2)]
        spread_done = [sem(f"spread_done{c}") for c in range(4)]
        cY_done = [sem(f"cY_done{c}") for c in range(4)]
        cX_done = [sem(f"cX_done{c}") for c in range(4)]
        X_done = [sem(f"X_done{c}") for c in range(4)]
        Y_done = [sem(f"Y_done{c}") for c in range(4)]
        stored = [sem(f"stored{c}") for c in range(4)]
        block = ctx.enter_context(nc.Block())

        CONSTS = ("ident trig gain sel_s lam w_o0 w_o1 future".split())

        def batches(eng, step):
            step(0, 0, 0)
            step(1, 1, 0)
            with eng.Fori(1, BATCH // 2 - 1) as i:
                step(eng.snap(i * 2), 0, i)
                step(eng.snap(i * 2 + 1), 1, i)
            step(BATCH - 2, 0, BATCH // 2 - 1)
            step(BATCH - 1, 1, BATCH // 2 - 1)

        def cycles(eng, half_cycle):
            half_cycle(0, 0, True, False)
            half_cycle(1, 1, True, False)
            half_cycle(2, 0, False, False)
            half_cycle(3, 1, False, False)
            half_cycle(4, 0, False, True)
            half_cycle(5, 1, False, True)

        @block.sync
        def _(sp):
            sp.dma_start(w_proj[:, :], A["w_proj"]).then_inc(n_["consts_loaded"], 16)
            for p in range(2):
                sp.dma_start(xT_in[p][:, :], A["xT"][p]).then_inc(xT_loaded[p], 16)
            tiles = dict(ident=ident, trig=trig, gain=gain, sel_s=sel_s, lam=lam, w_o0=w_o0, w_o1=w_o1, future=future_in)
            for name in CONSTS:
                sp.dma_start(tiles[name][:], A[name]).then_inc(n_["consts_loaded"], 16)
            for p in range(2):
                sp.dma_start(x_res[p][:, :, :], A["x"][p].rearrange("(t p) d -> p t d", p=128)).then_inc(res_loaded[p], 16)

            def load_projected(n, p):
                src = A["xT"][bass.ds(n + 2, 1)].rearrange("o d s -> d (o s)")
                sp.wait_ge(n_["proj_done"], n + 1)
                sp.dma_start(xT_in[p][:, :], src).then_inc(xT_loaded[p], 16)

            def load_residual(n, p):
                res = A["x"][bass.ds(n + 2, 1)].rearrange("o (t p) d -> p (o t) d", p=128)
                sp.wait_ge(n_["summed_done"], n + 1)
                sp.dma_start(x_res[p][:, :, :], res).then_inc(res_loaded[p], 16)

            load_projected(0, 0)
            load_projected(1, 1)
            with sp.Fori(1, BATCH // 2 - 1) as i:
                load_projected(sp.snap(i * 2), 0)
                load_residual(sp.snap(i * 2 - 2), 0)
                load_projected(sp.snap(i * 2 + 1), 1)
                load_residual(sp.snap(i * 2 - 1), 1)
            sp.wait_ge(n_["zeros_ready"], 2)
            loads = [(cn_w1[:, :], "cn_w1"), (cn_w2[:, :], "cn_w2"), (cn_w3[0:64, 0:32], "cn_w3"),
                     (cn_w3[64:128, 32:64], "cn_w3"), (cn_b1[:, :], "cn_b1"), (cn_b2[:, :], "cn_b2"),
                     (cn_b3[:, :], "cn_b3"), (cn_b4[:, 0:1], "cn_b4"), (gc_w1[:, :], "gc_w1"), (gc_w2[:, :], "gc_w2"),
                     (gc_w3[:, :], "gc_w3"), (gc_b1[:, :], "gc_b1"), (gc_b2[:, :], "gc_b2"), (gc_b3[:, 0:1], "gc_b3"),
                     (arange_in[:, :], "arange_in"), (pick[:, :, :], "pick")]
            loads += [(cn_w4[32 * c:32 * c + 32, c:c + 1], "cn_w4") for c in range(4)]
            assert len(loads) == FFN_LOADS
            for dst, name in loads:
                sp.dma_start(dst, A[name]).then_inc(n_["ffn_loaded"], 16)
            load_residual(BATCH - 4, 0)
            load_residual(BATCH - 3, 1)
            for f in range(8):
                sp.wait_ge(n_["result_ready"], f + 1)
                sp.dma_start(out.rearrange("(f t p) d -> f p t d", t=4, p=128)[f], result[:, f % 4, :, :])\
                  .then_inc(stored[f % 4], 16)
            for c in range(4):
                sp.wait_ge(stored[c], 32)

        @block.tensor
        def _(pe):
            def project(b, p, half_b):
                reach(pe, n_["qkvg_ready"], b)
                reach(pe, n_["summed_done"], b - 3)
                pe.wait_ge(xT_loaded[p], (half_b + 1) * 16)
                for t in range(T):
                    mm = pe.matmul(MA[:, t * PROJ:(t + 1) * PROJ], xT_in[p][:, t * 128:(t + 1) * 128], w_proj[:, :],
                                   start=True, stop=True)
                mm.then_inc(n_["proj_done"], 1)

            def turn_queries(b, parts_in="parts_ready", turned="turned"):
                pe.wait_ge(n_[parts_in], b + 1)
                reach(pe, n_["heads_done"], b - 1)
                for t, bank in enumerate((MB16, MC16)):
                    for n in range(R * 2):
                        u = (t * R * 2 + n) * G
                        mm = pe.transpose(bank[:, n * 128:(n + 1) * 128],
                                          parts[:, u:u + G, :, :].rearrange("p u s d -> p (u s d)"), ident16[:, :])
                    mm.then_inc(n_[f"q{t}_{turned}"], 1)

            def turn_keys(b):
                pe.wait_ge(n_["parts_ready"], b + 1)
                pe.wait_ge(n_["q1_ready"], b + 1)
                for n in range(T * 2):
                    u = NQ + n * G
                    mm = pe.transpose(MC16[:, n * 128:(n + 1) * 128],
                                      parts[:, u:u + G, :, :].rearrange("p u s d -> p (u s d)"), ident16[:, :])
                mm.then_inc(n_["k_turned"], 1)

            def blocks_for_maximum(b, p):
                pe.wait_ge(n_["q0_ready"], b + 1)
                pe.wait_ge(n_["q1_ready"], b + 1)
                pe.wait_ge(n_["k_ready"], b + 1)
                pe.wait_ge(n_["k_ready_act"], b + 1)
                for k, (kt, qt) in enumerate(KINDS):
                    for n in range(R * 2):
                        if k * R * 2 + n >= 2:
                            pe.wait_ge(n_["block_max_done"], b * BLOCKS + k * R * 2 + n - 1)
                        r, s = n // 2, n % 2
                        bank = (MB, MC)[n % 2]
                        mm = pe.matmul(bank[:, :].rearrange("p (g n) -> p g n", g=G), qT[p][:, qt, r, s, :],
                                       kT[p][:, :, kt, s, :], start=True, stop=k not in DIAGONAL)
                        if k in DIAGONAL:
                            mm = pe.matmul(bank[:, :], ident16[:, :], future16[:, :, :].rearrange("p g n -> p (g n)"),
                                           start=False, stop=True)
                        mm.then_inc(n_["block_scored"], 1)
                turn_queries(b, "max_parts_ready", "turned_max")

            def scores(b, p, k, g, general):
                pair = k * G + g
                kt, qt = KINDS[k]
                if k == 0 and g == 0:
                    pe.wait_ge(n_["k_ready"], b + 1)
                    pe.wait_ge(n_["k_ready_act"], b + 1)
                    pe.wait_ge(n_["q0_ready_max" if general else "q0_ready"], b + 1)
                if k == 1 and g == 0:
                    pe.wait_ge(n_["q1_ready_max" if general else "q1_ready"], b + 1)
                if pair >= 2:
                    pe.wait_ge(exp_done[(pair - 2) // G][(pair - 2) % G], b + 1)
                else:
                    reach(pe, exp_done[2][2 + pair], b)
                for s in range(2):
                    late = k in DIAGONAL and (general or g in MASKED_ON_PE)
                    mm = pe.matmul(S[pair % 2][:, s, :], kT[p][:, g, kt, s, :], qT[p][:, qt, :, s, :],
                                   start=True, stop=not late)
                    if late:
                        mm = pe.matmul(S[pair % 2][:, s, :].rearrange("p (r n) -> p r n", r=R), future16[:, 0, :],
                                       ident16[:, :].rearrange("p (o n) -> p o n", o=1).broadcast_to([128, R, 128]),
                                       start=False, stop=True)
                mm.then_inc(scores_done[k][g], 1)

            def weigh(b, p, k, s):
                kt, qt = KINDS[k]
                first = k == 0 and s == 0
                if first:
                    pe.wait_ge(n_["values_ready"], b + 1)
                    reach(pe, n_["o_ready"], b)
                if s == 0:
                    for g in range(G):
                        pe.wait_ge((exp_done if k not in DIAGONAL or g in MASKED_ON_PE else masked)[k][g], b + 1)
                at = PAD - OUTROW * (qt * 2 + s)
                for g in range(G):
                    mm = pe.matmul(O[32 * g:32 * g + 32, :], values[p][:, kt, g, s, at:at + 32], probs[:, k, g, s, :],
                                   start=first, stop=(k == 2 and s == 1))
                mm.then_inc(pv_done[k][s], 1)

            def turn_outputs(b):
                pe.wait_ge(n_["o_ready"], b + 1)
                reach(pe, n_["X0_ready"], b)
                for r in range(R):
                    mm = pe.transpose(MB[:, r * 128:(r + 1) * 128], o_sb[:, r * 128:(r + 1) * 128], ident[:, :])
                mm.then_inc(n_["o_turned"], 1)

            def turn_heads(b, projected_more):
                pe.wait_ge(n_["heads_done"], b + 1)
                reach(pe, n_["summed_done"], b)
                if projected_more:
                    pe.wait_ge(n_["qkvg_ready"], b + 4)
                for t in range(T):
                    mm = pe.transpose(MA[:, t * 128:(t + 1) * 128], heads[:, t, :], ident[:, :])
                mm.then_inc(n_["heads_turned"], 1)

            def output_projection(b):
                pe.wait_ge(n_["headsT_ready"], b + 1)
                for t in range(T):
                    mm = pe.matmul(MA[:, t * 128:(t + 1) * 128], headsT[:, t * 128:(t + 1) * 128], w_out[:, :],
                                   start=True, stop=True)
                mm.then_inc(n_["projected"], 1)

            def turn_x1(b):
                pe.wait_ge(n_["x1_ready"], b + 1)
                for t in range(T):
                    mm = pe.transpose(MB[:, t * 128:(t + 1) * 128], x1[:, t, :], ident[:, :])
                mm.then_inc(n_["x1_turned"], 1)

            def attend(b, p, half_b, general):
                first, second, last = (isinstance(b, int) and b == n for n in (0, 1, BATCH - 1))
                project_more = not last and not (isinstance(b, int) and b == BATCH - 2)
                scores(b, p, 0, 0, general)
                if project_more:
                    project(b + 2, p, half_b + 1)
                scores(b, p, 0, 1, general)
                if not first and not second:
                    turn_x1(b - 2)
                scores(b, p, 0, 2, general)
                if not first:
                    weigh(b - 1, 1 - p, 2, 0)
                scores(b, p, 0, 3, general)
                if not first:
                    weigh(b - 1, 1 - p, 2, 1)
                scores(b, p, 1, 0, general)
                scores(b, p, 1, 1, general)
                if not first:
                    turn_outputs(b - 1)
                scores(b, p, 1, 2, general)
                weigh(b, p, 0, 0)
                scores(b, p, 1, 3, general)
                weigh(b, p, 0, 1)
                scores(b, p, 2, 0, general)
                if not first:
                    turn_heads(b - 1, project_more)
                if not last:
                    turn_queries(b + 1)
                scores(b, p, 2, 1, general)
                if not first:
                    output_projection(b - 1)
                scores(b, p, 2, 2, general)
                weigh(b, p, 1, 0)
                if not last:
                    turn_keys(b + 1)
                    if general:
                        blocks_for_maximum(b + 1, 1 - p)
                scores(b, p, 2, 3, general)
                weigh(b, p, 1, 1)

            def attention(general):
                project(0, 0, 0)
                project(1, 1, 0)
                turn_queries(0)
                turn_keys(0)
                if general:
                    blocks_for_maximum(0, 0)
                pe.wait_ge(n_["w_out_step_done"], 3)
                batches(pe, lambda b, p, half_b: attend(b, p, half_b, general))
                last = BATCH - 1
                turn_x1(last - 1)
                weigh(last, last % 2, 2, 0)
                weigh(last, last % 2, 2, 1)
                turn_outputs(last)
                turn_heads(last, False)
                output_projection(last)
                turn_x1(last)

            pe.wait_ge(n_["consts_loaded"], 16 * (1 + len(CONSTS)))
            pe.wait_ge(n_["bounded_ready"], 1)
            is_bounded = pe.value_load(bounded[0:1, 0:1], min_val=0, max_val=1)
            with pe.If(is_bounded > 0):
                attention(False)
            with pe.Else():
                attention(True)

            pe.wait_ge(n_["xsum_ready"], BATCH)
            pe.wait_ge(n_["X0_ready"], BATCH)
            pe.wait_ge(n_["ffn_loaded"], 16 * FFN_LOADS)

            def dense1(u, h, first, c):
                if not first:
                    for j in (2 * c, 2 * c + 1):
                        pe.wait_ge(X_done[j], u - 1)
                if u >= 1:
                    pe.wait_ge(gelu1_done[c], u)
                for j in range(2):
                    at = h * 2048 + (2 * c + j) * 512
                    mm = pe.matmul(S[c][:, j, :], cn_w1[:, :], X[:, at:at + 512] if not first else X0[:, at:at + 512],
                                   start=True, stop=True)
                mm.then_inc(h1_done[c], 1)

            def dense2(u, c):
                pe.wait_ge(gelu1_done[c], u + 1)
                if c == 1:
                    pe.wait_ge(gelu2_done[0], u + 1)
                elif u >= 1:
                    pe.wait_ge(gelu2_done[1], u)
                for j in range(2):
                    mm = pe.matmul(MA[64 * j:64 * j + 64, :], cn_w2[:, :], h1[:, (2 * c + j) * 512:(2 * c + j + 1) * 512],
                                   start=True, stop=True)
                mm.then_inc(h2_done[c], 1)

            def dense3(u):
                if u >= 1:
                    pe.wait_ge(n_["tanh_ready"], u)
                for c in range(2):
                    pe.wait_ge(gelu2_done[c], u + 1)
                    mm = pe.matmul(MB[64 * c:64 * c + 64, :], cn_w3[:, :], h2[:, c * 512:(c + 1) * 512],
                                   start=True, stop=True)
                mm.then_inc(n_["h3_done"], 1)

            def dense4(u):
                pe.wait_ge(n_["gelu3_done"], u + 1)
                pe.matmul(MB[0:4, :], cn_w4[:, :], h3[:, :], start=True, stop=True).then_inc(n_["z_done"], 1)

            def spread_coupling(u, h, j):
                pe.wait_ge(n_["tanh_ready"], u + 1)
                if j >= 2:
                    pe.wait_ge((cX_done if u < 4 else cY_done)[j - 2], u + 1)
                elif u >= 1:
                    pe.wait_ge((cX_done if u - 1 < 4 else cY_done)[j + 2], u)
                pe.matmul((O, MC)[j % 2][:, :], spread[:, j, :], coup[h][:, :], start=True, stop=True)\
                  .then_inc(spread_done[j], 1)

            pe.matmul(MB[0:64, 0:BATCH], gc_w1[:, :], xsum[:, :], start=True, stop=True).then_inc(n_["g1_done"], 1)
            pe.wait_ge(n_["hg1_ready"], 1)
            pe.matmul(MB[0:32, 0:BATCH], gc_w2[:, :], hg1[:, :], start=True, stop=True).then_inc(n_["g2_done"], 1)
            pe.wait_ge(n_["hg2_ready"], 1)
            for n in range(4):
                first_batch = 8 * (n // 2) + n % 2
                mm = pe.matmul(MB[0:4, n:n + 1], hg2[:, first_batch:first_batch + 7:2], gc_w3[:, :], start=True, stop=True)
            mm.then_inc(n_["g3_done"], 1)
            pe.wait_ge(n_["tanh_g_ready"], 1)

            def half_cycle(u, h, first, last):
                dense1(u, h, first, 0)
                if u >= 1:
                    dense4(u - 1)
                dense1(u, h, first, 1)
                if u == 1:
                    pe.wait_ge(n_["coup_ready"], 1)
                    pe.wait_ge(n_["spread_ready"], 1)
                if u >= 1:
                    spread_coupling(u - 1, 1 - h, 0)
                    spread_coupling(u - 1, 1 - h, 1)
                dense2(u, 0)
                if u >= 1:
                    spread_coupling(u - 1, 1 - h, 2)
                dense2(u, 1)
                if u >= 1:
                    spread_coupling(u - 1, 1 - h, 3)
                dense3(u)

            def turn_back(f):
                pe.wait_ge(X_done[f % 4], CYCLES * 2 - 1 + f // 4)
                if f >= 4:
                    pe.wait_ge(n_["result_ready"], f - 3)
                bank = S[(f % 4) // 2][:, f % 2, :]
                for t in range(4):
                    at = f * 512 + t * 128
                    mm = pe.transpose(bank[:, t * 128:(t + 1) * 128], X0[:, at:at + 128], ident[:, :])
                mm.then_inc(n_["turned_back"], 1)

            cycles(pe, half_cycle)
            turn_back(0)
            turn_back(1)
            dense4(5)
            turn_back(2)
            turn_back(3)
            spread_coupling(5, 1, 0)
            spread_coupling(5, 1, 1)
            turn_back(4)
            spread_coupling(5, 1, 2)
            turn_back(5)
            spread_coupling(5, 1, 3)
            turn_back(6)
            turn_back(7)

        @block.scalar
        def _(act):
            def copy_projection(b, p):
                act.wait_ge(n_["proj_done"], b + 1)
                reach(act, n_["values_ready"], b - 1)
                act.activation(qkvg[p][:, :, :].rearrange("p t c -> p (t c)"), MA[:, 0:T * PROJ], ACT.Copy)\
                   .then_inc(n_["qkvg_ready"], 1)

            def keep_x1(b):
                at = b * SEQ
                act.wait_ge(n_["x1_turned"], b + 1)
                act.activation(X0[:, bass.ds(at, SEQ)], MB[:, 0:SEQ], ACT.Copy).then_inc(n_["X0_ready"], 1)

            def gate_tanh(b, p):
                act.wait_ge(n_["qkvg_ready"], b + 1)
                act.activation(gate[p][:, :, :], qkvg[p][:, :, QK + KV:PROJ], ACT.Tanh, scale=0.5)\
                   .then_inc(n_["gate_ready"], 1)

            def exponentials(b, k, g):
                act.wait_ge(scores_done[k][g], b + 1)
                if g == 0:
                    reach(act, pv_done[k][1], b)
                act.activation(probs[:, k, g, :, :], S[(k * G + g) % 2][:, :, :], ACT.Exp).then_inc(exp_done[k][g], 1)

            def copy_keys(b, p):
                act.wait_ge(n_["k_turned"], b + 1)
                for g in (2, 3):
                    q = slice(32 * g, 32 * g + 32)
                    last = act.activation(kT[p][q, g, :, :, :].rearrange("p t s n -> p (t s n)"), MC16[q, 0:T * 2 * 128], ACT.Copy)
                last.then_inc(n_["k_ready_act"], 1)

            def copy_heads(b):
                act.wait_ge(n_["heads_turned"], b + 1)
                reach(act, n_["projected"], b)
                act.activation(headsT[:, :], MA[:, 0:T * 128], ACT.Copy).then_inc(n_["headsT_ready"], 1)

            def attend(b, p, half_b):
                first, second, last = (isinstance(b, int) and b == n for n in (0, 1, BATCH - 1))
                project_more = not last and not (isinstance(b, int) and b == BATCH - 2)
                exponentials(b, 0, 0)
                if project_more:
                    copy_projection(b + 2, p)
                    gate_tanh(b + 2, p)
                exponentials(b, 0, 1)
                if not first and not second:
                    keep_x1(b - 2)
                exponentials(b, 0, 2)
                exponentials(b, 0, 3)
                for g in range(G):
                    exponentials(b, 1, g)
                exponentials(b, 2, 0)
                if not first:
                    copy_heads(b - 1)
                exponentials(b, 2, 1)
                exponentials(b, 2, 2)
                if not last:
                    copy_keys(b + 1, 1 - p)
                exponentials(b, 2, 3)

            for b in range(2):
                copy_projection(b, b)
                gate_tanh(b, b)
            copy_keys(0, 0)
            batches(act, attend)
            keep_x1(BATCH - 2)
            copy_heads(BATCH - 1)
            keep_x1(BATCH - 1)

            act.wait_ge(n_["ffn_loaded"], 16 * FFN_LOADS)
            act.mul(cn_b4[:, 1:2], cn_b4[:, 0:1], 0.5)
            act.mul(gc_b3[:, 1:2], gc_b3[:, 0:1], 0.5).then_inc(n_["half_ready"], 1)
            act.wait_ge(n_["half_ready"], 1)
            act.wait_ge(n_["g1_done"], 1)
            act.activation(hg1[:, :], MB[0:64, 0:BATCH], ACT.Gelu, bias=gc_b1[:, :], scale=1.0 / SEQ).then_inc(n_["hg1_ready"], 1)
            act.wait_ge(n_["g2_done"], 1)
            act.activation(hg2[:, :], MB[0:32, 0:BATCH], ACT.Gelu, bias=gc_b2[:, :]).then_inc(n_["hg2_ready"], 1)
            act.wait_ge(n_["g3_done"], 1)
            act.activation(tanh_g[:, :], MB[0:4, 0:4], ACT.Tanh, bias=gc_b3[:, 1:2], scale=0.5).then_inc(n_["tanh_g_ready"], 1)

            def gelu1(u, c):
                act.wait_ge(h1_done[c], u + 1)
                if u >= 1:
                    act.wait_ge(h2_done[c], u)
                act.activation(h1[:, c * 1024:(c + 1) * 1024], S[c][:, :, :].rearrange("p s n -> p (s n)"),
                               ACT.Gelu, bias=cn_b1[:, :]).then_inc(gelu1_done[c], 1)

            def coupling_tanh(u, h):
                act.wait_ge(n_["z_done"], u + 1)
                if u >= 2:
                    act.wait_ge(spread_done[3], u - 1)
                else:
                    act.wait_ge(n_["coup_ready"], 1)
                act.activation(coup[h][0:4, :], MB[0:4, :], ACT.Tanh, bias=cn_b4[:, 1:2], scale=0.5).then_inc(n_["tanh_ready"], 1)

            def half_cycle(u, h, first, last):
                gelu1(u, 0)
                if u >= 1:
                    coupling_tanh(u - 1, 1 - h)
                gelu1(u, 1)
                for c in range(2):
                    act.wait_ge(h2_done[c], u + 1)
                    if u >= 1:
                        act.wait_ge(n_["h3_done"], u)
                    act.activation(h2[:, c * 512:(c + 1) * 512], MA[:, :], ACT.Gelu, bias=cn_b2[:, :]).then_inc(gelu2_done[c], 1)
                act.wait_ge(n_["h3_done"], u + 1)
                if u >= 1:
                    act.wait_ge(n_["z_done"], u)
                act.activation(h3[:, :], MB[:, :], ACT.Gelu, bias=cn_b3[:, :]).then_inc(n_["gelu3_done"], 1)

            def store_normalized(f):
                act.wait_ge(n_["f_norm_step_done"], 4 * (f + 1))
                if f >= 4:
                    act.wait_ge(stored[f % 4], 16)
                bank = S[(f % 4) // 2][:, f % 2, :]
                for t in range(4):
                    a = act.activation(result[:, f % 4, t, :], bank[:, t * 128:(t + 1) * 128], ACT.Identity,
                                       bias=f_shift[:, f % 2, t:t + 1], scale=f_rstd[:, f % 2, t:t + 1])
                a.then_inc(n_["result_ready"], 1)

            cycles(act, half_cycle)
            coupling_tanh(5, 1)
            for f in range(8):
                store_normalized(f)

        @block.vector
        def _(dve):
            dve.memset(ln_eps[:, :], LN_EPS)
            dve.memset(one_half[:, :], 1.5)
            dve.memset(minus_half[:, :], -0.5).then_inc(n_["half_ready2"], 1)
            dve.wait_ge(n_["consts_loaded"], 16 * (1 + len(CONSTS)))
            dve.tensor_copy(ident16[:, :], ident[:, :])
            dve.tensor_copy(future16[:, :, :], future_in[:, :].rearrange("p (o n) -> p o n", o=1).broadcast_to([128, G, 128]))
            dve.tensor_tensor(gain_sq[:, :], gain[:, :], gain[:, :], ALU.mult).then_inc(n_["gain_step_done"], 1)
            dve.wait_ge(n_["gain_step_done"], 1)
            dve.tensor_reduce(gain_top[:, :], gain_sq[:, :], AX.X, ALU.max).then_inc(n_["gain_step_done"], 1)
            dve.wait_ge(n_["gain_step_done"], 2)
            dve.tensor_scalar(bounded[:, :], gain_top[:, :], SAFE_GAIN ** 2, None, ALU.is_le).then_inc(n_["bounded_ready"], 1)
            SCALE, ROOT = HALF ** -0.5 * HD ** 0.5, HD ** 0.5
            for t in range(T):
                for s in range(2):
                    for table, c, sign in ((rope_cos, 0, 1.0), (rope_sin, 1, 1.0 - 2.0 * s)):
                        row = trig[:, c, t, :].rearrange("p (o d) -> p o d", o=1)
                        dve.scalar_tensor_tensor(
                            out=table[:, t, 0:HEADS, s, :], in0=row.broadcast_to([128, HEADS, HALF]), scalar=SCALE * sign,
                            in1=gain[:, :].rearrange("p (h o) -> p h o", o=1).broadcast_to([128, HEADS, HALF]),
                            op0=ALU.mult, op1=ALU.mult)
                        last = dve.tensor_scalar(table[:, t, HEADS:, s, :], row.broadcast_to([128, G, HALF]), ROOT * sign, None, ALU.mult)
            last.then_inc(n_["tables_ready"], 1)

            def rotate(b, p):
                x_heads = qkvg[p][:, :, 0:QK].rearrange("p t (n d) -> p t n d", d=HALF)
                dve.wait_ge(n_["qkvg_ready"], b + 1)
                dve.tensor_tensor(square[:, :, :], qkvg[p][:, :, 0:QK], qkvg[p][:, :, 0:QK], ALU.mult).then_inc(n_["square_done"], 1)
                flat = lambda a: a.rearrange("p t h s d -> p t (h s d)")
                dve.tensor_tensor(flat(turned[:, :, :, :, :]), qkvg[p][:, :, 0:QK], flat(rope_cos[:, :, :, :, :]), ALU.mult)
                dve.wait_ge(n_["square_done"], b + 1)
                dve.tensor_reduce(sum_sq[:, :], square[:, :, :].rearrange("p t (h c) -> p (t h) c", c=HD), AX.X, ALU.add)\
                   .then_inc(n_["sum_sq_done"], 1)
                for t in range(T):
                    last = dve.tensor_tensor(turned2[:, t, :, :, :], qkvg[p][:, t, 0:QK].rearrange("p (h s d) -> p h s d", s=2, d=HALF)[:, :, ::-1, :],
                                             rope_sin[:, t, :, :, :], ALU.mult)
                last.then_inc(n_["turned_done"], 1)
                dve.wait_ge(n_["sum_sq_done"], b + 1)
                dve.tensor_scalar(sum_eps[:, :], sum_sq[:, :], HD * RMS_EPS, None, ALU.add).then_inc(n_["sum_eps_done"], 1)
                dve.wait_ge(n_["turned_done"], b + 1)
                dve.tensor_tensor(rotated[:, :, :], flat(turned[:, :, :, :, :]), flat(turned2[:, :, :, :, :]), ALU.add)\
                   .then_inc(n_["rotated_done"], 1)
                dve.wait_ge(n_["sum_eps_done"], b + 1)
                dve.tensor_scalar(estimate[0][:, :].bitcast(I32), sum_eps[:, :].bitcast(I32), -0.5, ROOT_BITS, ALU.mult, ALU.add)\
                   .then_inc(n_["estimate_ready"], 1)

            def normalize_queries(b):
                dve.wait_ge(n_["rotated_done"], b + 1)
                dve.wait_ge(n_["rstd_ready"], b + 1)
                for t in range(T):
                    for lo, hi, at, n in ((0, HEADS, t * R * 2 * G, R * 2), (HEADS, HEADS + G, NQ + t * 2 * G, 2)):
                        last = dve.tensor_tensor(
                            roped[:, at:at + n * G, :].rearrange("p (n g) d -> p g n d", g=G),
                            rotated[:, t, lo * HD:hi * HD].rearrange("p (g n d) -> p g n d", g=G, d=HALF),
                            rstd[:, t, lo:hi, :].rearrange("p h s -> p (h s)").rearrange("p (g n o) -> p g n o", g=G, o=1)
                            .broadcast_to([128, G, n, HALF]), ALU.mult)
                last.then_inc(n_["roped_done"], 1)

            def split(b):
                def slots(lo, n, a, b_, src):
                    dst = parts[:, a:b_, lo:lo + n, :]
                    src = src[:, a:b_, :].rearrange("p u (o d) -> p u o d", o=1)
                    return dst, (src.broadcast_to([128, b_ - a, n, HALF]) if n > 1 else src)
                N = NQ + NK
                dve.wait_ge(n_["roped_done"], b + 1)
                reach(dve, n_["k_turned"], b)
                dve.tensor_copy(*slots(0, 1, 0, N, roped)).then_inc(n_["part0_done"], 1)
                dve.tensor_copy(*slots(1, 2, 0, NQ, roped))
                dve.tensor_copy(*slots(4, 2, NQ, N, roped))
                dve.wait_ge(n_["part0_done"], b + 1)
                dve.tensor_tensor(rest1[:, :, :], roped[:, :, :], parts[:, :, 0, :], ALU.subtract).then_inc(n_["rest1_done"], 1)
                dve.wait_ge(n_["rest1_done"], b + 1)
                dve.tensor_copy(*slots(3, 1, 0, N, rest1)).then_inc(n_["part1_done"], 1)
                dve.tensor_copy(*slots(4, 1, 0, NQ, rest1))
                dve.tensor_copy(*slots(1, 1, NQ, N, rest1))
                dve.wait_ge(n_["part1_done"], b + 1)
                dve.tensor_tensor(parts[:, 0:NQ, 5, :], rest1[:, 0:NQ, :], parts[:, 0:NQ, 3, :], ALU.subtract)
                dve.tensor_tensor(parts[:, NQ:N, 2, :], rest1[:, NQ:N, :], parts[:, NQ:N, 3, :], ALU.subtract)\
                   .then_inc(n_["parts_ready"], 1)

            def gate_values(b, p):
                dve.wait_ge(n_["gate_ready"], b + 1)
                dve.scalar_tensor_tensor(out=values[p][:, :, :, :, PAD:PAD + HALF].rearrange("p t g s d -> p t (g s) d"),
                                         in0=gate[p][:, :, :].rearrange("p t (n d) -> p t n d", d=HALF), scalar=1.0,
                                         in1=qkvg[p][:, :, QK:QK + KV].rearrange("p t (n d) -> p t n d", d=HALF),
                                         op0=ALU.add, op1=ALU.mult)\
                   .then_inc(n_["values_ready"], 1)

            def copy_queries(b, p, suffix=""):
                for t, bank in enumerate((MB16, MC16)):
                    dve.wait_ge(n_[f"q{t}_turned{suffix}"], b + 1)
                    dve.tensor_copy(qT[p][:, t, :, :, :].rearrange("p r s n -> p (r s n)"), bank[:, :])\
                       .then_inc(n_[f"q{t}_ready{suffix}"], 1)

            def copy_keys(b, p):
                dve.wait_ge(n_["k_turned"], b + 1)
                for g in (0, 1):
                    q = slice(32 * g, 32 * g + 32)
                    last = dve.tensor_copy(kT[p][q, g, :, :, :].rearrange("p t s n -> p (t s n)"), MC16[q, 0:T * 2 * 128])
                last.then_inc(n_["k_ready"], 1)

            def subtract_maximum(b, p):
                for k in range(len(KINDS)):
                    for n in range(R * 2):
                        dve.wait_ge(n_["block_scored"], b * BLOCKS + k * R * 2 + n + 1)
                        dve.tensor_reduce(block_max[:, k, n * G:(n + 1) * G], (MB, MC)[n % 2][:, :].rearrange("p (g n) -> p g n", g=G),
                                          AX.X, ALU.max).then_inc(n_["block_max_done"], 1)
                dve.wait_ge(n_["block_max_done"], (b + 1) * BLOCKS)
                dve.tensor_scalar(row_max[:, 0:NQ // 2], block_max[:, 0, :], 1.0, None, ALU.mult)
                dve.tensor_tensor(row_max[:, NQ // 2:], block_max[:, 1, :], block_max[:, 2, :], ALU.max).then_inc(n_["max_step_done"], 1)
                dve.wait_ge(n_["max_step_done"], b * 6 + 1)
                dve.tensor_scalar(minus_max[:, :], row_max[:, :], -1.0, None, ALU.mult).then_inc(n_["max_step_done"], 1)
                slot = lambda d: parts[:, 0:NQ, 6, d]
                dve.wait_ge(n_["max_step_done"], b * 6 + 2)
                dve.tensor_copy(slot(0), minus_max[:, :]).then_inc(n_["max_step_done"], 1)
                dve.wait_ge(n_["max_step_done"], b * 6 + 3)
                dve.tensor_tensor(row_max[:, :], minus_max[:, :], slot(0), ALU.subtract).then_inc(n_["max_step_done"], 1)
                dve.wait_ge(n_["max_step_done"], b * 6 + 4)
                dve.tensor_copy(slot(1), row_max[:, :]).then_inc(n_["max_step_done"], 1)
                dve.wait_ge(n_["max_step_done"], b * 6 + 5)
                dve.tensor_tensor(minus_max[:, :], row_max[:, :], slot(1), ALU.subtract).then_inc(n_["max_step_done"], 1)
                dve.wait_ge(n_["max_step_done"], b * 6 + 6)
                dve.tensor_copy(slot(2), minus_max[:, :]).then_inc(n_["max_parts_ready"], 1)
                copy_queries(b, p, "_max")
                dve.memset(parts[:, 0:NQ, 6, 0:3], 0.0).then_inc(n_["slot_cleared"], 1)

            def copy_outputs(b):
                dve.wait_ge(pv_done[2][1], b + 1)
                dve.tensor_copy(o_sb[:, :], O[:, :]).then_inc(n_["o_ready"], 1)

            def normalize_heads(b):
                turned_o = MB[:, :].rearrange("p (n c) -> p n c", c=32)[:, :, 0:4 * OUTROW]\
                    .rearrange("p n (w c) -> p n w c", c=OUTROW)
                dve.wait_ge(n_["o_turned"], b + 1)
                dve.reciprocal(rden[:, :, :], turned_o[:, :, :, HALF]).then_inc(n_["rden_done"], 1)
                dve.wait_ge(n_["rden_done"], b + 1)
                for t in range(T):
                    last = dve.tensor_tensor(
                        heads[:, t, :].rearrange("p (n s d) -> p n s d", s=2, d=HALF),
                        turned_o[:, :, 2 * t:2 * t + 2, 0:HALF],
                        rden[:, :, 2 * t:2 * t + 2].rearrange("p n (s o) -> p n s o", o=1).broadcast_to([128, R * G, 2, HALF]),
                        ALU.mult)
                last.then_inc(n_["heads_done"], 1)

            def add_residual(b, p, half_b):
                dve.wait_ge(n_["projected"], b + 1)
                dve.wait_ge(res_loaded[p], (half_b + 1) * 16)
                dve.tensor_tensor(summed[:, :, :].rearrange("p t d -> p (t d)"), MA[:, 0:T * 128],
                                  x_res[p][:, :, :].rearrange("p t d -> p (t d)"), ALU.add).then_inc(n_["summed_done"], 1)
                dve.wait_ge(n_["summed_done"], b + 1)
                for t in range(T):
                    last = dve.bn_stats(stats[:, t, :], summed[:, t, :])
                last.then_inc(n_["stats_done"], 1)
                reach_alone(dve, n_["stats_done"], b + 1, n_["zeros_ready"])
                for t in range(T):
                    last = dve.bn_aggr(moments[:, t, :], stats[:, t, :])
                last.then_inc(n_["moments_done"], 1)

            def normalize(b):
                dve.wait_ge(n_["ln_rstd_ready"], b + 1)
                reach(dve, n_["x1_turned"], b)
                for t in range(T):
                    last = dve.tensor_scalar(x1[:, t, :], summed[:, t, :], moments[:, t, 0:1], ln_rstd[:, t:t + 1],
                                             ALU.subtract, ALU.mult)
                last.then_inc(n_["x1_ready"], 1)

            def sum_x1(b):
                at = b * SEQ
                reach_alone(dve, n_["X0_ready"], b + 1, n_["zeros_ready"])
                dve.tensor_reduce(xsum[:, bass.ds(b, 1)], X0[:, bass.ds(at, SEQ)], AX.X, ALU.add).then_inc(n_["xsum_ready"], 1)

            def attend(b, p, half_b, general):
                first, second, last = (isinstance(b, int) and b == n for n in (0, 1, BATCH - 1))
                project_more = not last and not (isinstance(b, int) and b == BATCH - 2)
                if not last:
                    normalize_queries(b + 1)
                    split(b + 1)
                if not first:
                    copy_outputs(b - 1)
                if not last:
                    gate_values(b + 1, 1 - p)
                if project_more:
                    rotate(b + 2, p)
                if not first:
                    normalize_heads(b - 1)
                if not last:
                    copy_queries(b + 1, 1 - p)
                if not first:
                    add_residual(b - 1, 1 - p, half_b - (1 - p))
                if not last:
                    copy_keys(b + 1, 1 - p)
                    if general:
                        subtract_maximum(b + 1, 1 - p)
                if not first:
                    normalize(b - 1)
                if not first and not second:
                    sum_x1(b - 2)

            dve.tensor_scalar(mix[:, 0:1], lam[:, :], sel_s[:, 1:2], sel_s[:, 0:1], ALU.mult, ALU.add)
            dve.tensor_scalar(mix[:, 1:2], lam[:, :], sel_s[:, 2:3], sel_s[:, 0:1], ALU.mult, ALU.add).then_inc(n_["w_out_step_done"], 1)
            dve.wait_ge(n_["w_out_step_done"], 1)
            dve.tensor_scalar(w_out[:, :], w_o1[:, :], mix[:, 0:1], None, ALU.mult).then_inc(n_["w_out_step_done"], 1)
            dve.wait_ge(n_["w_out_step_done"], 2)
            dve.scalar_tensor_tensor(out=w_out[:, :], in0=w_o0[:, :], scalar=mix[:, 1:2], in1=w_out[:, :],
                                     op0=ALU.mult, op1=ALU.add).then_inc(n_["w_out_step_done"], 1)
            dve.wait_ge(n_["tables_ready"], 1)
            dve.wait_ge(n_["zeros_ready"], 1)

            def attention(general):
                rotate(0, 0)
                gate_values(0, 0)
                normalize_queries(0)
                split(0)
                copy_queries(0, 0)
                copy_keys(0, 0)
                if general:
                    subtract_maximum(0, 0)
                rotate(1, 1)
                batches(dve, lambda b, p, half_b: attend(b, p, half_b, general))
                last_b = BATCH - 1
                sum_x1(last_b - 1)
                copy_outputs(last_b)
                normalize_heads(last_b)
                add_residual(last_b, 1, BATCH // 2 - 1)
                normalize(last_b)
                sum_x1(last_b)

            is_bounded = dve.value_load(bounded[0:1, 0:1], min_val=0, max_val=1)
            with dve.If(is_bounded > 0):
                attention(False)
            with dve.Else():
                attention(True)

            dve.wait_ge(n_["ffn_loaded"], 16 * FFN_LOADS)
            dve.tensor_scalar(arange7[:, :], arange_in[0:4, :], 0.7, None, ALU.mult)
            dve.tensor_scalar(spread[:, :, :], pick[:, :, :], 1.0, None, ALU.mult).then_inc(n_["pick_done"], 1)
            dve.wait_ge(n_["pick_done"], 1)
            dve.tensor_scalar(spread[0:4, :, :], pick[0:4, :, :], arange_in[0:4, :], 0.3, ALU.mult, ALU.mult)\
               .then_inc(n_["spread_ready"], 1)
            dve.wait_ge(n_["X0_ready"], BATCH)
            for q, (src, sign) in enumerate(((2, 1.0), (3, -1.0), (0, -1.0), (1, 1.0))):
                last = dve.tensor_scalar(Y[32 * q:32 * q + 32, :], X0[32 * src:32 * src + 32, :], sign, None, ALU.mult)
            last.then_inc(n_["XY_ready"], 1)
            dve.wait_ge(n_["tanh_g_ready"], 1)
            dve.wait_ge(n_["zeros_ready"], 3)
            dve.wait_ge(n_["spread_ready"], 1)
            for h in range(2):
                last = dve.tensor_scalar(coup[h][32:36, :].rearrange("p (n c) -> p n c", n=2),
                                         tanh_g[:, 2 * h:2 * h + 2].rearrange("p (n o) -> p n o", o=1).broadcast_to([4, 2, SEQ]),
                                         arange7[:, :], 0.1, ALU.mult, ALU.add)
            last.then_inc(n_["coup_ready"], 1)
            dve.wait_ge(n_["XY_ready"], 1)

            def rotate_pair(u, h, first, last, j):
                at = slice(h * 2048 + j * 512, h * 2048 + (j + 1) * 512)
                c = (O, MC)[j % 2]
                old = X0 if first else X
                dve.wait_ge(spread_done[j], u + 1)
                dve.tensor_tensor(cY[:, j % 2, :], c[:, :], Y[:, at], ALU.mult).then_inc(cY_done[j], 1)
                if not last:
                    if j >= 2:
                        dve.wait_ge(Y_done[j - 2], u + 1)
                    elif u >= 1:
                        dve.wait_ge(Y_done[j + 2], u)
                    dve.tensor_tensor(cX[:, j % 2, :], c[:, :], old[:, at], ALU.mult).then_inc(cX_done[j], 1)
                    dve.wait_ge(cY_done[j], u + 1)
                    dve.tensor_tensor(X[:, at], old[:, at], cY[:, j % 2, :], ALU.add).then_inc(X_done[j], 1)
                else:
                    dve.wait_ge(cY_done[j], u + 1)
                    dve.wait_ge(n_["sum_ready"], (u - 4) * 4 + j + 1)
                    dve.tensor_tensor(X0[:, at], X0[:, at], cY[:, j % 2, :], ALU.add).then_inc(X_done[j], 1)

            def half_cycle(u, h, first, last):
                for j in range(4):
                    rotate_pair(u, h, first, last, j)
                    if u == 5 and j >= 2:
                        stats_of(j + 2)
                if u == 4:
                    for f in range(4):
                        stats_of(f)

            def stats_of(f):
                dve.wait_ge(n_["turned_back"], f + 1)
                if f >= 2:
                    dve.wait_ge(n_["result_ready"], f - 1)
                bank = S[(f % 4) // 2][:, f % 2, :]
                for t in range(4):
                    last = dve.bn_stats(f_stats[:, f % 2, t, :], bank[:, t * 128:(t + 1) * 128])
                last.then_inc(n_["f_stats_done"], 1)
                dve.wait_ge(n_["f_stats_done"], f + 1)
                for t in range(4):
                    last = dve.bn_aggr(f_mom[:, f % 2, t, :], f_stats[:, f % 2, t, :])
                last.then_inc(n_["f_moments_done"], 1)

            cycles(dve, half_cycle)
            stats_of(6)
            stats_of(7)

        @block.gpsimd
        def _(pool):
            for p in range(2):
                pool.memset(kT[p][:, :, :, :, :], 0.0)
                pool.memset(values[p][:, :, :, :, :], 0.0)
            pool.memset(parts[:, :, :, :], 0.0).then_inc(n_["zeros_done"], 1)
            pool.wait_ge(n_["zeros_done"], 1)
            for p in range(2):
                pool.memset(values[p][:, :, :, :, PAD + HALF:PAD + OUTROW], 2.0)
            pool.memset(parts[:, NQ:, 6, 0:3], 1.0).then_inc(n_["zeros_ready"], 1)
            pool.memset(cn_w3[:, :], 0.0)
            pool.memset(cn_w4[:, :], 0.0).then_inc(n_["zeros_ready"], 1)
            for h in range(2):
                last = pool.memset(coup[h][:, :], 0.0)
            last.then_inc(n_["zeros_ready"], 1)

            def root(count, mean, eps, shifted, sem_in, sem_mid, out_, sem_out):
                n = shifted.shape[-1]
                pool.wait_ge(sem_in, count)
                pool.tensor_tensor(shifted, mean, eps[:, 0:n], ALU.add).then_inc(sem_mid, 1)
                pool.wait_ge(sem_mid, count)
                pool.tensor_tensor(out_, shifted, minus_half[:, 0:n], ALU.pow).then_inc(sem_out, 1)

            def refine(count):
                steps = 4 * NEWTON
                before = steps * (count - 1)
                done = n_["root_step_done"]
                pool.wait_ge(n_["estimate_ready"], count)
                pool.tensor_tensor(minus_half_sum[:, :], sum_eps[:, :], minus_half[:, :], ALU.mult).then_inc(done, 1)
                for n in range(NEWTON):
                    if n > 0:
                        pool.wait_ge(done, before + 4 * n + 1)
                    y = estimate[n][:, :]
                    pool.tensor_tensor(root_sq[:, :], y, y, ALU.mult).then_inc(done, 1)
                    pool.wait_ge(done, before + 4 * n + 2)
                    pool.tensor_tensor(root_step[:, :], root_sq[:, :], minus_half_sum[:, :], ALU.mult).then_inc(done, 1)
                    pool.wait_ge(done, before + 4 * n + 3)
                    pool.tensor_tensor(root_sq[:, :], root_step[:, :], one_half[:, :], ALU.add).then_inc(done, 1)
                    pool.wait_ge(done, before + 4 * n + 4)
                    if n < NEWTON - 1:
                        pool.tensor_tensor(estimate[n + 1][:, :], y, root_sq[:, :], ALU.mult).then_inc(done, 1)
                    else:
                        both = lambda a: a.rearrange("p (h o) -> p h o", o=1).broadcast_to([128, T * (HEADS + G), 2])
                        pool.tensor_tensor(rstd[:, :, :, :].rearrange("p t h s -> p (t h) s"), both(y), both(root_sq[:, :]),
                                           ALU.mult).then_inc(n_["rstd_ready"], 1)

            def mask(count, k, g):
                if g in MASKED_ON_PE:
                    return
                reach_alone(pool, exp_done[k][g], count, n_["zeros_ready"])
                p = probs[:, k, g, :, :].rearrange("p s (r q) -> p (s r) q", q=128)
                pool.affine_select(out=p, in_=p, compare_op=ALU.is_ge, fill=0.0, base=0,
                                   pattern=[[0, 2 * R], [1, 128]], channel_multiplier=-1).then_inc(masked[k][g], 1)

            def attend(now, first, refine_more):
                for g in range(G):
                    mask(now, 0, g)
                if refine_more:
                    refine(now + 2)
                mask(now, 2, 0)
                if not first:
                    root(now - 1, moments[:, :, 1], ln_eps, var_eps[:, :], n_["moments_done"], n_["var_eps_done"],
                         ln_rstd[:, :], n_["ln_rstd_ready"])
                for g in range(1, G):
                    mask(now, 2, g)

            pool.wait_ge(n_["half_ready2"], 1)
            refine(1)
            refine(2)
            attend(1, True, True)
            attend(2, False, True)
            with pool.Fori(3, BATCH - 1) as now:
                attend(now, False, True)
            attend(BATCH - 1, False, False)
            attend(BATCH, False, False)
            last_b = BATCH - 1
            root(last_b + 1, moments[:, :, 1], ln_eps, var_eps[:, :], n_["moments_done"], n_["var_eps_done"],
                 ln_rstd[:, :], n_["ln_rstd_ready"])

            pool.wait_ge(n_["XY_ready"], 1)

            def half_cycle(u, h, first, last):
                for j in range(4):
                    at = slice(h * 2048 + j * 512, h * 2048 + (j + 1) * 512)
                    if not last:
                        pool.wait_ge(cX_done[j], u + 1)
                        pool.tensor_tensor(Y[:, at], Y[:, at], cX[:, j % 2, :], ALU.subtract).then_inc(Y_done[j], 1)
                    else:
                        pool.wait_ge(X_done[j], u - 1)
                        pool.tensor_tensor(X0[:, at], X0[:, at], X[:, at], ALU.add).then_inc(n_["sum_ready"], 1)

            cycles(pool, half_cycle)
            for f in range(8):
                pool.wait_ge(n_["f_moments_done"], f + 1)
                pool.tensor_tensor(f_var[:, f % 2, :], f_mom[:, f % 2, :, 1], ln_eps[:, :], ALU.add).then_inc(n_["f_norm_step_done"], 1)
                pool.wait_ge(n_["f_norm_step_done"], 4 * f + 1)
                pool.tensor_tensor(f_rstd[:, f % 2, :], f_var[:, f % 2, :], minus_half[:, 0:4], ALU.pow).then_inc(n_["f_norm_step_done"], 1)
                pool.wait_ge(n_["f_norm_step_done"], 4 * f + 2)
                pool.tensor_tensor(f_var[:, f % 2, :], f_mom[:, f % 2, :, 0], f_rstd[:, f % 2, :], ALU.mult).then_inc(n_["f_norm_step_done"], 1)
                pool.wait_ge(n_["f_norm_step_done"], 4 * f + 3)
                pool.tensor_scalar(f_shift[:, f % 2, :], f_var[:, f % 2, :], -1.0, None, ALU.mult).then_inc(n_["f_norm_step_done"], 1)


FFN_LOADS = 20


def constants():
    import math
    import numpy as np
    pos = np.arange(SEQ, dtype=np.float32)
    angles = (np.arange(0, HD, 2, dtype=np.float32) / np.float32(HD) * np.float32(math.pi)).astype(np.float32)
    ang = pos[:, None] * angles[None, :]
    radius = np.float32(1.0) / (np.float32(1.0) + pos[:, None] * np.float32(0.01))
    table = np.stack([radius * np.cos(ang), radius * np.sin(ang)]).astype(np.float32)
    trig = table.reshape(2, T, 128, HALF).transpose(2, 0, 1, 3)
    s = (np.arange(128) // HALF) % 2
    sel_s = np.stack([s == 0, s == 1, -(s == 1).astype(np.float32)], 1).astype(np.float32)
    pick = np.zeros((36, 4, 128), np.float32)
    for c in range(4):
        pick[c, c] = 1.0
        pick[32 + c, c] = 1.0
    return dict(ident=np.eye(128, dtype=np.float32), trig=np.ascontiguousarray(trig), sel_s=sel_s, pick=pick,
                future=np.triu(np.full((128, 128), FUTURE, np.float32), 1))


def kernel(**inputs):
    import numpy as np
    import concourse.bacc as bacc
    from concourse.bass_utils import run_bass_kernel_spmd
    I = {k.replace("L0_attn_", "").replace("L0_ffn_", ""): np.asarray(v) for k, v in inputs.items()}
    x = I["x"]
    woT = np.transpose(I["Wo"]).reshape(G, R, 2, HALF, DIM).transpose(1, 0, 2, 3, 4)

    def by_head(a):
        return np.broadcast_to(a.reshape(G, R).T[:, :, None, None], (R, G, 2, HALF)).reshape(128, 1)

    def both(half):
        return np.broadcast_to(woT[:, :, half:half + 1], (R, G, 2, HALF, DIM)).reshape(128, DIM)

    col = lambda a, n: np.tile(a.reshape(-1, 1), (n, 1))
    arrays = dict(
        x=x, xT=np.transpose(x, (0, 2, 1)),
        w_proj=np.concatenate([np.transpose(I[n]) for n in ("Wq", "Wk", "Wv", "Wg")], 1),
        w_o0=both(0), w_o1=both(1), lam=by_head(I["lambda_param"]),
        gain=np.broadcast_to(I["q_gain"][None, :], (128, HEADS)),
        cn_w1=I["cn_w1"], cn_w2=I["cn_w2"], cn_w3=I["cn_w3"], cn_w4=I["cn_w4"],
        cn_b1=col(I["cn_b1"], 1), cn_b2=col(I["cn_b2"], 2), cn_b3=col(I["cn_b3"], 4), cn_b4=col(I["cn_b4"], 4),
        gc_w1=I["gc_w1"], gc_w2=I["gc_w2"], gc_w3=I["gc_w3"],
        gc_b1=col(I["gc_b1"], 1), gc_b2=col(I["gc_b2"], 1), gc_b3=col(I["gc_b3"], 4),
        arange_in=col(I["adaptive_range"], 128), **constants())
    arrays = {k: np.ascontiguousarray(v) for k, v in arrays.items()}
    nc = bacc.Bacc("TRN2", target_bir_lowering=False, num_devices=1)
    aps = {k: nc.dram_tensor(f"in_{k}", v.shape, mybir.dt.from_np(v.dtype), kind="ExternalInput").ap()
           for k, v in arrays.items()}
    out = nc.dram_tensor("out", (TOK, DIM), F32, kind="ExternalOutput").ap()
    block_kernel(nc, aps, out)
    r = run_bass_kernel_spmd(nc, [{f"in_{k}": v for k, v in arrays.items()}], core_ids=[0])
    return r.results[0]["out"].reshape(BATCH, SEQ, DIM)
```

```python
import concourse.bass as bass
from concourse import mybir
from contextlib import ExitStack

F32 = mybir.dt.float32
BF16 = mybir.dt.bfloat16
I32 = mybir.dt.int32
ALU = mybir.AluOpType
ACT = mybir.ActivationFunctionType
AX = mybir.AxisListType

BATCH, SEQ, DIM = 16, 256, 128
HEADS, G, HD = 16, 4, 8
R = HEADS // G
HALF = HD // 2
T = SEQ // 128
KV = G * HD
QK = DIM + KV
PROJ = DIM + 3 * KV
SLOTS = 8
OUTROW = HALF + 1
PAD = 3 * OUTROW
VWIDTH = PAD + 32
SAFE_GAIN = 8.0
FUTURE = -1e30
CYCLES = 3
TOK = BATCH * SEQ
NEWTON = 2
ROOT_BITS = float(0x5F3759DF)
LN_EPS = 1e-5
RMS_EPS = 1.1920928955078125e-07

KINDS = [(0, 0), (0, 1), (1, 1)]
DIAGONAL = (0, 2)
KEYS_ON_DVE = 3
BLOCKS = len(KINDS) * R * 2


def reach(eng, sem, n):
    if not isinstance(n, int) or n > 0:
        eng.wait_ge(sem, n)


def reach_alone(eng, sem, n, zeros_ready):
    eng.wait_ge(zeros_ready, 1)
    reach(eng, sem, n)


def block_kernel(nc, A, out):
    ctx = ExitStack()
    with ctx:
        def sb(name, shape, dt=F32):
            return ctx.enter_context(nc.sbuf_tensor(name, shape, dt))

        def ps(name, shape, dt=F32):
            return ctx.enter_context(nc.psum_tensor(name, shape, dt))

        def sem(name):
            return ctx.enter_context(nc.semaphore(name))

        ident = sb("ident", [128, 128])
        ident16 = sb("ident16", [128, 128], BF16)
        future_in = sb("future_in", [128, 128])
        future16 = sb("future16", [128, G, 128], BF16)
        gain_sq = sb("gain_sq", [128, HEADS])
        gain_top = sb("gain_top", [128, 1])
        bounded = sb("bounded", [128, 1], I32)
        w_proj = sb("w_proj", [128, PROJ])
        w_o0 = sb("w_o0", [128, DIM])
        w_o1 = sb("w_o1", [128, DIM])
        w_out = sb("w_out", [128, DIM])
        lam = sb("lam", [128, 1])
        sel_s = sb("sel_s", [128, 3])
        mix = sb("mix", [128, 2])
        gain = sb("gain", [128, HEADS])
        trig = sb("trig", [128, 2, T, HALF])
        rope_cos = sb("rope_cos", [128, T, HEADS + G, 2, HALF])
        rope_sin = sb("rope_sin", [128, T, HEADS + G, 2, HALF])
        minus_half = sb("minus_half", [128, T * (HEADS + G)])
        ln_eps = sb("ln_eps", [128, 4])

        xT_in = [sb(f"xT_in{p}", [128, SEQ]) for p in range(2)]
        x_res = [sb(f"x_res{p}", [128, T, DIM]) for p in range(2)]
        qkvg = [sb(f"qkvg{p}", [128, T, PROJ]) for p in range(2)]
        square = sb("square", [128, T, QK])
        sum_sq = sb("sum_sq", [128, T * (HEADS + G)])
        sum_eps = sb("sum_eps", [128, T * (HEADS + G)])
        estimate = [sb(f"estimate{n}", [128, T * (HEADS + G)]) for n in range(NEWTON)]
        bits = sb("bits", [128, T * (HEADS + G)])
        bits_sq = sb("bits_sq", [128, T * (HEADS + G)])
        bits_step = sb("bits_step", [128, T * (HEADS + G)])
        root_sq = sb("root_sq", [128, T * (HEADS + G)])
        root_step = sb("root_step", [128, T * (HEADS + G)])
        minus_half_sum = sb("minus_half_sum", [128, T * (HEADS + G)])
        rstd = sb("rstd", [128, T, HEADS + G, 2])
        rotated = sb("rotated", [128, T, QK])
        one_half = sb("one_half", [128, T * (HEADS + G)])
        turned = sb("turned", [128, T, HEADS + G, 2, HALF])
        turned2 = sb("turned2", [128, T, HEADS + G, 2, HALF])
        NQ = T * R * 2 * G
        NK = T * 2 * G
        roped = sb("roped", [128, NQ + NK, HALF])
        rest1 = sb("rest1", [128, NQ + NK, HALF])
        parts = sb("parts", [128, NQ + NK, SLOTS, HALF], BF16)
        block_max = sb("block_max", [128, len(KINDS), R * 2 * G])
        row_max = sb("row_max", [128, NQ])
        minus_max = sb("minus_max", [128, NQ])
        gate = [sb(f"gate{p}", [128, T, KV]) for p in range(2)]
        qT = [sb(f"qT{p}", [128, T, R, 2, 128], BF16) for p in range(2)]
        kT = [sb(f"kT{p}", [128, G, T, 2, 128], BF16) for p in range(2)]
        values = [sb(f"values{p}", [128, T, G, 2, VWIDTH]) for p in range(2)]

        probs = sb("probs", [128, len(KINDS), G, 2, R * 128])
        o_sb = sb("o_sb", [128, R * 128])
        rden = sb("rden", [128, R * G, T * 2])
        heads = sb("heads", [128, T, DIM])
        headsT = sb("headsT", [128, T * 128])
        summed = sb("summed", [128, T, DIM])
        stats = sb("stats", [128, T, 6])
        moments = sb("moments", [128, T, 2])
        var_eps = sb("var_eps", [128, T])
        ln_rstd = sb("ln_rstd", [128, T])
        x1 = sb("x1", [128, T, DIM])
        X0 = sb("X0", [128, TOK])
        xsum = sb("xsum", [128, BATCH])

        X = sb("X", [128, TOK])
        Y = sb("Y", [128, TOK])
        cn_w1 = sb("cn_w1", [128, 128])
        cn_w2 = sb("cn_w2", [128, 64])
        cn_w3 = sb("cn_w3", [128, 64])
        cn_w4 = sb("cn_w4", [128, 4])
        cn_b1 = sb("cn_b1", [128, 1])
        cn_b2 = sb("cn_b2", [128, 1])
        cn_b3 = sb("cn_b3", [128, 1])
        cn_b4 = sb("cn_b4", [4, 2])
        gc_w1 = sb("gc_w1", [128, 64])
        gc_w2 = sb("gc_w2", [64, 32])
        gc_w3 = sb("gc_w3", [32, 1])
        gc_b1 = sb("gc_b1", [64, 1])
        gc_b2 = sb("gc_b2", [32, 1])
        gc_b3 = sb("gc_b3", [4, 2])
        arange_in = sb("arange_in", [128, 1])
        arange7 = sb("arange7", [4, 1])
        spread = sb("spread", [36, 4, 128])
        pick = sb("pick", [36, 4, 128])
        hg1 = sb("hg1", [64, 8])
        hg2 = sb("hg2", [32, 8])
        tanh_g = sb("tanh_g", [4, 4])
        h1 = sb("h1", [128, 4 * 512])
        h2 = sb("h2", [128, 2 * 512])
        h3 = sb("h3", [128, 512])
        coup = [sb(f"coup{h}", [36, 512]) for h in range(2)]
        cY = sb("cY", [128, 2, 512])
        cX = sb("cX", [128, 2, 512])
        f_stats = sb("f_stats", [128, 8, 4, 6])
        f_mom = sb("f_mom", [128, 8, 4, 2])
        f_var = sb("f_var", [128, 8, 4])
        f_rstd = sb("f_rstd", [128, 8, 4])
        f_shift = sb("f_shift", [128, 8, 4])
        result = sb("result", [128, 4, 4, DIM])

        S = [ps(f"S{i}", [128, 2, R * 128]) for i in range(2)]
        O = ps("O", [128, R * 128])
        MA = ps("MA", [128, 512])
        MB = ps("MB", [128, 512])
        MC = ps("MC", [128, 512])
        MB16 = MB[:, :].bitcast(BF16)
        MC16 = MC[:, :].bitcast(BF16)

        names = ("w_proj_loaded trig_gain_loaded ident_future_loaded w_out_loaded ffn_loaded tables_ready zeros_ready biases_halved "
                 "proj_done qkvg_ready gate_ready values_ready "
                 "square_done sum_sq_done sum_eps_done bits_step_done estimate_ready root_step_done rstd_ready turned_done rotated_done roped_done "
                 "part0_done rest1_done part1_done parts_ready gain_step_done bounded_ready "
                 "block_scored block_max_done max_step_done max_parts_ready "
                 "q0_turned_max q1_turned_max q0_ready_max q1_ready_max "
                 "q0_turned q1_turned k_turned q0_ready q1_ready k_ready k_ready_act "
                 "o_ready o_turned rden_done heads_done heads_turned headsT_ready projected summed_done "
                 "stats_done moments_done var_eps_done ln_rstd_ready x1_ready x1_turned X0_ready xsum_ready "
                 "zeros_done powers_ready w_out_step_done pick_done g1_done hg1_ready g2_done hg2_ready g3_done tanh_g_ready coup_ready spread_ready XY_ready "
                 "h3_done gelu3_done z_done tanh_ready sum_ready "
                 "turned_back f_stats_done f_moments_done f_var_done f_rstd_done f_shift_done result_ready").split()
        n_ = {n: sem(n) for n in names}
        xT_loaded = [sem(f"xT_loaded{p}") for p in range(2)]
        res_loaded = [sem(f"res_loaded{p}") for p in range(2)]
        scores_done = [[sem(f"scores_done_{k}{g}") for g in range(G)] for k in range(3)]
        exp_done = [[sem(f"exp_done_{k}{g}") for g in range(G)] for k in range(3)]
        masked = {k: [sem(f"masked_{k}{g}") for g in range(G)] for k in DIAGONAL}
        pv_done = [sem(f"pv_done_{k}") for k in range(3)]
        h1_done = [sem(f"h1_done{c}") for c in range(2)]
        gelu1_done = [sem(f"gelu1_done{c}") for c in range(2)]
        h2_done = [sem(f"h2_done{c}") for c in range(2)]
        gelu2_done = [sem(f"gelu2_done{c}") for c in range(2)]
        spread_done = [sem(f"spread_done{c}") for c in range(4)]
        cY_done = [sem(f"cY_done{c}") for c in range(4)]
        cX_done = [sem(f"cX_done{c}") for c in range(4)]
        X_done = [sem(f"X_done{c}") for c in range(4)]
        Y_done = [sem(f"Y_done{c}") for c in range(4)]
        stored = [sem(f"stored{c}") for c in range(4)]
        block = ctx.enter_context(nc.Block())

        def batches(eng, step):
            step(0, 0, 0)
            step(1, 1, 0)
            with eng.Fori(1, BATCH // 2 - 1) as i:
                step(eng.snap(i * 2), 0, i)
                step(eng.snap(i * 2 + 1), 1, i)
            step(BATCH - 2, 0, BATCH // 2 - 1)
            step(BATCH - 1, 1, BATCH // 2 - 1)

        def cycles(eng, half_cycle):
            half_cycle(2, 0, False, False)
            half_cycle(3, 1, False, False)
            half_cycle(4, 0, False, True)
            half_cycle(5, 1, False, True)

        @block.sync
        def _(sp):
            sp.dma_start(w_proj[:, :], A["w_proj"]).then_inc(n_["w_proj_loaded"], 16)
            sp.dma_start(xT_in[0][:, :], A["xT"][0]).then_inc(xT_loaded[0], 16)
            sp.dma_start(trig[:, :, :, :], A["trig"]).then_inc(n_["trig_gain_loaded"], 16)
            sp.dma_start(gain[:, :], A["gain"]).then_inc(n_["trig_gain_loaded"], 16)
            sp.dma_start(ident[:, :], A["ident"]).then_inc(n_["ident_future_loaded"], 16)
            sp.dma_start(future_in[:, :], A["future"]).then_inc(n_["ident_future_loaded"], 16)
            sp.dma_start(xT_in[1][:, :], A["xT"][1]).then_inc(xT_loaded[1], 16)
            for tile, name in ((sel_s, "sel_s"), (lam, "lam"), (w_o0, "w_o0"), (w_o1, "w_o1")):
                sp.dma_start(tile[:, :], A[name]).then_inc(n_["w_out_loaded"], 16)
            for p in range(2):
                sp.dma_start(x_res[p][:, :, :], A["x"][p].rearrange("(t p) d -> p t d", p=128)).then_inc(res_loaded[p], 16)

            def load_projected(n, p):
                src = A["xT"][bass.ds(n + 2, 1)].rearrange("o d s -> d (o s)")
                sp.wait_ge(n_["proj_done"], n + 1)
                sp.dma_start(xT_in[p][:, :], src).then_inc(xT_loaded[p], 16)

            def load_residual(n, p):
                res = A["x"][bass.ds(n + 2, 1)].rearrange("o (t p) d -> p (o t) d", p=128)
                sp.wait_ge(n_["summed_done"], n + 1)
                sp.dma_start(x_res[p][:, :, :], res).then_inc(res_loaded[p], 16)

            load_projected(0, 0)
            load_projected(1, 1)
            with sp.Fori(1, BATCH // 2 - 1) as i:
                load_projected(sp.snap(i * 2), 0)
                load_residual(sp.snap(i * 2 - 2), 0)
                load_projected(sp.snap(i * 2 + 1), 1)
                load_residual(sp.snap(i * 2 - 1), 1)
            sp.wait_ge(n_["zeros_ready"], 2)
            loads = [(cn_w1[:, :], "cn_w1"), (cn_w2[:, :], "cn_w2"), (cn_w3[0:64, 0:32], "cn_w3"),
                     (cn_w3[64:128, 32:64], "cn_w3"), (cn_b1[:, :], "cn_b1"), (cn_b2[:, :], "cn_b2"),
                     (cn_b3[:, :], "cn_b3"), (cn_b4[:, 0:1], "cn_b4"), (gc_w1[:, :], "gc_w1"), (gc_w2[:, :], "gc_w2"),
                     (gc_w3[:, :], "gc_w3"), (gc_b1[:, :], "gc_b1"), (gc_b2[:, :], "gc_b2"), (gc_b3[:, 0:1], "gc_b3"),
                     (arange_in[:, :], "arange_in"), (pick[:, :, :], "pick")]
            loads += [(cn_w4[32 * c:32 * c + 32, c:c + 1], "cn_w4") for c in range(4)]
            assert len(loads) == FFN_LOADS
            for dst, name in loads:
                sp.dma_start(dst, A[name]).then_inc(n_["ffn_loaded"], 16)
            load_residual(BATCH - 4, 0)
            load_residual(BATCH - 3, 1)
            for f in range(8):
                sp.wait_ge(n_["result_ready"], f + 1)
                sp.dma_start(out.rearrange("(f t p) d -> f p t d", t=4, p=128)[f], result[:, f % 4, :, :])\
                  .then_inc(stored[f % 4], 16)
            for c in range(4):
                sp.wait_ge(stored[c], 32)

        @block.tensor
        def _(pe):
            def project(b, p, half_b):
                reach(pe, n_["qkvg_ready"], b)
                reach(pe, n_["summed_done"], b - 3)
                pe.wait_ge(xT_loaded[p], (half_b + 1) * 16)
                for t in range(T):
                    mm = pe.matmul(MA[:, t * PROJ:(t + 1) * PROJ], xT_in[p][:, t * 128:(t + 1) * 128], w_proj[:, :],
                                   start=True, stop=True)
                mm.then_inc(n_["proj_done"], 1)

            def turn_queries(b, t, parts_in="parts_ready", turned="turned"):
                pe.wait_ge(n_[parts_in], b + 1)
                if t == 1:
                    reach(pe, n_["X0_ready"], b - 2)
                bank = (MC16, MB16)[t]
                for n in range(R * 2):
                    u = (t * R * 2 + n) * G
                    mm = pe.transpose(bank[:, n * 128:(n + 1) * 128],
                                      parts[:, u:u + G, :, :].rearrange("p u s d -> p (u s d)"), ident16[:, :])
                mm.then_inc(n_[f"q{t}_{turned}"], 1)

            def turn_keys(b):
                pe.wait_ge(n_["parts_ready"], b + 1)
                pe.wait_ge(n_["q0_ready"], b + 1)
                for n in range(T * 2):
                    u = NQ + n * G
                    mm = pe.transpose(MC16[:, n * 128:(n + 1) * 128],
                                      parts[:, u:u + G, :, :].rearrange("p u s d -> p (u s d)"), ident16[:, :])
                mm.then_inc(n_["k_turned"], 1)

            def blocks_for_maximum(b, p):
                pe.wait_ge(n_["q0_ready"], b + 1)
                pe.wait_ge(n_["q1_ready"], b + 1)
                pe.wait_ge(n_["k_ready"], b + 1)
                pe.wait_ge(n_["k_ready_act"], b + 1)
                for k, (kt, qt) in enumerate(KINDS):
                    for n in range(R * 2):
                        if k * R * 2 + n >= 2:
                            pe.wait_ge(n_["block_max_done"], b * BLOCKS + k * R * 2 + n - 1)
                        r, s = n // 2, n % 2
                        bank = (MB, MC)[n % 2]
                        mm = pe.matmul(bank[:, :].rearrange("p (g n) -> p g n", g=G), qT[p][:, qt, r, s, :],
                                       kT[p][:, :, kt, s, :], start=True, stop=k not in DIAGONAL)
                        if k in DIAGONAL:
                            mm = pe.matmul(bank[:, :], ident16[:, :], future16[:, :, :].rearrange("p g n -> p (g n)"),
                                           start=False, stop=True)
                        mm.then_inc(n_["block_scored"], 1)
                for t in range(T):
                    turn_queries(b, t, "max_parts_ready", "turned_max")

            def scores(b, p, k, g, general):
                pair = k * G + g
                kt, qt = KINDS[k]
                if k == 0 and g == 0:
                    pe.wait_ge(n_["k_ready"], b + 1)
                    pe.wait_ge(n_["k_ready_act"], b + 1)
                    pe.wait_ge(n_["q0_ready_max" if general else "q0_ready"], b + 1)
                if k == 1 and g == 0:
                    pe.wait_ge(n_["q1_ready_max" if general else "q1_ready"], b + 1)
                if pair >= 2:
                    pe.wait_ge(exp_done[(pair - 2) // G][(pair - 2) % G], b + 1)
                else:
                    reach(pe, exp_done[2][2 + pair], b)
                for s in range(2):
                    late = general and k in DIAGONAL
                    mm = pe.matmul(S[pair % 2][:, s, :], kT[p][:, g, kt, s, :], qT[p][:, qt, :, s, :],
                                   start=True, stop=not late)
                    if late:
                        mm = pe.matmul(S[pair % 2][:, s, :].rearrange("p (r n) -> p r n", r=R), future16[:, 0, :],
                                       ident16[:, :].rearrange("p (o n) -> p o n", o=1).broadcast_to([128, R, 128]),
                                       start=False, stop=True)
                mm.then_inc(scores_done[k][g], 1)

            def weigh(b, p, k, s):
                kt, qt = KINDS[k]
                first = k == 0 and s == 0
                if first:
                    pe.wait_ge(n_["values_ready"], b + 1)
                    reach(pe, n_["o_ready"], b)
                if s == 0:
                    for g in range(G):
                        pe.wait_ge((masked if k in DIAGONAL else exp_done)[k][g], b + 1)
                at = PAD - OUTROW * (qt * 2 + s)
                for g in range(G):
                    mm = pe.matmul(O[32 * g:32 * g + 32, :], values[p][:, kt, g, s, at:at + 32], probs[:, k, g, s, :],
                                   start=first, stop=(k == 2 and s == 1))
                if s == 1:
                    mm.then_inc(pv_done[k], 1)

            def turn_outputs(b, more):
                pe.wait_ge(n_["o_ready"], b + 1)
                if more:
                    pe.wait_ge(n_["q1_ready"], b + 3)
                else:
                    pe.wait_ge(n_["X0_ready"], b)
                for r in range(R):
                    mm = pe.transpose(MB[:, r * 128:(r + 1) * 128], o_sb[:, r * 128:(r + 1) * 128], ident[:, :])
                mm.then_inc(n_["o_turned"], 1)

            def turn_heads(b, projected_more):
                pe.wait_ge(n_["heads_done"], b + 1)
                reach(pe, n_["summed_done"], b)
                if projected_more:
                    pe.wait_ge(n_["qkvg_ready"], b + 4)
                for t in range(T):
                    mm = pe.transpose(MA[:, t * 128:(t + 1) * 128], heads[:, t, :], ident[:, :])
                mm.then_inc(n_["heads_turned"], 1)

            def output_projection(b):
                pe.wait_ge(n_["headsT_ready"], b + 1)
                for t in range(T):
                    mm = pe.matmul(MA[:, t * 128:(t + 1) * 128], headsT[:, t * 128:(t + 1) * 128], w_out[:, :],
                                   start=True, stop=True)
                mm.then_inc(n_["projected"], 1)

            def turn_x1(b):
                pe.wait_ge(n_["x1_ready"], b + 1)
                for t in range(T):
                    mm = pe.transpose(MB[:, t * 128:(t + 1) * 128], x1[:, t, :], ident[:, :])
                mm.then_inc(n_["x1_turned"], 1)

            def attend(b, p, half_b, general):
                first, second, last = (isinstance(b, int) and b == n for n in (0, 1, BATCH - 1))
                project_more = not last and not (isinstance(b, int) and b == BATCH - 2)
                scores(b, p, 0, 0, general)
                if not first:
                    weigh(b - 1, 1 - p, 1, 1)
                scores(b, p, 0, 1, general)
                if project_more:
                    project(b + 2, p, half_b + 1)
                scores(b, p, 0, 2, general)
                if not first:
                    weigh(b - 1, 1 - p, 2, 0)
                scores(b, p, 0, 3, general)
                if not first and not second:
                    turn_x1(b - 2)
                if not last:
                    turn_queries(b + 1, 0)
                scores(b, p, 1, 0, general)
                if not first:
                    weigh(b - 1, 1 - p, 2, 1)
                scores(b, p, 1, 1, general)
                if not last:
                    turn_queries(b + 1, 1)
                scores(b, p, 1, 2, general)
                weigh(b, p, 0, 0)
                scores(b, p, 1, 3, general)
                if not last:
                    turn_keys(b + 1)
                if not first:
                    turn_outputs(b - 1, not last)
                scores(b, p, 2, 0, general)
                weigh(b, p, 0, 1)
                scores(b, p, 2, 1, general)
                if not first:
                    turn_heads(b - 1, project_more)
                scores(b, p, 2, 2, general)
                weigh(b, p, 1, 0)
                scores(b, p, 2, 3, general)
                if not first:
                    output_projection(b - 1)
                if general and not last:
                    blocks_for_maximum(b + 1, 1 - p)

            def attention(general):
                turn_queries(0, 0)
                turn_queries(0, 1)
                turn_keys(0)
                if general:
                    blocks_for_maximum(0, 0)
                pe.wait_ge(n_["w_out_step_done"], 3)
                batches(pe, lambda b, p, half_b: attend(b, p, half_b, general))

            pe.wait_ge(n_["w_proj_loaded"], 16)
            project(0, 0, 0)
            project(1, 1, 0)
            pe.wait_ge(n_["bounded_ready"], 1)
            is_bounded = pe.value_load(bounded[0:1, 0:1], min_val=0, max_val=1)
            with pe.If(is_bounded > 0):
                attention(False)
            with pe.Else():
                attention(True)

            def dense1(u, h, first, c):
                if not first:
                    for j in (2 * c, 2 * c + 1):
                        pe.wait_ge(X_done[j], u - 1)
                if u >= 1:
                    pe.wait_ge(gelu1_done[c], u)
                else:
                    pe.wait_ge(exp_done[2][2 + c], BATCH)
                for j in range(2):
                    at = h * 2048 + (2 * c + j) * 512
                    mm = pe.matmul(S[c][:, j, :], cn_w1[:, :], X[:, at:at + 512] if not first else X0[:, at:at + 512],
                                   start=True, stop=True)
                mm.then_inc(h1_done[c], 1)

            def dense2(u, c):
                pe.wait_ge(gelu1_done[c], u + 1)
                bank = MC if u == 0 else MA
                if c == 1:
                    pe.wait_ge(gelu2_done[0], u + 1)
                elif u >= 1:
                    pe.wait_ge(gelu2_done[1], u)
                else:
                    pe.wait_ge(n_["tanh_g_ready"], 1)
                for j in range(2):
                    mm = pe.matmul(bank[64 * j:64 * j + 64, :], cn_w2[:, :], h1[:, (2 * c + j) * 512:(2 * c + j + 1) * 512],
                                   start=True, stop=True)
                mm.then_inc(h2_done[c], 1)

            def dense3(u):
                if u >= 1:
                    pe.wait_ge(n_["tanh_ready"], u)
                for c in range(2):
                    pe.wait_ge(gelu2_done[c], u + 1)
                    mm = pe.matmul(MB[64 * c:64 * c + 64, :], cn_w3[:, :], h2[:, c * 512:(c + 1) * 512],
                                   start=True, stop=True)
                mm.then_inc(n_["h3_done"], 1)

            def dense4(u):
                pe.wait_ge(n_["gelu3_done"], u + 1)
                pe.matmul(MB[0:4, :], cn_w4[:, :], h3[:, :], start=True, stop=True).then_inc(n_["z_done"], 1)

            def spread_coupling(u, h, j):
                pe.wait_ge(n_["tanh_ready"], u + 1)
                if j >= 2:
                    pe.wait_ge((cX_done if u < 4 else cY_done)[j - 2], u + 1)
                elif u >= 1:
                    pe.wait_ge((cX_done if u - 1 < 4 else cY_done)[j + 2], u)
                pe.matmul((O, MC)[j % 2][:, :], spread[:, j, :], coup[h][:, :], start=True, stop=True)\
                  .then_inc(spread_done[j], 1)

            def global_net(h, layer):
                bank = (MC, MB)[h]
                if layer == 1:
                    pe.wait_ge(n_["xsum_ready"], 8 * (h + 1))
                    pe.matmul(bank[0:64, 0:8], gc_w1[:, :], xsum[:, 8 * h:8 * h + 8], start=True, stop=True).then_inc(n_["g1_done"], 1)
                elif layer == 2:
                    pe.wait_ge(n_["hg1_ready"], h + 1)
                    pe.matmul(bank[0:32, 0:8], gc_w2[:, :], hg1[:, :], start=True, stop=True).then_inc(n_["g2_done"], 1)
                else:
                    pe.wait_ge(n_["hg2_ready"], h + 1)
                    for n in range(2):
                        mm = pe.matmul(bank[0:4, n:n + 1], hg2[:, n:n + 7:2], gc_w3[:, :], start=True, stop=True)
                    mm.then_inc(n_["g3_done"], 1)

            def half_cycle(u, h, first, last):
                dense1(u, h, first, 0)
                dense4(u - 1)
                dense1(u, h, first, 1)
                spread_coupling(u - 1, 1 - h, 0)
                spread_coupling(u - 1, 1 - h, 1)
                dense2(u, 0)
                spread_coupling(u - 1, 1 - h, 2)
                dense2(u, 1)
                spread_coupling(u - 1, 1 - h, 3)
                dense3(u)

            def turn_back(f):
                pe.wait_ge(X_done[f % 4], CYCLES * 2 - 1 + f // 4)
                if f >= 4:
                    pe.wait_ge(n_["result_ready"], f - 3)
                bank = S[(f % 4) // 2][:, f % 2, :]
                for t in range(4):
                    at = f * 512 + t * 128
                    mm = pe.transpose(bank[:, t * 128:(t + 1) * 128], X0[:, at:at + 128], ident[:, :])
                mm.then_inc(n_["turned_back"], 1)

            last_b = BATCH - 1
            pe.wait_ge(n_["ffn_loaded"], 16 * FFN_LOADS)
            weigh(last_b, last_b % 2, 1, 1)
            global_net(0, 1)
            dense1(0, 0, True, 0)
            global_net(0, 2)
            dense1(0, 0, True, 1)
            global_net(0, 3)
            turn_x1(last_b - 1)
            dense2(0, 0)
            weigh(last_b, last_b % 2, 2, 0)
            dense2(0, 1)
            weigh(last_b, last_b % 2, 2, 1)
            turn_outputs(last_b, False)
            turn_heads(last_b, False)
            dense3(0)
            output_projection(last_b)
            dense4(0)
            pe.wait_ge(n_["spread_ready"], 1)
            spread_coupling(0, 0, 0)
            spread_coupling(0, 0, 1)
            turn_x1(last_b)
            pe.wait_ge(n_["X0_ready"], BATCH)
            dense1(1, 1, True, 0)
            spread_coupling(0, 0, 2)
            global_net(1, 1)
            dense1(1, 1, True, 1)
            global_net(1, 2)
            spread_coupling(0, 0, 3)
            dense2(1, 0)
            global_net(1, 3)
            dense2(1, 1)
            pe.wait_ge(n_["tanh_g_ready"], 2)
            dense3(1)

            cycles(pe, half_cycle)
            turn_back(0)
            turn_back(1)
            dense4(5)
            turn_back(2)
            turn_back(3)
            spread_coupling(5, 1, 0)
            spread_coupling(5, 1, 1)
            spread_coupling(5, 1, 2)
            turn_back(4)
            spread_coupling(5, 1, 3)
            turn_back(5)
            turn_back(6)
            turn_back(7)

        @block.scalar
        def _(act):
            def copy_projection(b, p):
                act.wait_ge(n_["proj_done"], b + 1)
                reach(act, n_["values_ready"], b - 1)
                act.activation(qkvg[p][:, :, :].rearrange("p t c -> p (t c)"), MA[:, 0:T * PROJ], ACT.Copy)\
                   .then_inc(n_["qkvg_ready"], 1)

            def keep_x1(b):
                at = b * SEQ
                act.wait_ge(n_["x1_turned"], b + 1)
                act.activation(X0[:, bass.ds(at, SEQ)], MB[:, 0:SEQ], ACT.Copy).then_inc(n_["X0_ready"], 1)

            def gate_tanh(b, p):
                act.wait_ge(n_["qkvg_ready"], b + 1)
                act.activation(gate[p][:, :, :], qkvg[p][:, :, QK + KV:PROJ], ACT.Tanh, scale=0.5)\
                   .then_inc(n_["gate_ready"], 1)

            def exponentials(b, k, g):
                act.wait_ge(scores_done[k][g], b + 1)
                if g == 0:
                    reach(act, pv_done[k], b)
                act.activation(probs[:, k, g, :, :], S[(k * G + g) % 2][:, :, :], ACT.Exp).then_inc(exp_done[k][g], 1)

            def copy_keys(b, p):
                act.wait_ge(n_["k_turned"], b + 1)
                for g in range(KEYS_ON_DVE, G):
                    q = slice(32 * g, 32 * g + 32)
                    last = act.activation(kT[p][q, g, :, :, :].rearrange("p t s n -> p (t s n)"), MC16[q, 0:T * 2 * 128], ACT.Copy)
                last.then_inc(n_["k_ready_act"], 1)

            def copy_heads(b):
                act.wait_ge(n_["heads_turned"], b + 1)
                reach(act, n_["projected"], b)
                act.activation(headsT[:, :], MA[:, 0:T * 128], ACT.Copy).then_inc(n_["headsT_ready"], 1)

            def attend(b, p, half_b):
                first, second, last = (isinstance(b, int) and b == n for n in (0, 1, BATCH - 1))
                project_more = not last and not (isinstance(b, int) and b == BATCH - 2)
                exponentials(b, 0, 0)
                exponentials(b, 0, 1)
                if project_more:
                    copy_projection(b + 2, p)
                exponentials(b, 0, 2)
                if project_more:
                    gate_tanh(b + 2, p)
                exponentials(b, 0, 3)
                if not first and not second:
                    keep_x1(b - 2)
                exponentials(b, 1, 0)
                exponentials(b, 1, 1)
                exponentials(b, 1, 2)
                exponentials(b, 1, 3)
                exponentials(b, 2, 0)
                if not last:
                    copy_keys(b + 1, 1 - p)
                exponentials(b, 2, 1)
                if not first:
                    copy_heads(b - 1)
                exponentials(b, 2, 2)
                exponentials(b, 2, 3)

            for b in range(2):
                copy_projection(b, b)
                gate_tanh(b, b)
            copy_keys(0, 0)
            batches(act, attend)
            act.wait_ge(n_["ffn_loaded"], 16 * FFN_LOADS)
            act.mul(cn_b4[:, 1:2], cn_b4[:, 0:1], 0.5)
            act.mul(gc_b3[:, 1:2], gc_b3[:, 0:1], 0.5).then_inc(n_["biases_halved"], 1)
            act.wait_ge(n_["biases_halved"], 1)

            def global_net(h, layer):
                bank = (MC, MB)[h]
                act.wait_ge(n_[f"g{layer}_done"], h + 1)
                if layer == 1:
                    act.activation(hg1[:, :], bank[0:64, 0:8], ACT.Gelu, bias=gc_b1[:, :], scale=1.0 / SEQ).then_inc(n_["hg1_ready"], 1)
                elif layer == 2:
                    act.activation(hg2[:, :], bank[0:32, 0:8], ACT.Gelu, bias=gc_b2[:, :]).then_inc(n_["hg2_ready"], 1)
                else:
                    act.activation(tanh_g[:, 2 * h:2 * h + 2], bank[0:4, 0:2], ACT.Tanh, bias=gc_b3[:, 1:2], scale=0.5)\
                       .then_inc(n_["tanh_g_ready"], 1)

            def gelu1(u, c):
                act.wait_ge(h1_done[c], u + 1)
                if u >= 1:
                    act.wait_ge(h2_done[c], u)
                act.activation(h1[:, c * 1024:(c + 1) * 1024], S[c][:, :, :].rearrange("p s n -> p (s n)"),
                               ACT.Gelu, bias=cn_b1[:, :]).then_inc(gelu1_done[c], 1)

            def coupling_tanh(u, h):
                act.wait_ge(n_["z_done"], u + 1)
                if u >= 2:
                    act.wait_ge(spread_done[3], u - 1)
                else:
                    act.wait_ge(n_["coup_ready"], u + 1)
                act.activation(coup[h][0:4, :], MB[0:4, :], ACT.Tanh, bias=cn_b4[:, 1:2], scale=0.5).then_inc(n_["tanh_ready"], 1)

            def gelu2(u, c):
                act.wait_ge(h2_done[c], u + 1)
                if u >= 1:
                    act.wait_ge(n_["h3_done"], u)
                act.activation(h2[:, c * 512:(c + 1) * 512], (MC if u == 0 else MA)[:, :], ACT.Gelu, bias=cn_b2[:, :])\
                   .then_inc(gelu2_done[c], 1)

            def gelu3(u):
                act.wait_ge(n_["h3_done"], u + 1)
                if u >= 1:
                    act.wait_ge(n_["z_done"], u)
                act.activation(h3[:, :], MB[:, :], ACT.Gelu, bias=cn_b3[:, :]).then_inc(n_["gelu3_done"], 1)

            def half_cycle(u, h, first, last):
                gelu1(u, 0)
                coupling_tanh(u - 1, 1 - h)
                gelu1(u, 1)
                gelu2(u, 0)
                gelu2(u, 1)
                gelu3(u)

            def store_normalized(f):
                act.wait_ge(n_["f_shift_done"], f + 1)
                if f >= 4:
                    act.wait_ge(stored[f % 4], 16)
                bank = S[(f % 4) // 2][:, f % 2, :]
                for t in range(4):
                    a = act.activation(result[:, f % 4, t, :], bank[:, t * 128:(t + 1) * 128], ACT.Identity,
                                       bias=f_shift[:, f, t:t + 1], scale=f_rstd[:, f, t:t + 1])
                a.then_inc(n_["result_ready"], 1)

            global_net(0, 1)
            gelu1(0, 0)
            global_net(0, 2)
            gelu1(0, 1)
            global_net(0, 3)
            keep_x1(BATCH - 2)
            gelu2(0, 0)
            gelu2(0, 1)
            copy_heads(BATCH - 1)
            gelu3(0)
            coupling_tanh(0, 0)
            keep_x1(BATCH - 1)
            gelu1(1, 0)
            global_net(1, 1)
            gelu1(1, 1)
            global_net(1, 2)
            gelu2(1, 0)
            global_net(1, 3)
            gelu2(1, 1)
            gelu3(1)

            cycles(act, half_cycle)
            coupling_tanh(5, 1)
            for f in range(8):
                store_normalized(f)

        @block.vector
        def _(dve):
            dve.memset(ln_eps[:, :], LN_EPS)
            dve.memset(one_half[:, :], 1.5)
            dve.memset(minus_half[:, :], -0.5).then_inc(n_["powers_ready"], 1)
            dve.wait_ge(n_["trig_gain_loaded"], 32)
            SCALE, ROOT = HALF ** -0.5 * HD ** 0.5, HD ** 0.5
            for t in range(T):
                for s in range(2):
                    for table, c, sign in ((rope_cos, 0, 1.0), (rope_sin, 1, 1.0 - 2.0 * s)):
                        row = trig[:, c, t, :].rearrange("p (o d) -> p o d", o=1)
                        dve.scalar_tensor_tensor(
                            out=table[:, t, 0:HEADS, s, :], in0=row.broadcast_to([128, HEADS, HALF]), scalar=SCALE * sign,
                            in1=gain[:, :].rearrange("p (h o) -> p h o", o=1).broadcast_to([128, HEADS, HALF]),
                            op0=ALU.mult, op1=ALU.mult)
                        last = dve.tensor_scalar(table[:, t, HEADS:, s, :], row.broadcast_to([128, G, HALF]), ROOT * sign, None, ALU.mult)
            last.then_inc(n_["tables_ready"], 1)

            def rotate(b, p):
                x_heads = qkvg[p][:, :, 0:QK].rearrange("p t (n d) -> p t n d", d=HALF)
                dve.wait_ge(n_["qkvg_ready"], b + 1)
                dve.tensor_tensor(square[:, :, :], qkvg[p][:, :, 0:QK], qkvg[p][:, :, 0:QK], ALU.mult).then_inc(n_["square_done"], 1)
                flat = lambda a: a.rearrange("p t h s d -> p t (h s d)")
                dve.tensor_tensor(flat(turned[:, :, :, :, :]), qkvg[p][:, :, 0:QK], flat(rope_cos[:, :, :, :, :]), ALU.mult)
                dve.wait_ge(n_["square_done"], b + 1)
                dve.tensor_reduce(sum_sq[:, :], square[:, :, :].rearrange("p t (h c) -> p (t h) c", c=HD), AX.X, ALU.add)\
                   .then_inc(n_["sum_sq_done"], 1)
                for t in range(T):
                    last = dve.tensor_tensor(turned2[:, t, :, :, :], qkvg[p][:, t, 0:QK].rearrange("p (h s d) -> p h s d", s=2, d=HALF)[:, :, ::-1, :],
                                             rope_sin[:, t, :, :, :], ALU.mult)
                last.then_inc(n_["turned_done"], 1)
                dve.wait_ge(n_["sum_sq_done"], b + 1)
                dve.tensor_scalar(sum_eps[:, :], sum_sq[:, :], HD * RMS_EPS, None, ALU.add).then_inc(n_["sum_eps_done"], 1)
                dve.wait_ge(n_["sum_eps_done"], b + 1)
                dve.tensor_scalar(bits[:, :].bitcast(I32), sum_eps[:, :].bitcast(I32), -0.5, ROOT_BITS, ALU.mult, ALU.add)\
                   .then_inc(n_["bits_step_done"], 1)
                dve.wait_ge(n_["turned_done"], b + 1)
                dve.tensor_tensor(rotated[:, :, :], flat(turned[:, :, :, :, :]), flat(turned2[:, :, :, :, :]), ALU.add)\
                   .then_inc(n_["rotated_done"], 1)
                dve.wait_ge(n_["bits_step_done"], b * 3 + 1)
                dve.tensor_tensor(bits_sq[:, :], bits[:, :], bits[:, :], ALU.mult).then_inc(n_["bits_step_done"], 1)
                dve.wait_ge(n_["bits_step_done"], b * 3 + 2)
                dve.scalar_tensor_tensor(out=bits_step[:, :], in0=bits_sq[:, :], scalar=-0.5, in1=sum_eps[:, :],
                                         op0=ALU.mult, op1=ALU.mult).then_inc(n_["bits_step_done"], 1)
                dve.wait_ge(n_["bits_step_done"], b * 3 + 3)
                dve.scalar_tensor_tensor(out=estimate[0][:, :], in0=bits_step[:, :], scalar=1.5, in1=bits[:, :],
                                         op0=ALU.add, op1=ALU.mult).then_inc(n_["estimate_ready"], 1)

            def normalize_queries(b):
                dve.wait_ge(n_["rotated_done"], b + 1)
                dve.wait_ge(n_["rstd_ready"], b + 1)
                for t in range(T):
                    for lo, hi, at, n in ((0, HEADS, t * R * 2 * G, R * 2), (HEADS, HEADS + G, NQ + t * 2 * G, 2)):
                        last = dve.tensor_tensor(
                            roped[:, at:at + n * G, :].rearrange("p (n g) d -> p g n d", g=G),
                            rotated[:, t, lo * HD:hi * HD].rearrange("p (g n d) -> p g n d", g=G, d=HALF),
                            rstd[:, t, lo:hi, :].rearrange("p h s -> p (h s)").rearrange("p (g n o) -> p g n o", g=G, o=1)
                            .broadcast_to([128, G, n, HALF]), ALU.mult)
                last.then_inc(n_["roped_done"], 1)

            def split(b):
                def slots(lo, n, a, b_, src):
                    dst = parts[:, a:b_, lo:lo + n, :]
                    src = src[:, a:b_, :].rearrange("p u (o d) -> p u o d", o=1)
                    return dst, (src.broadcast_to([128, b_ - a, n, HALF]) if n > 1 else src)
                N = NQ + NK
                dve.wait_ge(n_["roped_done"], b + 1)
                reach(dve, n_["k_turned"], b)
                dve.tensor_copy(*slots(0, 1, 0, N, roped)).then_inc(n_["part0_done"], 1)
                dve.tensor_copy(*slots(1, 2, 0, NQ, roped))
                dve.tensor_copy(*slots(4, 2, NQ, N, roped))
                dve.wait_ge(n_["part0_done"], b + 1)
                dve.tensor_tensor(rest1[:, :, :], roped[:, :, :], parts[:, :, 0, :], ALU.subtract).then_inc(n_["rest1_done"], 1)
                dve.wait_ge(n_["rest1_done"], b + 1)
                dve.tensor_copy(*slots(3, 1, 0, N, rest1)).then_inc(n_["part1_done"], 1)
                dve.tensor_copy(*slots(4, 1, 0, NQ, rest1))
                dve.tensor_copy(*slots(1, 1, NQ, N, rest1))
                dve.wait_ge(n_["part1_done"], b + 1)
                dve.tensor_tensor(parts[:, 0:NQ, 5, :], rest1[:, 0:NQ, :], parts[:, 0:NQ, 3, :], ALU.subtract)
                dve.tensor_tensor(parts[:, NQ:N, 2, :], rest1[:, NQ:N, :], parts[:, NQ:N, 3, :], ALU.subtract)\
                   .then_inc(n_["parts_ready"], 1)

            def gate_values(b, p):
                dve.wait_ge(n_["gate_ready"], b + 1)
                dve.scalar_tensor_tensor(out=values[p][:, :, :, :, PAD:PAD + HALF].rearrange("p t g s d -> p t (g s) d"),
                                         in0=gate[p][:, :, :].rearrange("p t (n d) -> p t n d", d=HALF), scalar=1.0,
                                         in1=qkvg[p][:, :, QK:QK + KV].rearrange("p t (n d) -> p t n d", d=HALF),
                                         op0=ALU.add, op1=ALU.mult)\
                   .then_inc(n_["values_ready"], 1)

            def copy_queries(b, p, t, suffix=""):
                dve.wait_ge(n_[f"q{t}_turned{suffix}"], b + 1)
                dve.tensor_copy(qT[p][:, t, :, :, :].rearrange("p r s n -> p (r s n)"), (MC16, MB16)[t][:, :])\
                   .then_inc(n_[f"q{t}_ready{suffix}"], 1)

            def copy_keys(b, p):
                dve.wait_ge(n_["k_turned"], b + 1)
                for g in range(KEYS_ON_DVE):
                    q = slice(32 * g, 32 * g + 32)
                    last = dve.tensor_copy(kT[p][q, g, :, :, :].rearrange("p t s n -> p (t s n)"), MC16[q, 0:T * 2 * 128])
                last.then_inc(n_["k_ready"], 1)

            def subtract_maximum(b, p):
                for k in range(len(KINDS)):
                    for n in range(R * 2):
                        dve.wait_ge(n_["block_scored"], b * BLOCKS + k * R * 2 + n + 1)
                        dve.tensor_reduce(block_max[:, k, n * G:(n + 1) * G], (MB, MC)[n % 2][:, :].rearrange("p (g n) -> p g n", g=G),
                                          AX.X, ALU.max).then_inc(n_["block_max_done"], 1)
                dve.wait_ge(n_["block_max_done"], (b + 1) * BLOCKS)
                dve.tensor_scalar(row_max[:, 0:NQ // 2], block_max[:, 0, :], 1.0, None, ALU.mult)
                dve.tensor_tensor(row_max[:, NQ // 2:], block_max[:, 1, :], block_max[:, 2, :], ALU.max).then_inc(n_["max_step_done"], 1)
                dve.wait_ge(n_["max_step_done"], b * 6 + 1)
                dve.tensor_scalar(minus_max[:, :], row_max[:, :], -1.0, None, ALU.mult).then_inc(n_["max_step_done"], 1)
                slot = lambda d: parts[:, 0:NQ, 6, d]
                dve.wait_ge(n_["max_step_done"], b * 6 + 2)
                dve.tensor_copy(slot(0), minus_max[:, :]).then_inc(n_["max_step_done"], 1)
                dve.wait_ge(n_["max_step_done"], b * 6 + 3)
                dve.tensor_tensor(row_max[:, :], minus_max[:, :], slot(0), ALU.subtract).then_inc(n_["max_step_done"], 1)
                dve.wait_ge(n_["max_step_done"], b * 6 + 4)
                dve.tensor_copy(slot(1), row_max[:, :]).then_inc(n_["max_step_done"], 1)
                dve.wait_ge(n_["max_step_done"], b * 6 + 5)
                dve.tensor_tensor(minus_max[:, :], row_max[:, :], slot(1), ALU.subtract).then_inc(n_["max_step_done"], 1)
                dve.wait_ge(n_["max_step_done"], b * 6 + 6)
                dve.tensor_copy(slot(2), minus_max[:, :]).then_inc(n_["max_parts_ready"], 1)
                for t in range(T):
                    copy_queries(b, p, t, "_max")
                dve.memset(parts[:, 0:NQ, 6, 0:3], 0.0)

            def copy_outputs(b):
                dve.wait_ge(pv_done[2], b + 1)
                dve.tensor_copy(o_sb[:, :], O[:, :]).then_inc(n_["o_ready"], 1)

            def normalize_heads(b):
                turned_o = MB[:, :].rearrange("p (n c) -> p n c", c=32)[:, :, 0:4 * OUTROW]\
                    .rearrange("p n (w c) -> p n w c", c=OUTROW)
                dve.wait_ge(n_["o_turned"], b + 1)
                dve.reciprocal(rden[:, :, :], turned_o[:, :, :, HALF]).then_inc(n_["rden_done"], 1)
                dve.wait_ge(n_["rden_done"], b + 1)
                for t in range(T):
                    last = dve.tensor_tensor(
                        heads[:, t, :].rearrange("p (n s d) -> p n s d", s=2, d=HALF),
                        turned_o[:, :, 2 * t:2 * t + 2, 0:HALF],
                        rden[:, :, 2 * t:2 * t + 2].rearrange("p n (s o) -> p n s o", o=1).broadcast_to([128, R * G, 2, HALF]),
                        ALU.mult)
                last.then_inc(n_["heads_done"], 1)

            def add_residual(b, p, half_b):
                dve.wait_ge(n_["projected"], b + 1)
                dve.wait_ge(res_loaded[p], (half_b + 1) * 16)
                dve.tensor_tensor(summed[:, :, :].rearrange("p t d -> p (t d)"), MA[:, 0:T * 128],
                                  x_res[p][:, :, :].rearrange("p t d -> p (t d)"), ALU.add).then_inc(n_["summed_done"], 1)
                dve.wait_ge(n_["summed_done"], b + 1)
                for t in range(T):
                    last = dve.bn_stats(stats[:, t, :], summed[:, t, :])
                last.then_inc(n_["stats_done"], 1)
                reach_alone(dve, n_["stats_done"], b + 1, n_["zeros_ready"])
                for t in range(T):
                    last = dve.bn_aggr(moments[:, t, :], stats[:, t, :])
                last.then_inc(n_["moments_done"], 1)

            def normalize(b):
                dve.wait_ge(n_["ln_rstd_ready"], b + 1)
                reach(dve, n_["x1_turned"], b)
                for t in range(T):
                    last = dve.tensor_scalar(x1[:, t, :], summed[:, t, :], moments[:, t, 0:1], ln_rstd[:, t:t + 1],
                                             ALU.subtract, ALU.mult)
                last.then_inc(n_["x1_ready"], 1)

            def sum_x1(b):
                at = b * SEQ
                reach_alone(dve, n_["X0_ready"], b + 1, n_["zeros_ready"])
                dve.tensor_reduce(xsum[:, bass.ds(b, 1)], X0[:, bass.ds(at, SEQ)], AX.X, ALU.add).then_inc(n_["xsum_ready"], 1)

            def attend(b, p, half_b, general):
                first, second, last = (isinstance(b, int) and b == n for n in (0, 1, BATCH - 1))
                project_more = not last and not (isinstance(b, int) and b == BATCH - 2)
                if not first and not second:
                    normalize(b - 2)
                if project_more:
                    rotate(b + 2, p)
                if not first:
                    copy_outputs(b - 1)
                if not last:
                    copy_queries(b + 1, 1 - p, 0)
                if not last:
                    copy_queries(b + 1, 1 - p, 1)
                    gate_values(b + 1, 1 - p)
                    copy_keys(b + 1, 1 - p)
                if not first:
                    normalize_heads(b - 1)
                if general:
                    if not first:
                        add_residual(b - 1, 1 - p, half_b - (1 - p))
                    if not last:
                        subtract_maximum(b + 1, 1 - p)
                if project_more:
                    normalize_queries(b + 2)
                    split(b + 2)
                if not first and not general:
                    add_residual(b - 1, 1 - p, half_b - (1 - p))
                if not first and not second:
                    sum_x1(b - 2)

            dve.wait_ge(n_["tables_ready"], 1)
            rotate(0, 0)
            dve.wait_ge(n_["ident_future_loaded"], 32)
            dve.tensor_copy(ident16[:, :], ident[:, :])
            dve.tensor_copy(future16[:, :, :], future_in[:, :].rearrange("p (o n) -> p o n", o=1).broadcast_to([128, G, 128]))
            dve.tensor_tensor(gain_sq[:, :], gain[:, :], gain[:, :], ALU.mult).then_inc(n_["gain_step_done"], 1)
            dve.wait_ge(n_["gain_step_done"], 1)
            dve.tensor_reduce(gain_top[:, :], gain_sq[:, :], AX.X, ALU.max).then_inc(n_["gain_step_done"], 1)
            dve.wait_ge(n_["gain_step_done"], 2)
            dve.tensor_scalar(bounded[:, :], gain_top[:, :], SAFE_GAIN ** 2, None, ALU.is_le).then_inc(n_["bounded_ready"], 1)
            dve.wait_ge(n_["w_out_loaded"], 64)
            dve.tensor_scalar(mix[:, 0:1], lam[:, :], sel_s[:, 1:2], sel_s[:, 0:1], ALU.mult, ALU.add)
            dve.tensor_scalar(mix[:, 1:2], lam[:, :], sel_s[:, 2:3], sel_s[:, 0:1], ALU.mult, ALU.add).then_inc(n_["w_out_step_done"], 1)
            dve.wait_ge(n_["w_out_step_done"], 1)
            dve.tensor_scalar(w_out[:, :], w_o1[:, :], mix[:, 0:1], None, ALU.mult).then_inc(n_["w_out_step_done"], 1)
            dve.wait_ge(n_["w_out_step_done"], 2)
            dve.scalar_tensor_tensor(out=w_out[:, :], in0=w_o0[:, :], scalar=mix[:, 1:2], in1=w_out[:, :],
                                     op0=ALU.mult, op1=ALU.add).then_inc(n_["w_out_step_done"], 1)
            dve.wait_ge(n_["zeros_ready"], 1)

            def attention(general):
                gate_values(0, 0)
                normalize_queries(0)
                split(0)
                rotate(1, 1)
                copy_queries(0, 0, 0)
                copy_queries(0, 0, 1)
                copy_keys(0, 0)
                if general:
                    subtract_maximum(0, 0)
                normalize_queries(1)
                split(1)
                batches(dve, lambda b, p, half_b: attend(b, p, half_b, general))
            is_bounded = dve.value_load(bounded[0:1, 0:1], min_val=0, max_val=1)
            with dve.If(is_bounded > 0):
                attention(False)
            with dve.Else():
                attention(True)

            dve.wait_ge(n_["ffn_loaded"], 16 * FFN_LOADS)
            dve.tensor_scalar(arange7[:, :], arange_in[0:4, :], 0.7, None, ALU.mult)
            dve.tensor_scalar(spread[:, :, :], pick[:, :, :], 1.0, None, ALU.mult).then_inc(n_["pick_done"], 1)
            dve.wait_ge(n_["pick_done"], 1)
            dve.tensor_scalar(spread[0:4, :, :], pick[0:4, :, :], arange_in[0:4, :], 0.3, ALU.mult, ALU.mult)\
               .then_inc(n_["spread_ready"], 1)

            def twist(h):
                at = slice(2048 * h, 2048 * h + 2048)
                dve.wait_ge(n_["X0_ready"], 8 * (h + 1))
                for q, (src, sign) in enumerate(((2, 1.0), (3, -1.0), (0, -1.0), (1, 1.0))):
                    last = dve.tensor_scalar(Y[32 * q:32 * q + 32, at], X0[32 * src:32 * src + 32, at], sign, None, ALU.mult)
                last.then_inc(n_["XY_ready"], 1)

            def constant_coupling(h):
                dve.wait_ge(n_["tanh_g_ready"], h + 1)
                dve.tensor_scalar(coup[h][32:36, :].rearrange("p (n c) -> p n c", n=2),
                                  tanh_g[:, 2 * h:2 * h + 2].rearrange("p (n o) -> p n o", o=1).broadcast_to([4, 2, SEQ]),
                                  arange7[:, :], 0.1, ALU.mult, ALU.add).then_inc(n_["coup_ready"], 1)

            def rotate_pair(u, h, first, last, j):
                at = slice(h * 2048 + j * 512, h * 2048 + (j + 1) * 512)
                c = (O, MC)[j % 2]
                old = X0 if first else X
                dve.wait_ge(spread_done[j], u + 1)
                dve.tensor_tensor(cY[:, j % 2, :], c[:, :], Y[:, at], ALU.mult).then_inc(cY_done[j], 1)
                if not last:
                    if j >= 2:
                        dve.wait_ge(Y_done[j - 2], u + 1)
                    elif u >= 1:
                        dve.wait_ge(Y_done[j + 2], u)
                    dve.tensor_tensor(cX[:, j % 2, :], c[:, :], old[:, at], ALU.mult).then_inc(cX_done[j], 1)
                    dve.wait_ge(cY_done[j], u + 1)
                    dve.tensor_tensor(X[:, at], old[:, at], cY[:, j % 2, :], ALU.add).then_inc(X_done[j], 1)
                else:
                    dve.wait_ge(cY_done[j], u + 1)
                    dve.wait_ge(n_["sum_ready"], (u - 4) * 4 + j + 1)
                    dve.tensor_tensor(X0[:, at], X0[:, at], cY[:, j % 2, :], ALU.add).then_inc(X_done[j], 1)

            def half_cycle(u, h, first, last):
                if u < 2:
                    dve.wait_ge(n_["XY_ready"], u + 1)
                for j in range(4):
                    rotate_pair(u, h, first, last, j)
                    if u == 5 and j < 2:
                        shift_of(j)
                        stats_of(j + 2)
                    if u == 5 and j >= 2:
                        shift_of(j)
                if u == 4:
                    for f in range(2):
                        stats_of(f)

            def stats_of(f):
                dve.wait_ge(n_["turned_back"], f + 1)
                bank = S[(f % 4) // 2][:, f % 2, :]
                for t in range(4):
                    last = dve.bn_stats(f_stats[:, f, t, :], bank[:, t * 128:(t + 1) * 128])
                last.then_inc(n_["f_stats_done"], 1)
                dve.wait_ge(n_["f_stats_done"], f + 1)
                for t in range(4):
                    last = dve.bn_aggr(f_mom[:, f, t, :], f_stats[:, f, t, :])
                last.then_inc(n_["f_moments_done"], 1)

            def shift_of(f):
                dve.wait_ge(n_["f_rstd_done"], f + 1)
                dve.scalar_tensor_tensor(out=f_shift[:, f, :], in0=f_mom[:, f, :, 0], scalar=-1.0, in1=f_rstd[:, f, :],
                                         op0=ALU.mult, op1=ALU.mult).then_inc(n_["f_shift_done"], 1)

            last_b = BATCH - 1
            normalize(last_b - 1)
            dve.wait_ge(n_["zeros_ready"], 3)
            dve.wait_ge(n_["spread_ready"], 1)
            twist(0)
            sum_x1(last_b - 1)
            copy_outputs(last_b)
            normalize_heads(last_b)
            constant_coupling(0)
            add_residual(last_b, 1, BATCH // 2 - 1)
            normalize(last_b)
            sum_x1(last_b)
            half_cycle(0, 0, True, False)
            twist(1)
            constant_coupling(1)
            half_cycle(1, 1, True, False)

            cycles(dve, half_cycle)
            stats_of(4)
            for f in range(5, 8):
                stats_of(f)
                shift_of(f - 1)
            shift_of(7)

        @block.gpsimd
        def _(pool):
            for p in range(2):
                pool.memset(kT[p][:, :, :, :, :], 0.0)
                pool.memset(values[p][:, :, :, :, :], 0.0)
            pool.memset(parts[:, :, :, :], 0.0).then_inc(n_["zeros_done"], 1)
            pool.wait_ge(n_["zeros_done"], 1)
            for p in range(2):
                pool.memset(values[p][:, :, :, :, PAD + HALF:PAD + OUTROW], 2.0)
            pool.memset(parts[:, NQ:, 6, 0:3], 1.0).then_inc(n_["zeros_ready"], 1)
            pool.memset(cn_w3[:, :], 0.0)
            pool.memset(cn_w4[:, :], 0.0).then_inc(n_["zeros_ready"], 1)
            for h in range(2):
                last = pool.memset(coup[h][:, :], 0.0)
            last.then_inc(n_["zeros_ready"], 1)

            def root(count, mean, eps, shifted, sem_in, sem_mid, out_, sem_out):
                n = shifted.shape[-1]
                pool.wait_ge(sem_in, count)
                pool.tensor_tensor(shifted, mean, eps[:, 0:n], ALU.add).then_inc(sem_mid, 1)
                pool.wait_ge(sem_mid, count)
                pool.tensor_tensor(out_, shifted, minus_half[:, 0:n], ALU.pow).then_inc(sem_out, 1)

            def refine(count):
                steps = 4 * NEWTON
                before = steps * (count - 1)
                done = n_["root_step_done"]
                pool.wait_ge(n_["estimate_ready"], count)
                pool.tensor_tensor(minus_half_sum[:, :], sum_eps[:, :], minus_half[:, :], ALU.mult).then_inc(done, 1)
                for n in range(NEWTON):
                    if n > 0:
                        pool.wait_ge(done, before + 4 * n + 1)
                    y = estimate[n][:, :]
                    pool.tensor_tensor(root_sq[:, :], y, y, ALU.mult).then_inc(done, 1)
                    pool.wait_ge(done, before + 4 * n + 2)
                    pool.tensor_tensor(root_step[:, :], root_sq[:, :], minus_half_sum[:, :], ALU.mult).then_inc(done, 1)
                    pool.wait_ge(done, before + 4 * n + 3)
                    pool.tensor_tensor(root_sq[:, :], root_step[:, :], one_half[:, :], ALU.add).then_inc(done, 1)
                    pool.wait_ge(done, before + 4 * n + 4)
                    if n < NEWTON - 1:
                        pool.tensor_tensor(estimate[n + 1][:, :], y, root_sq[:, :], ALU.mult).then_inc(done, 1)
                    else:
                        both = lambda a: a.rearrange("p (h o) -> p h o", o=1).broadcast_to([128, T * (HEADS + G), 2])
                        pool.tensor_tensor(rstd[:, :, :, :].rearrange("p t h s -> p (t h) s"), both(y), both(root_sq[:, :]),
                                           ALU.mult).then_inc(n_["rstd_ready"], 1)

            def mask(count, k, g):
                reach_alone(pool, exp_done[k][g], count, n_["zeros_ready"])
                p = probs[:, k, g, :, :].rearrange("p s (r q) -> p (s r) q", q=128)
                pool.affine_select(out=p, in_=p, compare_op=ALU.is_ge, fill=0.0, base=0,
                                   pattern=[[0, 2 * R], [1, 128]], channel_multiplier=-1).then_inc(masked[k][g], 1)

            def attend(now, first, refine_more):
                for g in range(G):
                    mask(now, 0, g)
                if refine_more:
                    refine(now + 2)
                for g in range(G):
                    mask(now, 2, g)
                if not first:
                    root(now - 1, moments[:, :, 1], ln_eps, var_eps[:, :], n_["moments_done"], n_["var_eps_done"],
                         ln_rstd[:, :], n_["ln_rstd_ready"])

            pool.wait_ge(n_["powers_ready"], 1)
            refine(1)
            refine(2)
            attend(1, True, True)
            attend(2, False, True)
            with pool.Fori(3, BATCH - 1) as now:
                attend(now, False, True)
            attend(BATCH - 1, False, False)
            attend(BATCH, False, False)
            last_b = BATCH - 1
            root(last_b + 1, moments[:, :, 1], ln_eps, var_eps[:, :], n_["moments_done"], n_["var_eps_done"],
                 ln_rstd[:, :], n_["ln_rstd_ready"])

            def half_cycle(u, h, first, last):
                for j in range(4):
                    at = slice(h * 2048 + j * 512, h * 2048 + (j + 1) * 512)
                    if not last:
                        pool.wait_ge(cX_done[j], u + 1)
                        pool.tensor_tensor(Y[:, at], Y[:, at], cX[:, j % 2, :], ALU.subtract).then_inc(Y_done[j], 1)
                    else:
                        pool.wait_ge(X_done[j], u - 1)
                        pool.tensor_tensor(X0[:, at], X0[:, at], X[:, at], ALU.add).then_inc(n_["sum_ready"], 1)

            for u in range(2):
                pool.wait_ge(n_["XY_ready"], u + 1)
                half_cycle(u, u, True, False)
            cycles(pool, half_cycle)
            for f in range(8):
                pool.wait_ge(n_["f_moments_done"], f + 1)
                pool.tensor_tensor(f_var[:, f, :], f_mom[:, f, :, 1], ln_eps[:, :], ALU.add).then_inc(n_["f_var_done"], 1)
                pool.wait_ge(n_["f_var_done"], f + 1)
                pool.tensor_tensor(f_rstd[:, f, :], f_var[:, f, :], minus_half[:, 0:4], ALU.pow).then_inc(n_["f_rstd_done"], 1)


FFN_LOADS = 20


def constants():
    import math
    import numpy as np
    pos = np.arange(SEQ, dtype=np.float32)
    angles = (np.arange(0, HD, 2, dtype=np.float32) / np.float32(HD) * np.float32(math.pi)).astype(np.float32)
    ang = pos[:, None] * angles[None, :]
    radius = np.float32(1.0) / (np.float32(1.0) + pos[:, None] * np.float32(0.01))
    table = np.stack([radius * np.cos(ang), radius * np.sin(ang)]).astype(np.float32)
    trig = table.reshape(2, T, 128, HALF).transpose(2, 0, 1, 3)
    s = (np.arange(128) // HALF) % 2
    sel_s = np.stack([s == 0, s == 1, -(s == 1).astype(np.float32)], 1).astype(np.float32)
    pick = np.zeros((36, 4, 128), np.float32)
    for c in range(4):
        pick[c, c] = 1.0
        pick[32 + c, c] = 1.0
    return dict(ident=np.eye(128, dtype=np.float32), trig=np.ascontiguousarray(trig), sel_s=sel_s, pick=pick,
                future=np.triu(np.full((128, 128), FUTURE, np.float32), 1))


def kernel(**inputs):
    import numpy as np
    import concourse.bacc as bacc
    from concourse.bass_utils import run_bass_kernel_spmd
    I = {k.replace("L0_attn_", "").replace("L0_ffn_", ""): np.asarray(v) for k, v in inputs.items()}
    x = I["x"]
    woT = np.transpose(I["Wo"]).reshape(G, R, 2, HALF, DIM).transpose(1, 0, 2, 3, 4)

    def by_head(a):
        return np.broadcast_to(a.reshape(G, R).T[:, :, None, None], (R, G, 2, HALF)).reshape(128, 1)

    def both(half):
        return np.broadcast_to(woT[:, :, half:half + 1], (R, G, 2, HALF, DIM)).reshape(128, DIM)

    col = lambda a, n: np.tile(a.reshape(-1, 1), (n, 1))
    arrays = dict(
        x=x, xT=np.transpose(x, (0, 2, 1)),
        w_proj=np.concatenate([np.transpose(I[n]) for n in ("Wq", "Wk", "Wv", "Wg")], 1),
        w_o0=both(0), w_o1=both(1), lam=by_head(I["lambda_param"]),
        gain=np.broadcast_to(I["q_gain"][None, :], (128, HEADS)),
        cn_w1=I["cn_w1"], cn_w2=I["cn_w2"], cn_w3=I["cn_w3"], cn_w4=I["cn_w4"],
        cn_b1=col(I["cn_b1"], 1), cn_b2=col(I["cn_b2"], 2), cn_b3=col(I["cn_b3"], 4), cn_b4=col(I["cn_b4"], 4),
        gc_w1=I["gc_w1"], gc_w2=I["gc_w2"], gc_w3=I["gc_w3"],
        gc_b1=col(I["gc_b1"], 1), gc_b2=col(I["gc_b2"], 1), gc_b3=col(I["gc_b3"], 4),
        arange_in=col(I["adaptive_range"], 128), **constants())
    arrays = {k: np.ascontiguousarray(v) for k, v in arrays.items()}
    nc = bacc.Bacc("TRN2", target_bir_lowering=False, num_devices=1)
    aps = {k: nc.dram_tensor(f"in_{k}", v.shape, mybir.dt.from_np(v.dtype), kind="ExternalInput").ap()
           for k, v in arrays.items()}
    out = nc.dram_tensor("out", (TOK, DIM), F32, kind="ExternalOutput").ap()
    block_kernel(nc, aps, out)
    r = run_bass_kernel_spmd(nc, [{f"in_{k}": v for k, v in arrays.items()}], core_ids=[0])
    return r.results[0]["out"].reshape(BATCH, SEQ, DIM)
```
